# Optimizing a Trainium2 kernel written in Bass

```python
import numpy as np
import jax
import jax.numpy as jnp

def _softmax(x, axis=-1):
    return jax.nn.softmax(x, axis=axis)

def _gelu(x):
    return jax.nn.gelu(x, approximate=True)

def _silu(x):
    return jax.nn.silu(x)

def _sigmoid(x):
    return jax.nn.sigmoid(x)

def _layernorm(x, axis=-1, eps=1e-05):
    m = jnp.mean(x, axis=axis, keepdims=True)
    v = jnp.var(x, axis=axis, keepdims=True)
    return (x - m) / jnp.sqrt(v + eps)

def _scatter_add(tgt, idx, src, axis=0):
    return tgt.at[idx].add(src)

def _segment_sum(src, seg, n):
    return jax.ops.segment_sum(src, seg, n)
kernel_name = 'mk_gnn_resnorm_d4_gnn_r64_87bb19'

def setup_inputs(seed: int=0):
    np.random.seed(seed)
    _w = jnp.asarray

    def _rec_inputs():
        import jax
        import jax.numpy as jnp
        _gk = jax.random.key(seed)
        x = -0.0003713 + 1 * jax.random.normal(jax.random.fold_in(_gk, 1), (100000, 128), jnp.float32)
        src = jax.random.randint(jax.random.fold_in(_gk, 2), (25000,), 0, 100000, jnp.int32)
        dst = jax.random.randint(jax.random.fold_in(_gk, 3), (25000,), 0, 100000, jnp.int32)
        _o = jnp.argsort(dst, stable=True)
        src = src[_o]
        dst = dst[_o]
        edge_attr_128 = -8.16379e-05 + 0.999858 * jax.random.normal(jax.random.fold_in(_gk, 13), (25000, 128), jnp.float32)
        edge_weight = jax.random.uniform(jax.random.fold_in(_gk, 15), (25000,), jnp.float32, 0.0, 1)
        return (x, src, dst, edge_attr_128, edge_weight)
    x, src, dst, edge_attr_128, edge_weight = _rec_inputs()

    def _L0_gnn_setup():
        import jax, jax.numpy as jnp
        import numpy as np
        N_NODES = 100000
        N_EDGES = 25000
        D_IN = 128
        D_OUT = 128
        key = jax.random.key(seed)
        k1, k2, k3, k4 = jax.random.split(key, 4)
        features = jax.random.normal(k1, (N_NODES, D_IN), dtype=jnp.float32)
        src = jax.random.randint(k2, (N_EDGES,), 0, N_NODES, dtype=jnp.int32)
        dst = jax.random.randint(k3, (N_EDGES,), 0, N_NODES, dtype=jnp.int32)
        bound = 1.0 / np.sqrt(D_IN)
        W = jax.random.uniform(k4, (D_OUT, D_IN), dtype=jnp.float32, minval=-bound, maxval=bound)
        b = jnp.zeros((D_OUT,), dtype=jnp.float32)
        return {'features': features, 'src': src, 'dst': dst, 'W': W, 'b': b}
    _L0_gnn_all = _L0_gnn_setup()
    _L0_gnn_in = {k: v for k, v in _L0_gnn_all.items() if k in ('W', 'b')}
    del _L0_gnn_all

    def _L1_gnn_setup():
        import jax, jax.numpy as jnp
        import numpy as np
        N = 100000
        E = 12500
        D = 128
        key = jax.random.key(seed)
        ks = jax.random.split(key, 12)
        s = lambda fan_in: 1.0 / np.sqrt(fan_in)
        return {'h': jax.random.normal(ks[0], (N, D), dtype=jnp.float32), 'w': jax.random.uniform(ks[1], (E,), dtype=jnp.float32), 'src': jax.random.randint(ks[2], (E,), 0, N, dtype=jnp.int32), 'dst': jax.random.randint(ks[3], (E,), 0, N, dtype=jnp.int32), 'W1': jax.random.uniform(ks[4], (2 * D + 1, D), jnp.float32, -s(2 * D + 1), s(2 * D + 1)), 'b1': jnp.zeros((D,), jnp.float32), 'W2': jax.random.uniform(ks[5], (D, D), jnp.float32, -s(D), s(D)), 'b2': jnp.zeros((D,), jnp.float32), 'U1': jax.random.uniform(ks[6], (2 * D, D), jnp.float32, -s(2 * D), s(2 * D)), 'c1': jnp.zeros((D,), jnp.float32), 'U2': jax.random.uniform(ks[7], (D, D), jnp.float32, -s(D), s(D)), 'c2': jnp.zeros((D,), jnp.float32)}
    _L1_gnn_all = _L1_gnn_setup()
    _L1_gnn_in = {k: v for k, v in _L1_gnn_all.items() if k in ('W1', 'b1', 'W2', 'b2', 'U1', 'c1', 'U2', 'c2')}
    del _L1_gnn_all

    def _L2_gnn_setup():
        import jax, jax.numpy as jnp
        import numpy as np
        N = 50000
        NE = 12500
        DIN = 128
        DOUT = 128
        H = 8
        DH = DOUT // H
        key = jax.random.key(seed)
        ks = jax.random.split(key, 12)
        w = lambda k, shape: jax.random.normal(k, shape, jnp.float32) / np.sqrt(shape[-1])
        return {'x': jax.random.normal(ks[0], (N, DIN), jnp.float32), 'edge_attr': jax.random.normal(ks[1], (NE, DIN), jnp.float32), 'edge_index': jax.random.randint(ks[2], (2, NE), 0, N, dtype=jnp.int32), 'batch_vec': jnp.zeros((N,), jnp.int32), 'Wq': w(ks[3], (DOUT, DIN)), 'bq': jnp.zeros((DOUT,), jnp.float32), 'Wk': w(ks[4], (DOUT, DIN)), 'bk': jnp.zeros((DOUT,), jnp.float32), 'We': w(ks[5], (DOUT, DIN)), 'be': jnp.zeros((DOUT,), jnp.float32), 'Wv': w(ks[6], (DOUT, DIN)), 'bv': jnp.zeros((DOUT,), jnp.float32)}
    _L2_gnn_all = _L2_gnn_setup()
    _L2_gnn_in = {k: v for k, v in _L2_gnn_all.items() if k in ('Wq', 'bq', 'Wk', 'bk', 'We', 'be', 'Wv', 'bv')}
    del _L2_gnn_all

    def _L3_gnn_setup():
        import jax, jax.numpy as jnp
        import numpy as np
        V = 100000
        IN_DIM = 128
        HID_DIM = 128
        OUT_DIM = 128
        E = 50000

        def _gcn_conv(x, edge_index, edge_weight, W, b):
            num_nodes = x.shape[0]
            xw = x @ W
            src, dst = (edge_index[0], edge_index[1])
            loop = jnp.arange(num_nodes, dtype=edge_index.dtype)
            row = jnp.concatenate([src, loop])
            col = jnp.concatenate([dst, loop])
            w = jnp.concatenate([edge_weight, jnp.ones((num_nodes,), dtype=x.dtype)])
            deg = jax.ops.segment_sum(w, col, num_segments=num_nodes)
            dinv = jnp.where(deg > 0, jax.lax.rsqrt(deg), 0.0)
            norm = dinv[row] * w * dinv[col]
            out = jax.ops.segment_sum(xw[row] * norm[:, None], col, num_segments=num_nodes)
            return out + b

        def _layernorm(h, gamma, beta, eps=1e-05):
            mu = jnp.mean(h, axis=-1, keepdims=True)
            var = jnp.var(h, axis=-1, keepdims=True)
            return (h - mu) * jax.lax.rsqrt(var + eps) * gamma + beta
        key = jax.random.key(seed)
        ks = jax.random.split(key, 10)
        x = jax.random.normal(ks[0], (V, IN_DIM), dtype=jnp.float32)
        edge_index = jax.random.randint(ks[1], (2, E), 0, V, dtype=jnp.int64)
        edge_weight = jax.random.uniform(ks[2], (E,), dtype=jnp.float32)
        W1 = jax.random.normal(ks[3], (IN_DIM, HID_DIM), dtype=jnp.float32) * 0.02
        b1 = jnp.zeros((HID_DIM,), dtype=jnp.float32)
        g1 = jnp.ones((HID_DIM,), dtype=jnp.float32)
        beta1 = jnp.zeros((HID_DIM,), dtype=jnp.float32)
        W2 = jax.random.normal(ks[4], (HID_DIM, OUT_DIM), dtype=jnp.float32) * 0.02
        b2 = jnp.zeros((OUT_DIM,), dtype=jnp.float32)
        return {'x': x, 'edge_weight': edge_weight, 'W1': W1, 'b1': b1, 'g1': g1, 'beta1': beta1, 'W2': W2, 'b2': b2, 'edge_index': edge_index}
    _L3_gnn_all = _L3_gnn_setup()
    _L3_gnn_in = {k: v for k, v in _L3_gnn_all.items() if k in ('W1', 'b1', 'g1', 'beta1', 'W2', 'b2')}
    del _L3_gnn_all
    return {'x': x, 'src': src, 'dst': dst, 'edge_attr_128': edge_attr_128, 'edge_weight': edge_weight, 'L0_gnn_W': _L0_gnn_in['W'], 'L0_gnn_b': _L0_gnn_in['b'], 'L1_gnn_W1': _L1_gnn_in['W1'], 'L1_gnn_b1': _L1_gnn_in['b1'], 'L1_gnn_W2': _L1_gnn_in['W2'], 'L1_gnn_b2': _L1_gnn_in['b2'], 'L1_gnn_U1': _L1_gnn_in['U1'], 'L1_gnn_c1': _L1_gnn_in['c1'], 'L1_gnn_U2': _L1_gnn_in['U2'], 'L1_gnn_c2': _L1_gnn_in['c2'], 'L2_gnn_Wq': _L2_gnn_in['Wq'], 'L2_gnn_bq': _L2_gnn_in['bq'], 'L2_gnn_Wk': _L2_gnn_in['Wk'], 'L2_gnn_bk': _L2_gnn_in['bk'], 'L2_gnn_We': _L2_gnn_in['We'], 'L2_gnn_be': _L2_gnn_in['be'], 'L2_gnn_Wv': _L2_gnn_in['Wv'], 'L2_gnn_bv': _L2_gnn_in['bv'], 'L3_gnn_W1': _L3_gnn_in['W1'], 'L3_gnn_b1': _L3_gnn_in['b1'], 'L3_gnn_g1': _L3_gnn_in['g1'], 'L3_gnn_beta1': _L3_gnn_in['beta1'], 'L3_gnn_W2': _L3_gnn_in['W2'], 'L3_gnn_b2': _L3_gnn_in['b2']}

def reference(x, src, dst, edge_attr_128, edge_weight, L0_gnn_W, L0_gnn_b, L1_gnn_W1, L1_gnn_b1, L1_gnn_W2, L1_gnn_b2, L1_gnn_U1, L1_gnn_c1, L1_gnn_U2, L1_gnn_c2, L2_gnn_Wq, L2_gnn_bq, L2_gnn_Wk, L2_gnn_bk, L2_gnn_We, L2_gnn_be, L2_gnn_Wv, L2_gnn_bv, L3_gnn_W1, L3_gnn_b1, L3_gnn_g1, L3_gnn_beta1, L3_gnn_W2, L3_gnn_b2):
    import jax
    import jax.numpy as jnp

    def _L0_gnn_ref(features, src, dst, W, b):
        import jax, jax.numpy as jnp
        import numpy as np
        N_NODES = 100000
        N_EDGES = 25000
        D_IN = 128
        D_OUT = 128
        msgs = features[src]
        h_neigh = jax.ops.segment_sum(msgs, dst, num_segments=N_NODES)
        return jnp.einsum('nd,od->no', h_neigh, W) + b

    def _L1_gnn_ref(h, w, src, dst, W1, b1, W2, b2, U1, c1, U2, c2):
        import jax, jax.numpy as jnp
        import numpy as np
        N = 100000
        E = 12500
        D = 128
        n = h.shape[0]
        msg_in = jnp.concatenate([h[src], h[dst], w[:, None]], axis=1)
        msg = jax.nn.relu(msg_in @ W1 + b1) @ W2 + b2
        agg = jax.ops.segment_max(msg, dst, num_segments=n)
        deg = jax.ops.segment_sum(jnp.ones((dst.shape[0],), jnp.int32), dst, num_segments=n)
        agg = jnp.where((deg > 0)[:, None], agg, jnp.zeros((), h.dtype))
        upd_in = jnp.concatenate([h, agg], axis=1)
        return jax.nn.relu(upd_in @ U1 + c1) @ U2 + c2

    def _L2_gnn_ref(x, edge_attr, edge_index, batch_vec, Wq, bq, Wk, bk, We, be, Wv, bv):
        import jax, jax.numpy as jnp
        import numpy as np
        N = 50000
        NE = 12500
        DIN = 128
        DOUT = 128
        H = 8
        DH = DOUT // H
        num_node = batch_vec.shape[0]
        Qh = (x @ Wq.T + bq).reshape(-1, H, DH)
        Kh = (x @ Wk.T + bk).reshape(-1, H, DH)
        Vh = (x @ Wv.T + bv).reshape(-1, H, DH)
        E = (edge_attr @ We.T + be).reshape(-1, H, DH)
        src = edge_index[0]
        dst = edge_index[1]
        scale = 1.0 / np.sqrt(DH).astype(np.float32)
        s = jnp.sum(Kh[src] * Qh[dst] * scale * E, axis=-1)
        score = jnp.exp(jnp.clip(s, -5.0, 5.0))[..., None]
        msg = Vh[src] * score
        wV = jax.ops.segment_sum(msg, dst, num_segments=num_node)
        return wV.reshape(num_node, H * DH)

    def _L3_gnn_ref(x, edge_weight, W1, b1, g1, beta1, W2, b2, edge_index):
        import jax, jax.numpy as jnp
        import numpy as np
        V = 100000
        IN_DIM = 128
        HID_DIM = 128
        OUT_DIM = 128
        E = 50000

        def _gcn_conv(x, edge_index, edge_weight, W, b):
            num_nodes = x.shape[0]
            xw = x @ W
            src, dst = (edge_index[0], edge_index[1])
            loop = jnp.arange(num_nodes, dtype=edge_index.dtype)
            row = jnp.concatenate([src, loop])
            col = jnp.concatenate([dst, loop])
            w = jnp.concatenate([edge_weight, jnp.ones((num_nodes,), dtype=x.dtype)])
            deg = jax.ops.segment_sum(w, col, num_segments=num_nodes)
            dinv = jnp.where(deg > 0, jax.lax.rsqrt(deg), 0.0)
            norm = dinv[row] * w * dinv[col]
            out = jax.ops.segment_sum(xw[row] * norm[:, None], col, num_segments=num_nodes)
            return out + b

        def _layernorm(h, gamma, beta, eps=1e-05):
            mu = jnp.mean(h, axis=-1, keepdims=True)
            var = jnp.var(h, axis=-1, keepdims=True)
            return (h - mu) * jax.lax.rsqrt(var + eps) * gamma + beta
        h = _gcn_conv(x, edge_index, edge_weight, W1, b1)
        h = jax.nn.relu(h)
        h = _layernorm(h, g1, beta1)
        out = _gcn_conv(h, edge_index, edge_weight, W2, b2)
        return out
    edge_index = jnp.stack([src, dst])
    batch0 = jnp.zeros((100000,), jnp.int32)
    x = _layernorm(x + _L0_gnn_ref(x, src, dst, L0_gnn_W, L0_gnn_b), axis=-1)
    x = _layernorm(x + _L1_gnn_ref(x, edge_weight, src, dst, L1_gnn_W1, L1_gnn_b1, L1_gnn_W2, L1_gnn_b2, L1_gnn_U1, L1_gnn_c1, L1_gnn_U2, L1_gnn_c2), axis=-1)
    x = _layernorm(x + _L2_gnn_ref(x, edge_attr_128, edge_index, batch0, L2_gnn_Wq, L2_gnn_bq, L2_gnn_Wk, L2_gnn_bk, L2_gnn_We, L2_gnn_be, L2_gnn_Wv, L2_gnn_bv), axis=-1)
    x = _layernorm(x + _L3_gnn_ref(x, edge_weight, L3_gnn_W1, L3_gnn_b1, L3_gnn_g1, L3_gnn_beta1, L3_gnn_W2, L3_gnn_b2, edge_index), axis=-1)
    return x

_drawn_inputs = setup_inputs


def setup_inputs(seed=0):
    import zlib

    import numpy as np

    out = dict(_drawn_inputs(seed))
    spreads = {'L0_gnn_b': (0.0, 0.1),
     'L1_gnn_b1': (0.0, 0.8),
     'L1_gnn_b2': (0.0, 0.8),
     'L1_gnn_c1': (0.0, 0.1),
     'L1_gnn_c2': (0.0, 0.1),
     'L2_gnn_bq': (0.0, 0.1),
     'L2_gnn_bk': (0.0, 0.1),
     'L2_gnn_be': (0.0, 0.1),
     'L2_gnn_bv': (0.0, 0.1),
     'L3_gnn_b1': (0.0, 0.1),
     'L3_gnn_g1': (1.0, 0.2),
     'L3_gnn_beta1': (0.0, 0.355),
     'L3_gnn_b2': (0.0, 0.1)}
    factors = {'L1_gnn_W1': 3.959, 'L1_gnn_W2': 3.2}
    for name, (base, spread) in spreads.items():
        noise = np.random.default_rng([zlib.crc32(name.encode()), seed]).standard_normal(out[name].shape)
        drawn = base * np.exp(spread * noise) if base else spread * noise
        out[name] = jnp.asarray(drawn.astype(out[name].dtype))
    for name, factor in factors.items():
        out[name] = (out[name] * factor).astype(out[name].dtype)
    return out
```

```python
from contextlib import ExitStack

import concourse.bass as bass
from concourse import mybir

F32 = mybir.dt.float32
I32 = mybir.dt.int32
BF16 = mybir.dt.bfloat16
ALU = mybir.AluOpType
ACT = mybir.ActivationFunctionType

P = 128
D = 128
TILES = 4
G = P * TILES
EPS = 1e-5
NO_ROW = 1 << 20
BIG = 3.0e38

SRC, DSTC, SCAT, PAY, LAST, FIRST, DINV, WROW = 0, 4, 8, 12, 20, 24, 28, 32
REC = 36
PEN_B, KEEP_B, KEEP_F, W_F = 0, 1, 2, 3

WEIGHTS = ["W0", "Wq", "Wk", "We", "Wv", "M1S", "M1D", "M2", "U1X", "U1A", "U2", "G1", "G2"]
VECTORS = ["b0", "mb1", "mb2", "c1", "c2", "bq", "bk", "be", "bv", "gb1", "gamma", "beta", "gb2"]


class Step:

    def __init__(self, j, unroll, off):
        self.j, self.unroll, self.off = j, unroll, off
        self.fixed = isinstance(j, int)

    def lin(self, mult=1, add=0, div=1):
        return self.j * (mult * (self.unroll // div)) + (mult * (self.off // div) + add)

    def slot(self, count=2):
        return self.off % count


def wait(eng, sem, value):
    if isinstance(value, int) and value <= 0:
        return
    eng.wait_ge(sem, value)


def uses(count, k, ring):
    return (count + ring - 1 - k) // ring


def run_groups(eng, count, unroll, stages):
    deepest = max(lag for lag, _ in stages)
    first = -(-(deepest + 4) // unroll)
    last = (count - 1) // unroll

    def at(j, u):
        for lag, work in stages:
            step = Step(j, unroll, u - lag)
            if step.fixed and not 0 <= step.lin() < count:
                continue
            work(step)

    for t in range(first * unroll):
        at(t // unroll, t % unroll)
    with eng.Fori(first, last) as j:
        for u in range(unroll):
            at(j, u)
    for t in range(last * unroll, count + deepest):
        at(t // unroll, t % unroll)


class Room:

    def __init__(self, nc, ctx, name):
        self.nc, self.ctx, self.name = nc, ctx, name
        self.counts = []
        self.passed = self.sem("passed")

    def hold(self, eng, sem, value):
        if isinstance(value, int):
            wait(eng, sem, value)
            return
        eng.wait_ge(sem, value)
        eng.sem_inc(self.passed, 1)

    def sb(self, name, shape, dt=F32):
        return self.ctx.enter_context(self.nc.sbuf_tensor(f"{self.name}_{name}", shape, dt))

    def two(self, name, shape, dt=F32, count=2):
        return [self.sb(f"{name}{i}", shape, dt) for i in range(count)]

    def bank(self, name):
        return self.ctx.enter_context(self.nc.psum_tensor(f"{self.name}_bank_{name}", [P, G], F32))

    def sem(self, name):
        self.counts.append(self.ctx.enter_context(self.nc.semaphore(f"{self.name}_{name}")))
        return self.counts[-1]

    def sem2(self, name, count=2):
        return [self.sem(f"{name}{i}") for i in range(count)]

    def swdge2(self, name, count=2):
        return [self.nc.alloc_semaphore(f"{self.name}_{name}{i}") for i in range(count)]

    def block(self):
        self.ctx.callback(self.clear)
        return self.ctx.enter_context(self.nc.Block())

    def clear(self):
        numbers = sorted(sem.num for sem in self.counts)
        start = 0
        for i, number in enumerate(numbers):
            if i + 1 == len(numbers) or numbers[i + 1] != number + 1:
                self.nc.gpsimd.sem_clear(range(numbers[start], number + 1))
                start = i + 1
        self.nc.all_engine_barrier()


def tile(buf, c):
    return buf[:, c * D:(c + 1) * D]


def tiles3(buf):
    return buf[:, :].rearrange("p (c d) -> p c d", c=TILES)


def cols_of(table, g, width):
    return table[:, bass.ds(g * width, width)]


def edge_rows(table, g, base=0):
    return table[bass.ds(g * G + base, G), :].rearrange("(c p) d -> p c d", p=P)


def over_tiles(row):
    return row.unsqueeze(1).broadcast_to([P, TILES, D])


class Norm:

    def __init__(self, room, name, eps_col):
        self.st = room.two(f"{name}_st", [P, 6 * TILES])
        self.mv = room.two(f"{name}_mv", [P, 2 * TILES])
        self.sd = room.two(f"{name}_sd", [P, TILES])
        self.rs = room.two(f"{name}_rs", [P, TILES])
        self.rm = room.two(f"{name}_rm", [P, TILES])
        self.st_done = room.sem(f"{name}_st_done")
        self.settled = room.sem(f"{name}_st_settled")
        self.mv_done = room.sem(f"{name}_mv_done")
        self.sd_done = room.sem(f"{name}_sd_done")
        self.rs_done = room.sem(f"{name}_rs_done")
        self.rm_done = room.sem(f"{name}_rm_done")
        self.eps = eps_col

    def stats(self, v, s, rows):
        k = s.slot()
        for c in range(TILES):
            ins = v.bn_stats(self.st[k][:, 6 * c:6 * c + 6], tile(rows, c))
        ins.then_inc(self.st_done, 1)
        v.wait_ge(self.st_done, s.lin(1, 1))
        v.sem_inc(self.settled, 1)
        for c in range(TILES):
            ins = v.bn_aggr(self.mv[k][:, 2 * c:2 * c + 2], self.st[k][:, 6 * c:6 * c + 6])
        ins.then_inc(self.mv_done, 1)

    def root(self, a, s):
        k = s.slot()
        a.wait_ge(self.mv_done, s.lin(1, 1))
        a.activation(self.sd[k][:, :], self.mv[k][:, 1::2], ACT.Sqrt, bias=self.eps).then_inc(self.sd_done, 1)

    def finish(self, v, s, rows, out, out_done, mask=None, out_free=None):
        k = s.slot()
        v.wait_ge(self.sd_done, s.lin(1, 1))
        v.reciprocal(self.rs[k][:, :], self.sd[k][:, :]).then_inc(self.rs_done, 1)
        v.wait_ge(self.rs_done, s.lin(1, 1))
        factor = self.rs[k]
        if mask is not None:
            v.tensor_tensor(self.rm[k][:, :], self.rs[k][:, :], mask, ALU.mult).then_inc(self.rm_done, 1)
            v.wait_ge(self.rm_done, s.lin(1, 1))
            factor = self.rm[k]
        if out_free is not None:
            out_free()
        for c in range(TILES):
            ins = v.tensor_scalar(tile(out, c), tile(rows, c), self.mv[k][:, 2 * c:2 * c + 1],
                                  factor[:, c:c + 1], ALU.subtract, ALU.mult)
        ins.then_inc(out_done, 1)


class Weights:

    def __init__(self, room):
        n = len(WEIGHTS)
        self.mats = room.sb("mats", [P, n * D])
        self.turned = room.sb("turned", [P, 5 * D])
        self.cols = room.sb("cols", [P, len(VECTORS)])
        self.rows = room.sb("rows", [P, len(VECTORS) * D])
        self.wrow = room.sb("wrow", [1, D])
        self.ident = room.sb("ident", [P, P])
        self.center = room.sb("center", [P, P])
        self.heads = room.sb("heads", [P, P])
        self.mean_col = room.sb("mean_col", [P, 1])
        self.eps = room.sb("eps", [P, 1])
        self.eps2 = room.sb("eps2", [P, 1])
        self.u1c = room.sb("u1c", [P, D])
        self.g1c = room.sb("g1c", [P, D])
        self.u2c = room.sb("u2c", [P, D])
        self.g2c = room.sb("g2c", [P, D])
        self.c2c = room.sb("c2c", [P, D])
        self.gb2c = room.sb("gb2c", [P, D])
        self.negc2 = room.sb("negc2", [P, 1])
        self.neggb2 = room.sb("neggb2", [P, 1])
        self.c1b = room.sb("c1b", [P, 1])
        self.ones16 = room.sb("ones16", [P, P], BF16)
        self.c2s = room.sb("c2s", [P, D], BF16)

    def mat(self, name):
        i = WEIGHTS.index(name)
        return self.mats[:, i * D:(i + 1) * D]

    def t(self, i):
        return self.turned[:, i * D:(i + 1) * D]

    def col(self, name):
        i = VECTORS.index(name)
        return self.cols[:, i:i + 1]

    def row(self, name):
        i = VECTORS.index(name)
        return self.rows[:, i * D:(i + 1) * D]


def prepare_weights(nc, w, mats_in, vec_cols, vec_rows, wrow_in):
    with ExitStack() as ctx:
        room = Room(nc, ctx, "prep")
        ps_turn = [room.bank(f"ps_turn{i}") for i in range(2)]
        ps_mats = room.bank("ps_mats")
        ps_cols = room.bank("ps_cols")
        gw2 = room.sb("gw2", [P, D])
        gw2l = room.sb("gw2l", [P, D])
        gb2full = room.sb("gb2full", [P, D])
        sums = room.sb("sums", [P, 4])
        beta_b = room.sb("beta_b", [P, P])
        rest = room.sb("rest", [P, D])
        part = room.sb("part", [P, D], BF16)
        loaded = room.sem("loaded")
        const = room.sem("const")
        ident_ok = room.sem("ident_ok")
        turned = room.sem("turned")
        kept = room.sem("kept")
        v1 = room.sem("v1")
        prod = room.sem("prod")
        back = room.sem("back")
        block = room.block()

        @block.sync
        def _(sp):
            sp.dma_start(w.mats[:, :], mats_in).then_inc(loaded, 16)
            sp.dma_start(w.cols[:, :], vec_cols).then_inc(loaded, 16)
            sp.dma_start(w.rows[:, :], vec_rows.rearrange("k d -> (k d)").partition_broadcast(P)).then_inc(loaded, 16)
            sp.dma_start(w.wrow[:, :], wrow_in).then_inc(loaded, 16)

        @block.gpsimd
        def _(pool):
            nc.gpsimd.memset(w.ident[:, :], 0.0).then_inc(const, 1)
            nc.gpsimd.memset(w.center[:, :], -1.0 / P).then_inc(const, 1)
            nc.gpsimd.memset(w.heads[:, :], 0.25).then_inc(const, 1)
            nc.gpsimd.memset(w.mean_col[:, :], 1.0 / P).then_inc(const, 1)
            nc.gpsimd.memset(w.eps[:, :], EPS).then_inc(const, 1)
            nc.gpsimd.memset(w.eps2[:, :], EPS * EPS).then_inc(const, 1)
            pool.wait_ge(const, 6)
            nc.gpsimd.affine_select(out=w.ident[:, :], in_=w.ident[:, :], compare_op=ALU.not_equal, fill=1.0,
                                    base=0, pattern=[[-1, P]], channel_multiplier=1).then_inc(ident_ok, 1)
            nc.gpsimd.affine_select(out=w.center[:, :], in_=w.center[:, :], compare_op=ALU.not_equal,
                                    fill=1.0 - 1.0 / P, base=0, pattern=[[-1, P]], channel_multiplier=1).then_inc(ident_ok, 1)
            heads3 = w.heads[:, :].rearrange("p (h d) -> p h d", d=16)
            nc.gpsimd.affine_select(out=heads3, in_=heads3, compare_op=ALU.is_ge, fill=0.0, base=0,
                                    pattern=[[-16, 8], [0, 16]], channel_multiplier=1).then_inc(ident_ok, 1)
            pool.wait_ge(ident_ok, 3)
            nc.gpsimd.affine_select(out=heads3, in_=heads3, compare_op=ALU.is_ge, fill=0.0, base=15,
                                    pattern=[[16, 8], [0, 16]], channel_multiplier=-1).then_inc(ident_ok, 1)

        @block.tensor
        def _(pe):
            pe.wait_ge(ident_ok, 4)
            pe.wait_ge(loaded, 64)
            for i in range(5):
                ins = pe.transpose(ps_turn[i // 4][:, (i % 4) * D:(i % 4 + 1) * D], w.mats[:, i * D:(i + 1) * D], w.ident[:, :])
            ins.then_inc(turned, 1)
            pe.matmul(ps_mats[:, 0:D], w.center[:, :], w.mat("U1X"), start=True, stop=True)
            pe.matmul(ps_mats[:, D:2 * D], w.center[:, :], w.mat("G1"), start=True, stop=True)
            pe.wait_ge(v1, 1)
            pe.matmul(ps_mats[:, 2 * D:3 * D], w.center[:, :], gw2[:, :], start=True, stop=True)
            pe.wait_ge(v1, 2)
            pe.matmul(ps_mats[:, 3 * D:4 * D], beta_b[:, :], w.mat("G2"), start=True, stop=True)
            pe.matmul(ps_cols[:, 0:1], w.mat("U1A"), w.col("mb2"), start=True, stop=True).then_inc(prod, 1)
            pe.wait_ge(v1, 3)
            pe.transpose(ps_turn[0][:, 0:128], w.c2c[:, :], w.ident[:, :])
            pe.transpose(ps_turn[0][:, 128:256], w.gb2c[:, :], w.ident[:, :]).then_inc(back, 1)

        @block.vector
        def _(v):
            n = [0]

            def keep(ins):
                n[0] += 1
                ins.then_inc(kept, 1)
                v.wait_ge(kept, n[0])

            v.wait_ge(loaded, 64)
            v.tensor_scalar(gw2[:, :], w.mat("G2"), w.col("gamma"), None, ALU.mult).then_inc(v1, 1)
            v.wait_ge(const, 6)
            v.wait_ge(ident_ok, 4)
            keep(v.memset(beta_b[:, :], 0.0))
            v.tensor_scalar(beta_b[:, :], beta_b[:, :], w.col("beta"), None, ALU.add).then_inc(v1, 1)
            v.wait_ge(turned, 1)
            v.tensor_copy(w.turned[:, 0:4 * D], ps_turn[0][:, :])
            v.tensor_copy(w.turned[:, 4 * D:5 * D], ps_turn[1][:, 0:D])
            keep(v.reduce_sum(sums[:, 0:1], w.mat("U2"), mybir.AxisListType.X))
            keep(v.tensor_scalar(sums[:, 0:1], sums[:, 0:1], 1.0 / P, None, ALU.mult))
            v.tensor_scalar(w.u2c[:, :], w.mat("U2"), sums[:, 0:1], None, ALU.subtract)
            keep(v.reduce_sum(sums[:, 1:2], w.row("c2"), mybir.AxisListType.X))
            keep(v.tensor_scalar(sums[:, 1:2], sums[:, 1:2], 1.0 / P, None, ALU.mult))
            keep(v.tensor_scalar(w.c2c[:, :], w.row("c2"), sums[:, 1:2], None, ALU.subtract))
            v.wait_ge(prod, 1)
            v.tensor_copy(w.u1c[:, :], ps_mats[:, 0:D])
            v.tensor_copy(w.g1c[:, :], ps_mats[:, D:2 * D])
            keep(v.tensor_copy(gw2l[:, :], ps_mats[:, 2 * D:3 * D]))
            keep(v.reduce_sum(sums[:, 2:3], gw2l[:, :], mybir.AxisListType.X))
            keep(v.tensor_scalar(sums[:, 2:3], sums[:, 2:3], 1.0 / P, None, ALU.mult))
            v.tensor_scalar(w.g2c[:, :], gw2l[:, :], sums[:, 2:3], None, ALU.subtract)
            keep(v.tensor_tensor(gb2full[:, :], ps_mats[:, 3 * D:4 * D], w.row("gb2"), ALU.add))
            keep(v.reduce_sum(sums[:, 3:4], gb2full[:, :], mybir.AxisListType.X))
            keep(v.tensor_scalar(sums[:, 3:4], sums[:, 3:4], 1.0 / P, None, ALU.mult))
            v.tensor_scalar(w.gb2c[:, :], gb2full[:, :], sums[:, 3:4], None, ALU.subtract).then_inc(v1, 1)
            v.tensor_tensor(w.c1b[:, :], ps_cols[:, 0:1], w.col("c1"), ALU.add)
            v.wait_ge(back, 1)
            v.tensor_scalar(w.negc2[:, :], ps_turn[0][:, 0:1], -1.0, None, ALU.mult)
            keep(v.tensor_scalar(w.neggb2[:, :], ps_turn[0][:, 128:129], -1.0, None, ALU.mult))

            def split(row, parts):
                keep(v.memset(parts[:, :], 0.0))
                keep(v.tensor_copy(rest[:, :], row[:, :]))
                for i in range(3):
                    keep(v.tensor_copy(part[:, :], rest[:, :]))
                    at = slice(32 * i, 32 * i + 1)
                    keep(v.tensor_copy(parts[at, :], part[at, :]))
                    keep(v.tensor_tensor(rest[:, :], rest[:, :], part[:, :], ALU.subtract))

            keep(v.memset(w.ones16[:, :], 1.0))
            split(w.c2c, w.c2s)


def prepare_edges(nc, w, ng, nodes, ints_in, ew_in, along, facts, slots):
    with ExitStack() as ctx:
        room = Room(nc, ctx, "edges")
        I = {k: room.sb(k, [ng, G], I32) for k in ("src", "dst", "dprev", "dnext")}
        f = {k: room.sb("f_" + k, [ng, G]) for k in ("dst", "dprev", "dnext", "last", "first", "w", "pos", "carry",
                                                      "degsum", "begin", "deg", "scat", "dstc", "src", "dinv", "pay")}
        al = room.sb("along", [ng, 4, G])
        ends = room.sb("ends", [ng, 4])
        erow = room.sb("erow", [1, 4, 64])
        crow = room.sb("crow", [1, 2, 64])
        ccol = room.sb("ccol", [ng, 2])
        rec = room.sb("rec", [P, ng, REC], I32)
        iota_id = room.sb("iota_id", [125, nodes // 125, 2], I32)
        ps_e = room.bank("ps_e")
        ps = [room.bank(f"ps{i}") for i in range(7)]
        loaded, kept, posed, ended, ends_back, carried, col_back, turned, evac, rooted, stored = (
            room.sem(x) for x in ("loaded", "kept", "posed", "ended", "ends_back", "carried", "col_back", "turned",
                                  "evac", "rooted", "stored"))
        ready = room.sem("ready")
        alongs = room.sem("alongs")
        rec_ok = room.sem("rec_ok")
        ids = room.sem("ids")
        TURN = [("src", SRC), ("dstc", DSTC), ("scat", SCAT), ("last", LAST), ("first", FIRST), ("dinv", DINV), ("w", WROW)]
        block = room.block()

        @block.sync
        def _(sp):
            for i, k in enumerate(("src", "dst", "dprev", "dnext")):
                sp.dma_start(I[k][:, :], ints_in[i]).then_inc(loaded, 16)
            sp.dma_start(f["w"][:, :], ew_in).then_inc(loaded, 16)
            sp.wait_ge(ids, 2)
            sp.dma_start(slots.rearrange("(a b) c -> a b c", a=125), iota_id[:, :, :]).then_inc(stored, 16)
            sp.wait_ge(alongs, 1)
            sp.dma_start(along, al[:, :, :]).then_inc(stored, 16)
            sp.wait_ge(rec_ok, 1)
            sp.dma_start(facts, rec[:, :, :]).then_inc(stored, 16)
            sp.wait_ge(stored, 48)

        @block.gpsimd
        def _(pool):
            nc.gpsimd.iota(iota_id[:, :, 1], pattern=[[1, nodes // 125]], base=0,
                           channel_multiplier=nodes // 125).then_inc(ids, 1)
            nc.gpsimd.memset(iota_id[:, :, 0], NO_ROW).then_inc(ids, 1)
            nc.gpsimd.iota(f["pos"][:, :], pattern=[[1, G]], base=0, channel_multiplier=G,
                           allow_small_or_imprecise_dtypes=True).then_inc(posed, 1)
            nc.gpsimd.iota(rec[:, :, PAY:PAY + 2 * TILES:2], pattern=[[G, ng], [P, TILES]], base=0,
                           channel_multiplier=1).then_inc(posed, 1)

        @block.vector
        def _(v):
            n = [0]

            def keep(ins):
                n[0] += 1
                ins.then_inc(kept, 1)
                v.wait_ge(kept, n[0])

            v.wait_ge(loaded, 80)
            v.tensor_copy(f["dst"][:, :], I["dst"][:, :])
            v.tensor_copy(f["src"][:, :], I["src"][:, :])
            v.tensor_copy(f["dprev"][:, :], I["dprev"][:, :])
            keep(v.tensor_copy(f["dnext"][:, :], I["dnext"][:, :]))
            v.tensor_tensor(al[:, KEEP_F, :], f["dst"][:, :], f["dprev"][:, :], ALU.is_equal)
            keep(v.tensor_tensor(al[:, KEEP_B, :], f["dst"][:, :], f["dnext"][:, :], ALU.is_equal))
            v.tensor_scalar(al[:, PEN_B, :], al[:, KEEP_B, :], BIG, BIG, ALU.mult, ALU.subtract)
            v.tensor_copy(al[:, W_F, :], f["w"][:, :]).then_inc(alongs, 1)
            v.tensor_scalar(f["last"][:, :], al[:, KEEP_B, :], -1.0, 1.0, ALU.mult, ALU.add)
            keep(v.tensor_scalar(f["first"][:, :], al[:, KEEP_F, :], -1.0, 1.0, ALU.mult, ALU.add))
            v.tensor_scalar(f["dstc"][:, :], f["dst"][:, :], float(nodes - 1), None, ALU.min)
            v.scalar_tensor_tensor(out=f["scat"][:, :], in0=al[:, KEEP_B, :], scalar=float(NO_ROW), in1=f["dst"][:, :],
                                   op0=ALU.mult, op1=ALU.add)
            v.wait_ge(posed, 1)
            keep(v.tensor_tensor(f["pos"][:, :], f["pos"][:, :], f["first"][:, :], ALU.mult))
            v.tensor_tensor_scan(f["degsum"][:, :], al[:, KEEP_F, :], f["w"][:, :], 0.0, ALU.mult, ALU.add)
            v.tensor_tensor_scan(f["begin"][:, :], al[:, KEEP_F, :], f["pos"][:, :], 0.0, ALU.mult, ALU.add)
            keep(v.memset(f["deg"][:, :], 0.0))
            keep(v.tensor_tensor_scan(f["carry"][:, :], al[:, KEEP_F, :], f["deg"][:, :], 1.0, ALU.mult, ALU.add))
            v.tensor_copy(ends[:, 0:1], f["carry"][:, G - 1:G])
            v.tensor_copy(ends[:, 1:2], f["degsum"][:, G - 1:G])
            v.tensor_copy(ends[:, 2:3], f["begin"][:, G - 1:G]).then_inc(ended, 1)
            v.wait_ge(ends_back, 1)
            keep(v.tensor_copy(erow[:, 0:3, 0:ng], ps_e[0:1, 0:3 * 64].rearrange("p (k n) -> p k n", k=3)[:, :, 0:ng]))
            v.tensor_tensor_scan(crow[:, 0, 1:ng + 1], erow[:, 0, 0:ng], erow[:, 1, 0:ng], 0.0, ALU.mult, ALU.add)
            keep(v.tensor_tensor_scan(crow[:, 1, 1:ng + 1], erow[:, 0, 0:ng], erow[:, 2, 0:ng], 0.0, ALU.mult, ALU.add))
            keep(v.memset(crow[:, :, 0:1], 0.0))
            v.sem_inc(carried, 1)
            v.wait_ge(col_back, 1)
            keep(v.tensor_copy(ccol[:, :], ps_e[0:ng, 256:258]))
            keep(v.scalar_tensor_tensor(out=f["deg"][:, :], in0=f["carry"][:, :], scalar=ccol[:, 0:1],
                                        in1=f["degsum"][:, :], op0=ALU.mult, op1=ALU.add))
            keep(v.scalar_tensor_tensor(out=f["pay"][:, :], in0=f["carry"][:, :], scalar=ccol[:, 1:2],
                                        in1=f["begin"][:, :], op0=ALU.mult, op1=ALU.add))
            v.tensor_scalar(f["pay"][:, :], f["pay"][:, :], float(nodes), None, ALU.add)
            keep(v.tensor_scalar(f["deg"][:, :], f["deg"][:, :], 1.0, None, ALU.add))
            v.tensor_scalar(f["carry"][:, :], f["deg"][:, :], 0.0, None, ALU.is_gt)
            keep(v.tensor_scalar(f["deg"][:, :], f["deg"][:, :], 1e-30, None, ALU.max))
            v.sem_inc(ready, 1)
            v.wait_ge(rooted, 1)
            keep(v.reciprocal(f["dinv"][:, :], f["begin"][:, :]))
            keep(v.tensor_tensor(f["dinv"][:, :], f["dinv"][:, :], f["carry"][:, :], ALU.mult))
            v.sem_inc(ready, 1)
            fl = rec[:, :, :].bitcast(F32)
            v.wait_ge(turned, 1)
            v.wait_ge(posed, 2)
            for i, (k, at) in enumerate(TURN):
                out = fl if at >= LAST else rec
                v.tensor_copy(out[:, :, at:at + TILES], ps[i][:, 0:TILES * ng].rearrange("p (c g) -> p g c", c=TILES))
            v.tensor_copy(rec[:, :, PAY + 1:PAY + 2 * TILES:2],
                          ps[0][:, TILES * ng:2 * TILES * ng].rearrange("p (c g) -> p g c", c=TILES)).then_inc(rec_ok, 1)

        @block.scalar
        def _(a):
            a.wait_ge(ready, 1)
            a.activation(f["begin"][:, :], f["deg"][:, :], ACT.Sqrt).then_inc(rooted, 1)

        @block.tensor
        def _(pe):
            pe.wait_ge(ended, 1)
            for k in range(3):
                ins = pe.transpose(ps_e[0:1, 64 * k:64 * k + ng], ends[:, k:k + 1], w.ident[0:ng, 0:ng])
            ins.then_inc(ends_back, 1)
            pe.wait_ge(carried, 1)
            for k in range(2):
                ins = pe.transpose(ps_e[0:ng, 256 + k:257 + k], crow[:, k, 0:ng], w.ident[0:1, 0:1])
            ins.then_inc(col_back, 1)
            pe.wait_ge(ready, 2)
            for i, (k, at) in enumerate(TURN):
                for c in range(TILES):
                    pe.transpose(ps[i][:, c * ng:(c + 1) * ng], f[k][:, c * P:(c + 1) * P], w.ident[0:ng, 0:ng])
            for c in range(TILES):
                ins = pe.transpose(ps[0][:, (TILES + c) * ng:(TILES + c + 1) * ng], f["pay"][:, c * P:(c + 1) * P],
                                   w.ident[0:ng, 0:ng])
            ins.then_inc(turned, 1)


def dense_pass(nc, w, ng, nodes, x, out, t2, facts, slots, mapped):
    count = -(-nodes // G)
    half = -(-(count // 2) // 4) * 4
    with ExitStack() as ctx:
        room = Room(nc, ctx, "dense")
        xin, u, z, x2, x3b, z4, o = (room.two(k, [P, G], count=4) for k in "xin u z x2 x3b z4 o".split())
        x1T, rT, x3T, hT, hsq = (room.two(k, [P, G]) for k in "x1T rT x3T hT hsq".split())
        junk2 = room.sb("junk2", [P, G])
        junk4 = room.sb("junk4", [P, G])
        st = room.two("st", [P, 6 * TILES])
        mv = room.two("mv", [P, 2 * TILES])
        sd23, rs23, hst = (room.two(k, [P, 2 * TILES]) for k in "sd23 rs23 hst".split())
        sd1, rs1, sq2, hm2, hvar, sdh, rsh, sq4, sd4, rs4 = (
            room.two(k, [P, TILES]) for k in "sd1 rs1 sq2 hm2 hvar sdh rsh sq4 sd4 rs4".split())
        rec = room.two("rec", [P, REC], I32)
        got = room.two("got", [P, 2 * TILES], I32)
        ps_t1, ps_t3, ps_u, ps_w, ps_z, ps_h = (room.bank(k) for k in ("t1", "t3", "u", "w", "z", "h"))
        ps_p = [room.bank("p0"), room.bank("p1")]
        names = ("y st settled mv sd1 rs1 u t1 x1T ua rT zp z sq2 sd23 rs23 x2 x3b t3 x3T wa hT hsq pp hst hm2 "
                 "hvar0 hvar sdh rsh z4 sq4 sd4 rs4 o").split()
        done = {k: room.sem(k + "_done") for k in names}
        x_in, x2_out, o_out = room.sem2("x_in", 4), room.sem2("x2_out", 4), room.sem2("o_out", 4)
        rec_in, put, found, kept = (room.swdge2(k) for k in ("rec_in", "put", "found", "kept"))

        def rows(table, s):
            at = min(s.lin(G), nodes - G) if s.fixed else s.lin(G)
            return table[bass.ds(at, G), :].rearrange("(p c) d -> p (c d)", c=TILES)

        def each_tile(factors):
            return factors.unsqueeze(2).broadcast_to([P, TILES, D])

        block = room.block()

        @block.sync
        def _(sp):
            def load(s):
                k = s.slot(4)
                room.hold(sp, done["u"], s.lin(1, -3))
                sp.dma_start(xin[k][:, :], rows(x, s)).then_inc(x_in[k], 16)

            def store(s, table, buf, written, landed):
                k = s.slot(4)
                if s.fixed and s.lin() == count - 1:
                    sp.wait_ge(landed[(count - 2) % 4], 16 * ((count - 2) // 4 + 1))
                room.hold(sp, written, s.lin(1, 1))
                sp.dma_start(rows(table, s), buf[k][:, :]).then_inc(landed[k], 16)

            run_groups(sp, count, 4, [(0, load), (8, lambda s: store(s, t2, x2, done["x2"], x2_out)),
                                      (13, lambda s: store(s, out, o, done["o"], o_out))])
            for k in range(4):
                sp.wait_ge(x2_out[k], 16 * uses(count, k, 4))
                sp.wait_ge(o_out[k], 16 * uses(count, k, 4))

        @block.vector
        def _(v):
            def stats1(s):
                k = s.slot()
                v.wait_ge(done["y"], s.lin(1, 1))
                for c in range(TILES):
                    ins = v.bn_stats(st[k][:, 6 * c:6 * c + 6], tile(xin[s.slot(4)], c))
                ins.then_inc(done["st"], 1)

            def moments1(s):
                k = s.slot()
                v.wait_ge(done["st"], s.lin(1, 1))
                v.sem_inc(done["settled"], 1)
                for c in range(TILES):
                    ins = v.bn_aggr(mv[k][:, 2 * c:2 * c + 2], st[k][:, 6 * c:6 * c + 6])
                ins.then_inc(done["mv"], 1)

            def invert1(s):
                k = s.slot()
                v.wait_ge(done["sd1"], s.lin(1, 1))
                v.reciprocal(rs1[k][:, :], sd1[k][:, :]).then_inc(done["rs1"], 1)

            def scale1(s):
                k, k4 = s.slot(), s.slot(4)
                v.wait_ge(done["rs1"], s.lin(1, 1))
                for c in range(TILES):
                    ins = v.tensor_scalar(tile(u[k4], c), tile(xin[k4], c), mv[k][:, 2 * c:2 * c + 1],
                                          rs1[k][:, c:c + 1], ALU.subtract, ALU.mult)
                ins.then_inc(done["u"], 1)

            def add_mlp(s):
                k4 = s.slot(4)
                v.wait_ge(done["zp"], s.lin(1, 1))
                v.tensor_tensor(z[k4][:, :], ps_z[:, :], u[k4][:, :], ALU.add).then_inc(done["z"], 1)

            def invert23(s):
                k = s.slot()
                v.wait_ge(done["sd23"], s.lin(1, 1))
                v.reciprocal(rs23[k][:, :], sd23[k][:, :]).then_inc(done["rs23"], 1)

            def scale3(s):
                k, k4 = s.slot(), s.slot(4)
                v.wait_ge(done["rs23"], s.lin(1, 1))
                for c in range(TILES):
                    ins = v.scalar_tensor_tensor(out=tile(x3b[k4], c), in0=tile(z[k4], c),
                                                 scalar=rs23[k][:, TILES + c:TILES + c + 1], in1=w.gb2c[:, :],
                                                 op0=ALU.mult, op1=ALU.add)
                ins.then_inc(done["x3b"], 1)

            def scale2(s):
                k, k4 = s.slot(), s.slot(4)
                wait(v, x2_out[k4], s.lin(16, 0, div=4))
                v.tensor_tensor(tiles3(x2[k4]), tiles3(z[k4]), each_tile(rs23[k][:, 0:TILES]), ALU.mult).then_inc(done["x2"], 1)

            def moments_h(s):
                k = s.slot()
                v.wait_ge(done["pp"], s.lin(1, 1))
                v.tensor_copy(hst[k][:, :], ps_h[:, 0:2 * TILES]).then_inc(done["hst"], 1)

            def square_h(s):
                k = s.slot()
                v.wait_ge(done["hst"], s.lin(1, 1))
                v.tensor_tensor(hm2[k][:, :], hst[k][:, TILES:2 * TILES], hst[k][:, TILES:2 * TILES], ALU.mult).then_inc(done["hm2"], 1)

            def var_h(s):
                k = s.slot()
                v.wait_ge(done["hm2"], s.lin(1, 1))
                v.tensor_tensor(hvar[k][:, :], hst[k][:, 0:TILES], hm2[k][:, :], ALU.subtract).then_inc(done["hvar0"], 1)

            def clamp_h(s):
                k = s.slot()
                v.wait_ge(done["hvar0"], s.lin(1, 1))
                v.tensor_scalar(hvar[k][:, :], hvar[k][:, :], 0.0, None, ALU.max).then_inc(done["hvar"], 1)

            def invert_h(s):
                k = s.slot()
                v.wait_ge(done["sdh"], s.lin(1, 1))
                v.reciprocal(rsh[k][:, :], sdh[k][:, :]).then_inc(done["rsh"], 1)

            def add_gcn(s):
                k, k4 = s.slot(), s.slot(4)
                v.wait_ge(done["rsh"], s.lin(1, 1))
                for c in range(TILES):
                    ins = v.scalar_tensor_tensor(out=tile(z4[k4], c), in0=tile(ps_p[k], c), scalar=rsh[k][:, c:c + 1],
                                                 in1=tile(x3b[k4], c), op0=ALU.mult, op1=ALU.add)
                ins.then_inc(done["z4"], 1)

            def invert4(s):
                k = s.slot()
                v.wait_ge(done["sd4"], s.lin(1, 1))
                v.reciprocal(rs4[k][:, :], sd4[k][:, :]).then_inc(done["rs4"], 1)

            def scale4(s):
                k, k4 = s.slot(), s.slot(4)
                v.wait_ge(done["rs4"], s.lin(1, 1))
                wait(v, o_out[k4], s.lin(16, 0, div=4))
                v.tensor_tensor(tiles3(o[k4]), tiles3(z4[k4]), each_tile(rs4[k][:, :]), ALU.mult).then_inc(done["o"], 1)

            run_groups(v, count, 4, [(8, moments_h), (1, invert1), (5, invert23), (8, square_h), (5, scale3),
                                     (8, var_h), (1, scale1), (8, clamp_h), (3, add_mlp), (5, scale2), (10, invert4),
                                     (0, stats1), (10, scale4), (0, moments1), (8, invert_h), (8, add_gcn)])

        @block.scalar
        def _(a):
            def root1(s):
                k = s.slot()
                a.wait_ge(done["mv"], s.lin(1, 1))
                a.activation(sd1[k][:, :], mv[k][:, 1::2], ACT.Sqrt, bias=w.eps[:, :]).then_inc(done["sd1"], 1)

            def mlp_in(s):
                k = s.slot()
                a.wait_ge(done["t1"], s.lin(1, 1))
                a.copy(x1T[k][:, :], ps_t1[:, :]).then_inc(done["x1T"], 1)

            def mlp_mid(s):
                k = s.slot()
                a.wait_ge(done["ua"], s.lin(1, 1))
                a.activation(rT[k][:, :], ps_u[:, :], ACT.Relu, bias=w.col("c1")).then_inc(done["rT"], 1)

            def squares2(s):
                k, k4 = s.slot(), s.slot(4)
                a.wait_ge(done["z"], s.lin(1, 1))
                for c in range(TILES):
                    ins = a.activation(tile(junk2, c), tile(z[k4], c), ACT.Square, accum_out=sq2[k][:, c:c + 1])
                ins.then_inc(done["sq2"], 1)

            def root23(s):
                k = s.slot()
                a.wait_ge(done["sq2"], s.lin(1, 1))
                a.activation(sd23[k][:, 0:TILES], sq2[k][:, :], ACT.Sqrt, bias=w.eps[:, :], scale=1.0 / D)
                a.activation(sd23[k][:, TILES:2 * TILES], sq2[k][:, :], ACT.Sqrt, bias=w.eps2[:, :],
                             scale=(1.0 + EPS) / D).then_inc(done["sd23"], 1)

            def gcn_in(s):
                k = s.slot()
                a.wait_ge(done["t3"], s.lin(1, 1))
                a.activation(x3T[k][:, :], ps_t3[:, :], ACT.Identity, bias=w.neggb2[:, :]).then_inc(done["x3T"], 1)

            def gcn_mid(s):
                k = s.slot()
                a.wait_ge(done["wa"], s.lin(1, 1))
                wait(a, done["pp"], s.lin(1, -1))
                a.activation(hT[k][:, :], ps_w[:, :], ACT.Relu, bias=w.col("gb1")).then_inc(done["hT"], 1)

            def square_h(s):
                k = s.slot()
                a.wait_ge(done["hT"], s.lin(1, 1))
                a.activation(hsq[k][:, :], hT[k][:, :], ACT.Square).then_inc(done["hsq"], 1)

            def root_h(s):
                k = s.slot()
                a.wait_ge(done["hvar"], s.lin(1, 1))
                a.activation(sdh[k][:, :], hvar[k][:, :], ACT.Sqrt, bias=w.eps[:, :]).then_inc(done["sdh"], 1)

            def squares4(s):
                k, k4 = s.slot(), s.slot(4)
                a.wait_ge(done["z4"], s.lin(1, 1))
                for c in range(TILES):
                    ins = a.activation(tile(junk4, c), tile(z4[k4], c), ACT.Square, accum_out=sq4[k][:, c:c + 1])
                ins.then_inc(done["sq4"], 1)

            def root4(s):
                k = s.slot()
                a.wait_ge(done["sq4"], s.lin(1, 1))
                a.activation(sd4[k][:, :], sq4[k][:, :], ACT.Sqrt, bias=w.eps[:, :], scale=1.0 / D).then_inc(done["sd4"], 1)

            run_groups(a, count, 4, [(4, squares2), (2, mlp_mid), (4, root23), (6, gcn_mid), (9, squares4), (6, square_h),
                                     (9, root4), (8, root_h), (5, gcn_in), (1, mlp_in), (0, root1)])

        @block.tensor
        def _(pe):
            def turn1(s):
                pe.wait_ge(done["u"], s.lin(1, 1))
                wait(pe, done["x1T"], s.lin())
                for c in range(TILES):
                    ins = pe.transpose(tile(ps_t1, c), tile(u[s.slot(4)], c), w.ident[:, :])
                ins.then_inc(done["t1"], 1)

            def mlp1(s):
                k = s.slot()
                pe.wait_ge(done["x1T"], s.lin(1, 1))
                wait(pe, done["rT"], s.lin())
                pe.matmul(ps_u[:, :], w.u1c[:, :], x1T[k][:, :], start=True, stop=True).then_inc(done["ua"], 1)

            def mlp2(s):
                k = s.slot()
                pe.wait_ge(done["rT"], s.lin(1, 1))
                wait(pe, done["z"], s.lin())
                for c in range(TILES):
                    pe.matmul(tile(ps_z, c), w.ones16[:, :], w.c2s[:, :], start=True, stop=False)
                    ins = pe.matmul(tile(ps_z, c), tile(rT[k], c), w.u2c[:, :], start=False, stop=True)
                ins.then_inc(done["zp"], 1)

            def turn3(s):
                pe.wait_ge(done["x3b"], s.lin(1, 1))
                wait(pe, done["x3T"], s.lin())
                for c in range(TILES):
                    ins = pe.transpose(tile(ps_t3, c), tile(x3b[s.slot(4)], c), w.ident[:, :])
                ins.then_inc(done["t3"], 1)

            def gcn1(s):
                k = s.slot()
                pe.wait_ge(done["x3T"], s.lin(1, 1))
                wait(pe, done["hT"], s.lin())
                pe.matmul(ps_w[:, :], w.g1c[:, :], x3T[k][:, :], start=True, stop=True).then_inc(done["wa"], 1)

            def gcn2(s):
                k = s.slot()
                pe.wait_ge(done["hT"], s.lin(1, 1))
                wait(pe, done["z4"], s.lin(1, -1))
                for c in range(TILES):
                    pe.matmul(tile(ps_p[k], c), tile(hT[k], c), w.g2c[:, :], start=True, stop=True)
                wait(pe, done["hst"], s.lin())
                for c in range(TILES):
                    pe.matmul(ps_h[:, TILES + c:TILES + c + 1], tile(hT[k], c), w.mean_col[:, :], start=True, stop=True)
                pe.wait_ge(done["hsq"], s.lin(1, 1))
                for c in range(TILES):
                    ins = pe.matmul(ps_h[:, c:c + 1], tile(hsq[k], c), w.mean_col[:, :], start=True, stop=True)
                ins.then_inc(done["pp"], 1)

            run_groups(pe, count, 4, [(2, mlp1), (6, gcn1), (3, mlp2), (7, gcn2), (5, turn3), (1, turn1)])

        @block.gpsimd
        def _(pool):
            top = pool.to_reg(nodes - 1)

            def add_b0(s):
                k4 = s.slot(4)
                pool.wait_ge(x_in[k4], s.lin(16, 16, div=4))
                pool.tensor_tensor(tiles3(xin[k4]), tiles3(xin[k4]), over_tiles(w.row("b0")), ALU.add).then_inc(done["y"], 1)

            def after(base):
                return lambda s: add_b0(Step(s.j, s.unroll, s.off + base))

            def put_load(s):
                k = s.slot()
                room.hold(pool, put[k], s.lin(16 * TILES, 0, div=2))
                pool.dma_start(rec[k][:, :], cols_of(facts, s.lin(), REC)).then_inc(rec_in[k], 16)

            def put_slots(s):
                k = s.slot()
                room.hold(pool, rec_in[k], s.lin(16, 16, div=2))
                for c in range(TILES):
                    pool.indirect_dma_start(slots, bass.IndirectOffsetOnAxis(rec[k][:, SCAT + c:SCAT + c + 1], 0),
                                            rec[k][:, PAY + 2 * c:PAY + 2 * c + 2], None, bounds_check=top,
                                            oob_is_err=False).then_inc(put[k], 16)

            def find_load(s):
                k = s.slot()
                room.hold(pool, found[k], s.lin(16 * TILES, 0, div=2))
                pool.dma_start(rec[k][:, :], cols_of(facts, s.lin(), REC)).then_inc(rec_in[k], 16)

            def find_slots(s):
                k = s.slot()
                room.hold(pool, kept[k], s.lin(16, 0, div=2))
                room.hold(pool, rec_in[k], s.lin(16, 16 * (uses(ng, k, 2) + 1), div=2))
                for c in range(TILES):
                    pool.indirect_dma_start(got[k][:, 2 * c:2 * c + 2], None, slots,
                                            bass.IndirectOffsetOnAxis(rec[k][:, SRC + c:SRC + c + 1], 0),
                                            bounds_check=top, oob_is_err=False).then_inc(found[k], 16)

            def keep_slots(s):
                k = s.slot()
                room.hold(pool, found[k], s.lin(16 * TILES, 16 * TILES, div=2))
                pool.dma_start(cols_of(mapped, s.lin(), 2 * TILES),
                               got[k][:, :]).then_inc(kept[k], 16)

            def paced(base, groups, loops, stages):
                def dense_at(s, part):
                    n = Step(s.j, 4, 2 * s.off + part + base) if not s.fixed else Step(0, 4, 2 * s.lin() + part + base)
                    if n.fixed and not base <= n.lin() < base + groups:
                        return
                    add_b0(n)
                run_groups(pool, loops, 2, stages + [(0, lambda s: dense_at(s, 0)), (0, lambda s: dense_at(s, 1))])
                for n in range(base + 2 * loops, base + groups):
                    add_b0(Step(0, 4, n))

            paced(0, half, ng, [(1, put_slots), (0, put_load)])
            for k in range(2):
                pool.wait_ge(put[k], 16 * TILES * uses(ng, k, 2))
            paced(half, count - half, ng, [(2, keep_slots), (1, find_slots), (0, find_load)])
            for k in range(2):
                pool.wait_ge(kept[k], 16 * uses(ng, k, 2))


def sum_layer(nc, w, ng, nodes, x, facts, along, t1, s1):
    with ExitStack() as ctx:
        room = Room(nc, ctx, "sum")
        rec = room.two("rec", [P, REC], I32)
        keep = room.two("keep", [P, G])
        xs = room.two("xs", [P, G])
        xd = room.two("xd", [P, G])
        ys = room.two("ys", [P, G])
        yd = room.two("yd", [P, G])
        hT = room.two("hT", [P, G])
        x1 = room.two("x1", [P, G])
        x1s = room.two("x1s", [P, G])
        ps_t = [room.bank(f"t{i}") for i in range(2)]
        ps_w = [room.bank(f"w{i}") for i in range(2)]
        nd = Norm(room, "nd", w.eps[:, :])
        ns = Norm(room, "ns", w.eps[:, :])
        done = {k: room.sem(k + "_done") for k in "turn scan wsum ys yd ydb x1 x1s".split()}
        rec_in, keep_in, x1_out, x1s_out = (room.sem2(k) for k in ("rec_in", "keep_in", "x1_out", "x1s_out"))
        x_in = room.swdge2("x_in")
        block = room.block()

        @block.sync
        def _(sp):
            def load(s):
                k = s.slot()
                room.hold(sp, done["x1"], s.lin(1, -1))
                sp.dma_start(rec[k][:, :], cols_of(facts, s.lin(), REC)).then_inc(rec_in[k], 16)
                sp.dma_start(keep[k][:, :], along[s.lin(), KEEP_F, :].partition_broadcast(P)
                             if s.fixed else along[bass.ds(s.lin(), 1), KEEP_F, :].rearrange("a g -> (a g)")
                             .partition_broadcast(P)).then_inc(keep_in[k], 16)

            def store(s):
                k = s.slot()
                room.hold(sp, done["x1s"], s.lin(1, 1))
                sp.dma_start(edge_rows(s1, s.lin()), tiles3(x1s[k])).then_inc(x1s_out[k], 16)
                room.hold(sp, done["x1"], s.lin(1, 1))
                sp.dma_start(edge_rows(t1, s.lin()), tiles3(x1[k])).then_inc(x1_out[k], 16)

            run_groups(sp, ng, 2, [(0, load), (2, store)])
            for k in range(2):
                sp.wait_ge(x1_out[k], 16 * ((ng + 1 - k) // 2))
                sp.wait_ge(x1s_out[k], 16 * ((ng + 1 - k) // 2))

        @block.gpsimd
        def _(pool):
            top = pool.to_reg(nodes - 1)

            def gather(s):
                k = s.slot()
                room.hold(pool, done["turn"], s.lin(1, -1))
                room.hold(pool, done["ydb"], s.lin(1, -1))
                room.hold(pool, rec_in[k], s.lin(16, 16, div=2))
                for c in range(TILES):
                    for buf, at in ((xs, SRC), (xd, DSTC)):
                        pool.indirect_dma_start(tile(buf[k], c), None, x,
                                                bass.IndirectOffsetOnAxis(rec[k][:, at + c:at + c + 1], 0),
                                                bounds_check=top, oob_is_err=False).then_inc(x_in[k], 16)

            run_groups(pool, ng, 2, [(0, gather)])

        @block.tensor
        def _(pe):
            def turn(s):
                k = s.slot()
                pe.wait_ge(x_in[k], s.lin(128, 128, div=2))
                wait(pe, done["scan"], s.lin(1, -1))
                for c in range(TILES):
                    ins = pe.transpose(tile(ps_t[k], c), tile(xs[k], c), w.ident[:, :])
                ins.then_inc(done["turn"], 1)

            def product(s):
                k = s.slot()
                pe.wait_ge(done["scan"], s.lin(1, 1))
                wait(pe, done["yd"], s.lin(1, -1))
                for c in range(TILES):
                    ins = pe.matmul(tile(ps_w[k], c), tile(hT[k], c), w.t(0), start=True, stop=True)
                ins.then_inc(done["wsum"], 1)

            run_groups(pe, ng, 2, [(1, product), (0, turn)])

        @block.vector
        def _(v):
            def scan(s):
                k = s.slot()
                wait(v, done["wsum"], s.lin(1, -1))
                v.wait_ge(keep_in[k], s.lin(16, 16, div=2))
                v.wait_ge(done["turn"], s.lin(1, 1))
                wait(v, done["scan"], s.lin())
                first = s.fixed and s.lin() == 0
                v.tensor_tensor_scan(hT[k][:, :], keep[k][:, :], ps_t[k][:, :], 0.0 if first else hT[1 - k][:, G - 1:G],
                                     ALU.mult, ALU.add).then_inc(done["scan"], 1)

            def src_stats(s):
                k = s.slot()
                v.wait_ge(x_in[k], s.lin(128, 128, div=2))
                v.tensor_tensor(tiles3(ys[k]), tiles3(xs[k]), over_tiles(w.row("b0")), ALU.add).then_inc(done["ys"], 1)
                v.wait_ge(done["ys"], s.lin(1, 1))
                ns.stats(v, s, ys[k])

            def dst_stats(s):
                k = s.slot()
                v.wait_ge(done["wsum"], s.lin(1, 1))
                v.tensor_tensor(yd[k][:, :], ps_w[k][:, :], xd[k][:, :], ALU.add).then_inc(done["yd"], 1)
                v.wait_ge(done["yd"], s.lin(1, 1))
                v.tensor_tensor(tiles3(yd[k]), tiles3(yd[k]), over_tiles(w.row("b0")), ALU.add).then_inc(done["ydb"], 1)
                v.wait_ge(done["ydb"], s.lin(1, 1))
                nd.stats(v, s, yd[k])

            def src_out(s):
                k = s.slot()
                ns.finish(v, s, ys[k], x1s[k], done["x1s"],
                          out_free=lambda: wait(v, x1s_out[k], s.lin(16, 0, div=2)))

            def dst_out(s):
                k = s.slot()
                nd.finish(v, s, yd[k], x1[k], done["x1"], mask=rec[k][:, LAST:LAST + TILES].bitcast(F32),
                          out_free=lambda: wait(v, x1_out[k], s.lin(16, 0, div=2)))

            run_groups(v, ng, 2, [(0, scan), (1, dst_stats), (0, src_stats), (1, dst_out), (0, src_out)])

        @block.scalar
        def _(a):
            run_groups(a, ng, 2, [(1, lambda s: nd.root(a, s)), (0, lambda s: ns.root(a, s))])


def max_layer(nc, w, ng, nodes, facts, along, ew_row, mapped, t1, s1, t2):
    rows_all = ng * G
    with ExitStack() as ctx:
        room = Room(nc, ctx, "max")
        rec = room.two("rec", [P, REC], I32)
        mi = room.two("mi", [P, 2 * TILES], I32)
        flags = room.two("flags", [P, 2, G])
        wr = room.two("wr", [1, G])
        xs = room.two("xs", [P, G])
        xd = room.two("xd", [P, G])
        xsT = room.two("xsT", [P, G])
        xdT = room.two("xdT", [P, G])
        hT = room.two("hT", [P, G])
        ag = room.two("ag", [P, G])
        rT = room.two("rT", [P, G])
        z = room.two("z", [P, G])
        x2 = room.two("x2", [P, G])
        ps_d, ps_s, ps_h, ps_m, ps_r = (room.bank(k) for k in "dshmr")
        ps_z = [room.bank("z0"), room.bank("z1")]
        nz = Norm(room, "nz", w.eps[:, :])
        done = {k: room.sem(k + "_done") for k in "turnd turns xsT spread ha hT ma max ra rT zp z x2".split()}
        rec_in, mi_in, flags_in, wr_in, xd_in, xs_in, x2_out = (
            room.sem2(k) for k in ("rec_in", "mi_in", "flags_in", "wr_in", "xd_in", "xs_in", "x2_out"))
        over_in = room.swdge2("over_in")
        block = room.block()

        def group(s):
            return (ng - 1) - s.lin() if s.fixed else s.lin(-1, ng - 1)

        @block.sync
        def _(sp):
            def load(s):
                k = s.slot()
                room.hold(sp, done["x2"], s.lin(1, -1))
                g = group(s)
                sp.dma_start(mi[k][:, :], cols_of(mapped, g, 2 * TILES)).then_inc(mi_in[k], 16)
                sp.dma_start(tiles3(xs[k]), edge_rows(s1, g)).then_inc(xs_in[k], 16)
                sp.dma_start(tiles3(xd[k]), edge_rows(t1, g)).then_inc(xd_in[k], 16)
                sp.dma_start(flags[k][:, :, :], along[bass.ds(g, 1), PEN_B:KEEP_B + 1, :]
                             .rearrange("a k g -> (a k) g").partition_broadcast(P)).then_inc(flags_in[k], 16)
                sp.dma_start(wr[k][:, :], ew_row[bass.ds(g, 1), :]).then_inc(wr_in[k], 16)
                sp.dma_start(rec[k][:, :], cols_of(facts, g, REC)).then_inc(rec_in[k], 16)

            def store(s):
                k = s.slot()
                room.hold(sp, done["x2"], s.lin(1, 1))
                sp.dma_start(edge_rows(t2, group(s), nodes), tiles3(x2[k])).then_inc(x2_out[k], 16)

            run_groups(sp, ng, 2, [(3, store), (0, load)])
            for k in range(2):
                sp.wait_ge(x2_out[k], 16 * ((ng + 1 - k) // 2))

        @block.gpsimd
        def _(pool):
            top = pool.to_reg(rows_all - 1)

            def overlay(s):
                k = s.slot()
                room.hold(pool, xs_in[k], s.lin(16, 16, div=2))
                room.hold(pool, mi_in[k], s.lin(16, 16, div=2))
                for c in range(TILES):
                    pool.indirect_dma_start(tile(xs[k], c), None, t1,
                                            bass.IndirectOffsetOnAxis(mi[k][:, 2 * c:2 * c + 1], 0),
                                            bounds_check=top, oob_is_err=False).then_inc(over_in[k], 16)

            run_groups(pool, ng, 2, [(0, overlay)])

        @block.tensor
        def _(pe):
            def turns(s):
                k = s.slot()
                pe.wait_ge(xd_in[k], s.lin(16, 16, div=2))
                wait(pe, done["spread"], s.lin())
                for c in range(TILES):
                    ins = pe.transpose(tile(ps_d, c), tile(xd[k], c), w.ident[:, :])
                ins.then_inc(done["turnd"], 1)
                pe.wait_ge(over_in[k], s.lin(64, 64, div=2))
                wait(pe, done["xsT"], s.lin())
                for c in range(TILES):
                    ins = pe.transpose(tile(ps_s, c), tile(xs[k], c), w.ident[:, :])
                ins.then_inc(done["turns"], 1)

            def hidden(s):
                k = s.slot()
                wait(pe, done["hT"], s.lin())
                pe.wait_ge(wr_in[k], s.lin(16, 16, div=2))
                pe.matmul(ps_h[:, :], w.wrow[:, :], wr[k][:, :], start=True, stop=False)
                pe.wait_ge(done["spread"], s.lin(1, 1))
                pe.matmul(ps_h[:, :], w.mat("M1D"), xdT[k][:, :], start=False, stop=False)
                pe.wait_ge(done["xsT"], s.lin(1, 1))
                pe.matmul(ps_h[:, :], w.mat("M1S"), xsT[k][:, :], start=False, stop=True).then_inc(done["ha"], 1)

            def message(s):
                k = s.slot()
                pe.wait_ge(done["hT"], s.lin(1, 1))
                wait(pe, done["max"], s.lin())
                pe.matmul(ps_m[:, :], w.mat("M2"), hT[k][:, :], start=True, stop=True).then_inc(done["ma"], 1)

            def update1(s):
                k = s.slot()
                wait(pe, done["rT"], s.lin())
                pe.matmul(ps_r[:, :], w.mat("U1X"), xdT[k][:, :], start=True, stop=False)
                pe.wait_ge(done["max"], s.lin(1, 1))
                pe.matmul(ps_r[:, :], w.mat("U1A"), ag[k][:, :], start=False, stop=True).then_inc(done["ra"], 1)

            def update2(s):
                k = s.slot()
                wait(pe, done["z"], s.lin(1, -1))
                pe.wait_ge(done["rT"], s.lin(1, 1))
                for c in range(TILES):
                    pe.matmul(tile(ps_z[k], c), tile(xdT[k], c), w.ident[:, :], start=True, stop=False)
                    ins = pe.matmul(tile(ps_z[k], c), tile(rT[k], c), w.mat("U2"), start=False, stop=True)
                ins.then_inc(done["zp"], 1)

            run_groups(pe, ng, 2, [(1, update1), (0, turns), (0, hidden), (1, update2), (0, message)])

        @block.vector
        def _(v):
            def spread(s):
                k = s.slot()
                wait(v, done["zp"], s.lin(1, -1))
                v.wait_ge(flags_in[k], s.lin(16, 16, div=2))
                v.wait_ge(done["turnd"], s.lin(1, 1))
                wait(v, done["spread"], s.lin())
                first = s.fixed and s.lin() == 0
                v.tensor_tensor_scan(xdT[k][:, ::-1], flags[k][:, 1, ::-1], ps_d[:, ::-1],
                                     0.0 if first else xdT[1 - k][:, 0:1], ALU.mult, ALU.add).then_inc(done["spread"], 1)

            def maximum(s):
                k = s.slot()
                wait(v, done["ra"], s.lin(1, -1))
                v.wait_ge(done["ma"], s.lin(1, 1))
                wait(v, done["max"], s.lin())
                first = s.fixed and s.lin() == 0
                v.tensor_tensor_scan(ag[k][:, ::-1], flags[k][:, 0, ::-1], ps_m[:, ::-1],
                                     0.0 if first else ag[1 - k][:, 0:1], ALU.add, ALU.max).then_inc(done["max"], 1)

            def stats(s):
                k = s.slot()
                v.wait_ge(done["zp"], s.lin(1, 1))
                v.tensor_tensor(tiles3(z[k]), tiles3(ps_z[k]), over_tiles(w.row("c2")), ALU.add).then_inc(done["z"], 1)
                v.wait_ge(done["z"], s.lin(1, 1))
                nz.stats(v, s, z[k])

            def finish(s):
                k = s.slot()
                v.wait_ge(rec_in[k], s.lin(16, 16, div=2))
                nz.finish(v, s, z[k], x2[k], done["x2"], mask=rec[k][:, FIRST:FIRST + TILES].bitcast(F32),
                          out_free=lambda: wait(v, x2_out[k], s.lin(16, 0, div=2)))

            run_groups(v, ng, 2, [(0, spread), (1, stats), (0, maximum), (1, finish)])

        @block.scalar
        def _(a):
            def copy_src(s):
                k = s.slot()
                wait(a, done["ha"], s.lin(1, -1))
                a.wait_ge(done["turns"], s.lin(1, 1))
                a.copy(xsT[k][:, :], ps_s[:, :]).then_inc(done["xsT"], 1)

            def relu1(s):
                k = s.slot()
                wait(a, done["ma"], s.lin(1, -1))
                a.wait_ge(done["ha"], s.lin(1, 1))
                a.activation(hT[k][:, :], ps_h[:, :], ACT.Relu, bias=w.col("mb1")).then_inc(done["hT"], 1)

            def relu2(s):
                k = s.slot()
                wait(a, done["zp"], s.lin(1, -1))
                a.wait_ge(done["ra"], s.lin(1, 1))
                a.activation(rT[k][:, :], ps_r[:, :], ACT.Relu, bias=w.c1b[:, :]).then_inc(done["rT"], 1)

            run_groups(a, ng, 2, [(1, relu2), (0, copy_src), (0, relu1), (1, lambda s: nz.root(a, s))])


def attention_layer(nc, w, ng, nodes, facts, along, edge_attr, mapped, t2, t3, s3, d3):
    rows_all = nodes + ng * G
    with ExitStack() as ctx:
        room = Room(nc, ctx, "att")
        rec = room.two("rec", [P, REC], I32)
        mi = room.two("mi", [P, 2 * TILES], I32)
        keep = room.two("keep", [P, G])
        ea = room.two("ea", [P, G])
        xs = room.two("xs", [P, G])
        xd = room.two("xd", [P, G])
        xsT = room.two("xsT", [P, G])
        eT = room.two("eT", [P, G])
        xdT = room.two("xdT", [P, G])
        q = room.two("q", [P, G])
        ev = room.two("ev", [P, G])
        qk = room.two("qk", [P, G])
        qke = room.two("qke", [P, G])
        sc = room.two("sc", [P, G])
        pr = room.two("pr", [P, G])
        m = room.two("m", [P, G])
        wv = room.two("wv", [P, G])
        zT = room.two("zT", [P, G])
        x3 = room.two("x3", [P, G])
        x3n = room.two("x3n", [P, G])
        x3s = room.two("x3s", [P, G])
        ps_d, ps_s, ps_q, ps_e, ps_k, ps_v, ps_sc, ps_z = (room.bank(k) for k in ("d", "s", "q", "e", "k", "v", "sc", "z"))
        nz = Norm(room, "nz", w.eps[:, :])
        ns = Norm(room, "ns", w.eps[:, :])
        done = {k: room.sem(k + "_done") for k in
                ("turnd turns turne xsT eT spread qa q eva ev ka qk qke sca sc pr va m sum zT turnz x3 x3n x3s").split()}
        rec_in, mi_in, keep_in, ea_in, xd_in, x3_out, x3n_out, x3s_out = (
            room.sem2(k) for k in ("rec_in", "mi_in", "keep_in", "ea_in", "xd_in", "x3_out", "x3n_out", "x3s_out"))
        xs_in = room.swdge2("xs_in")
        block = room.block()

        @block.sync
        def _(sp):
            def load(s):
                k = s.slot()
                room.hold(sp, done["x3n"], s.lin(1, -1))
                g = s.lin()
                sp.dma_start(mi[k][:, :], cols_of(mapped, g, 2 * TILES)).then_inc(mi_in[k], 16)
                sp.dma_start(tiles3(xd[k]), edge_rows(t2, g, nodes)).then_inc(xd_in[k], 16)
                sp.dma_start(tiles3(ea[k]), edge_rows(edge_attr, g)).then_inc(ea_in[k], 16)
                sp.dma_start(keep[k][:, :], along[bass.ds(g, 1), KEEP_F, :].rearrange("a g -> (a g)")
                             .partition_broadcast(P)).then_inc(keep_in[k], 16)
                sp.dma_start(rec[k][:, :], cols_of(facts, g, REC)).then_inc(rec_in[k], 16)

            def store(s):
                k = s.slot()
                g = s.lin()
                room.hold(sp, done["x3s"], s.lin(1, 1))
                sp.dma_start(edge_rows(s3, g), tiles3(x3s[k])).then_inc(x3s_out[k], 16)
                room.hold(sp, done["x3"], s.lin(1, 1))
                sp.dma_start(edge_rows(d3, g), tiles3(x3[k])).then_inc(x3_out[k], 16)
                room.hold(sp, done["x3n"], s.lin(1, 1))
                sp.dma_start(edge_rows(t3, g), tiles3(x3n[k])).then_inc(x3n_out[k], 16)

            run_groups(sp, ng, 2, [(3, store), (0, load)])
            for k in range(2):
                for sem in (x3_out, x3n_out, x3s_out):
                    sp.wait_ge(sem[k], 16 * ((ng + 1 - k) // 2))

        @block.gpsimd
        def _(pool):
            top = pool.to_reg(rows_all - 1)

            def gather(s):
                k = s.slot()
                room.hold(pool, done["turns"], s.lin(1, -1))
                room.hold(pool, done["x3s"], s.lin(1, -1))
                room.hold(pool, mi_in[k], s.lin(16, 16, div=2))
                for c in range(TILES):
                    pool.indirect_dma_start(tile(xs[k], c), None, t2,
                                            bass.IndirectOffsetOnAxis(mi[k][:, 2 * c + 1:2 * c + 2], 0),
                                            bounds_check=top, oob_is_err=False).then_inc(xs_in[k], 16)

            run_groups(pool, ng, 2, [(0, gather)])

        @block.tensor
        def _(pe):
            def turn(s, buf, bank, arrived, per, freed, over):
                k = s.slot()
                pe.wait_ge(arrived[k], s.lin(per, per, div=2))
                wait(pe, freed, s.lin())
                for c in range(TILES):
                    ins = pe.transpose(tile(bank, c), tile(buf[k], c), w.ident[:, :])
                ins.then_inc(over, 1)

            def turns(s):
                turn(s, ea, ps_e, ea_in, 16, done["ev"], done["turne"])
                turn(s, xd, ps_d, xd_in, 16, done["spread"], done["turnd"])
                turn(s, xs, ps_s, xs_in, 64, done["xsT"], done["turns"])

            def products(s):
                k = s.slot()
                pe.wait_ge(done["eT"], s.lin(1, 1))
                pe.matmul(ps_e[:, :], w.t(3), eT[k][:, :], start=True, stop=True).then_inc(done["eva"], 1)
                pe.wait_ge(done["spread"], s.lin(1, 1))
                wait(pe, done["q"], s.lin())
                pe.matmul(ps_q[:, :], w.t(1), xdT[k][:, :], start=True, stop=True).then_inc(done["qa"], 1)
                pe.wait_ge(done["xsT"], s.lin(1, 1))
                wait(pe, done["qk"], s.lin())
                pe.matmul(ps_k[:, :], w.t(2), xsT[k][:, :], start=True, stop=True).then_inc(done["ka"], 1)
                wait(pe, done["m"], s.lin())
                pe.matmul(ps_v[:, :], w.t(4), xsT[k][:, :], start=True, stop=True).then_inc(done["va"], 1)

            def scores(s):
                k = s.slot()
                pe.wait_ge(done["qke"], s.lin(1, 1))
                wait(pe, done["sc"], s.lin())
                pe.matmul(ps_sc[:, :], w.heads[:, :], qke[k][:, :], start=True, stop=True).then_inc(done["sca"], 1)

            def turn_z(s):
                k = s.slot()
                pe.wait_ge(done["zT"], s.lin(1, 1))
                wait(pe, done["x3"], s.lin())
                for c in range(TILES):
                    ins = pe.transpose(tile(ps_z, c), tile(zT[k], c), w.ident[:, :])
                ins.then_inc(done["turnz"], 1)

            run_groups(pe, ng, 2, [(1, scores), (0, turns), (1, turn_z), (0, products)])

        @block.vector
        def _(v):
            def spread(s):
                k = s.slot()
                wait(v, done["qa"], s.lin(1, -1))
                v.wait_ge(keep_in[k], s.lin(16, 16, div=2))
                v.wait_ge(done["turnd"], s.lin(1, 1))
                wait(v, done["spread"], s.lin())
                first = s.fixed and s.lin() == 0
                v.tensor_tensor_scan(xdT[k][:, :], keep[k][:, :], ps_d[:, :],
                                     0.0 if first else xdT[1 - k][:, G - 1:G], ALU.mult, ALU.add).then_inc(done["spread"], 1)

            def src_stats(s):
                k = s.slot()
                v.wait_ge(xs_in[k], s.lin(64, 64, div=2))
                ns.stats(v, s, xs[k])

            def src_out(s):
                k = s.slot()
                ns.finish(v, s, xs[k], x3s[k], done["x3s"], out_free=lambda: wait(v, x3s_out[k], s.lin(16, 0, div=2)))

            def multiply(s):
                k = s.slot()
                v.wait_ge(done["q"], s.lin(1, 1))
                v.wait_ge(done["ka"], s.lin(1, 1))
                v.scalar_tensor_tensor(out=qk[k][:, :], in0=ps_k[:, :], scalar=w.col("bk"), in1=q[k][:, :],
                                       op0=ALU.add, op1=ALU.mult).then_inc(done["qk"], 1)
                v.wait_ge(done["qk"], s.lin(1, 1))
                v.wait_ge(done["ev"], s.lin(1, 1))
                wait(v, done["sca"], s.lin(1, -1))
                v.tensor_tensor(qke[k][:, :], qk[k][:, :], ev[k][:, :], ALU.mult).then_inc(done["qke"], 1)

            def clip(s):
                k = s.slot()
                v.wait_ge(done["sca"], s.lin(1, 1))
                v.tensor_scalar(sc[k][:, :], ps_sc[:, :], -5.0, 5.0, ALU.max, ALU.min).then_inc(done["sc"], 1)

            def weigh(s):
                k = s.slot()
                v.wait_ge(done["pr"], s.lin(1, 1))
                v.wait_ge(done["va"], s.lin(1, 1))
                v.scalar_tensor_tensor(out=m[k][:, :], in0=ps_v[:, :], scalar=w.col("bv"), in1=pr[k][:, :],
                                       op0=ALU.add, op1=ALU.mult).then_inc(done["m"], 1)
                v.wait_ge(done["m"], s.lin(1, 1))
                wait(v, done["sum"], s.lin())
                first = s.fixed and s.lin() == 0
                v.tensor_tensor_scan(wv[k][:, :], keep[k][:, :], m[k][:, :],
                                     0.0 if first else wv[1 - k][:, G - 1:G], ALU.mult, ALU.add).then_inc(done["sum"], 1)
                v.wait_ge(done["sum"], s.lin(1, 1))
                wait(v, done["turnz"], s.lin(1, -1))
                v.tensor_tensor(zT[k][:, :], wv[k][:, :], xdT[k][:, :], ALU.add).then_inc(done["zT"], 1)

            def dst_stats(s):
                v.wait_ge(done["turnz"], s.lin(1, 1))
                nz.stats(v, s, ps_z)

            def dst_out(s):
                k = s.slot()
                v.wait_ge(rec_in[k], s.lin(16, 16, div=2))
                nz.finish(v, s, ps_z, x3[k], done["x3"], mask=rec[k][:, LAST:LAST + TILES].bitcast(F32),
                          out_free=lambda: wait(v, x3_out[k], s.lin(16, 0, div=2)))
                v.wait_ge(done["x3"], s.lin(1, 1))
                wait(v, x3n_out[k], s.lin(16, 0, div=2))
                dinv = rec[k][:, DINV:DINV + TILES].bitcast(F32)
                for c in range(TILES):
                    ins = v.tensor_scalar(tile(x3n[k], c), tile(x3[k], c), dinv[:, c:c + 1], None, ALU.mult)
                ins.then_inc(done["x3n"], 1)

            run_groups(v, ng, 2, [(1, clip), (0, spread), (1, weigh), (0, src_stats), (0, multiply), (1, dst_stats),
                                  (0, src_out), (1, dst_out)])

        @block.scalar
        def _(a):
            def out_of(s, out, bank, before, over, bias=None):
                a.wait_ge(before, s.lin(1, 1))
                if bias is None:
                    a.copy(out[s.slot()][:, :], bank[:, :]).then_inc(over, 1)
                else:
                    a.activation(out[s.slot()][:, :], bank[:, :], ACT.Identity, bias=bias).then_inc(over, 1)

            def inputs(s):
                wait(a, done["eva"], s.lin(1, -1))
                out_of(s, eT, ps_e, done["turne"], done["eT"])
                wait(a, done["va"], s.lin(1, -1))
                out_of(s, xsT, ps_s, done["turns"], done["xsT"])

            def factors(s):
                out_of(s, ev, ps_e, done["eva"], done["ev"], w.col("be"))
                out_of(s, q, ps_q, done["qa"], done["q"], w.col("bq"))

            def exponent(s):
                k = s.slot()
                a.wait_ge(done["sc"], s.lin(1, 1))
                a.activation(pr[k][:, :], sc[k][:, :], ACT.Exp).then_inc(done["pr"], 1)

            run_groups(a, ng, 2, [(1, exponent), (0, inputs), (0, factors), (1, lambda s: nz.root(a, s)),
                                  (0, lambda s: ns.root(a, s))])


def gcn_layer(nc, w, ng, nodes, facts, along, mapped, own_t, src_t, last, next_t=None, next_s=None, d3=None, out=None):
    with ExitStack() as ctx:
        room = Room(nc, ctx, "gcn2" if last else "gcn1")
        rec = room.two("rec", [P, REC], I32)
        mi = room.two("mi", [P, 2 * TILES], I32)
        flags = room.two("flags", [P, 2, G])
        xs = room.two("xs", [P, G])
        xd = room.two("xd", [P, G])
        xsT = room.two("xsT", [P, G])
        ws = room.two("ws", [P, G])
        aT = room.two("aT", [P, G])
        sT = room.two("sT", [P, G])
        c_d = room.two("c_d", [P, G])
        r_d = room.two("r_d", [P, G])
        h_d = room.two("h_d", [P, G])
        o_d = room.two("o_d", [P, G])
        x3 = room.two("x3", [P, G]) if last else None
        c_s = None if last else room.two("c_s", [P, G])
        r_s = None if last else room.two("r_s", [P, G])
        h_s = None if last else room.two("h_s", [P, G])
        o_s = None if last else room.two("o_s", [P, G])
        ps_s = [room.bank("s0"), room.bank("s1")]
        ps_d = [room.bank("d0"), room.bank("d1")]
        ps_pd = [room.bank("pd0"), room.bank("pd1")]
        ps_ps = [room.bank("ps0"), room.bank("ps1")]
        nd = Norm(room, "nd", w.eps[:, :])
        ns = None if last else Norm(room, "ns", w.eps[:, :])
        weight, bias = (w.mat("G2"), w.row("gb2")) if last else (w.mat("G1"), w.row("gb1"))
        done = {k: room.sem(k + "_done") for k in
                "turns turnd xsT ws sum sT pd psr cd rd hd hg hb od cs rs hs sg os".split()}
        rec_in, mi_in, flags_in, xd_in, xs_in, x3_in, os_out = (
            room.sem2(k) for k in ("rec_in", "mi_in", "flags_in", "xd_in", "xs_in", "x3_in", "os_out"))
        over_in = room.swdge2("over_in")
        od_out = room.swdge2("od_out") if last else room.sem2("od_out")
        block = room.block()

        @block.sync
        def _(sp):
            def load(s):
                k = s.slot()
                room.hold(sp, done["od"], s.lin(1, -1))
                if last:
                    room.hold(sp, od_out[k], s.lin(16 * TILES, 0, div=2))
                g = s.lin()
                sp.dma_start(mi[k][:, :], cols_of(mapped, g, 2 * TILES)).then_inc(mi_in[k], 16)
                sp.dma_start(tiles3(xs[k]), edge_rows(src_t, g)).then_inc(xs_in[k], 16)
                sp.dma_start(flags[k][:, :, :], along[bass.ds(g, 1), KEEP_F:W_F + 1, :]
                             .rearrange("a k g -> (a k) g").partition_broadcast(P)).then_inc(flags_in[k], 16)
                sp.dma_start(tiles3(xd[k]), edge_rows(own_t, g)).then_inc(xd_in[k], 16)
                sp.dma_start(rec[k][:, :], cols_of(facts, g, REC)).then_inc(rec_in[k], 16)
                if last:
                    sp.dma_start(tiles3(x3[k]), edge_rows(d3, g)).then_inc(x3_in[k], 16)

            def store(s):
                k = s.slot()
                g = s.lin()
                room.hold(sp, done["os"], s.lin(1, 1))
                sp.dma_start(edge_rows(next_s, g), tiles3(o_s[k])).then_inc(os_out[k], 16)
                room.hold(sp, done["od"], s.lin(1, 1))
                sp.dma_start(edge_rows(next_t, g), tiles3(o_d[k])).then_inc(od_out[k], 16)

            if last:
                run_groups(sp, ng, 2, [(0, load)])
            else:
                run_groups(sp, ng, 2, [(3, store), (0, load)])
                for k in range(2):
                    sp.wait_ge(os_out[k], 16 * ((ng + 1 - k) // 2))
                    sp.wait_ge(od_out[k], 16 * ((ng + 1 - k) // 2))

        @block.gpsimd
        def _(pool):
            top = pool.to_reg(ng * G - 1)
            top_node = pool.to_reg(nodes - 1)

            def overlay(s):
                k = s.slot()
                room.hold(pool, xs_in[k], s.lin(16, 16, div=2))
                room.hold(pool, mi_in[k], s.lin(16, 16, div=2))
                for c in range(TILES):
                    pool.indirect_dma_start(tile(xs[k], c), None, own_t,
                                            bass.IndirectOffsetOnAxis(mi[k][:, 2 * c:2 * c + 1], 0),
                                            bounds_check=top, oob_is_err=False).then_inc(over_in[k], 16)

            def scatter(s):
                k = s.slot()
                room.hold(pool, done["od"], s.lin(1, 1))
                for c in range(TILES):
                    pool.indirect_dma_start(out, bass.IndirectOffsetOnAxis(rec[k][:, SCAT + c:SCAT + c + 1], 0),
                                            tile(o_d[k], c), None, bounds_check=top_node,
                                            oob_is_err=False).then_inc(od_out[k], 16)

            if last:
                run_groups(pool, ng, 2, [(2, scatter), (0, overlay)])
                for k in range(2):
                    pool.wait_ge(od_out[k], 16 * TILES * ((ng + 1 - k) // 2))
            else:
                run_groups(pool, ng, 2, [(0, overlay)])

        @block.tensor
        def _(pe):
            def turns(s):
                k = s.slot()
                pe.wait_ge(over_in[k], s.lin(64, 64, div=2))
                wait(pe, done["ws"] if last else done["xsT"], s.lin(1, -1))
                for c in range(TILES):
                    ins = pe.transpose(tile(ps_s[k], c), tile(xs[k], c), w.ident[:, :])
                ins.then_inc(done["turns"], 1)
                pe.wait_ge(xd_in[k], s.lin(16, 16, div=2))
                wait(pe, done["sT"], s.lin(1, -1))
                for c in range(TILES):
                    ins = pe.transpose(tile(ps_d[k], c), tile(xd[k], c), w.ident[:, :])
                ins.then_inc(done["turnd"], 1)

            def src_product(s):
                k = s.slot()
                pe.wait_ge(done["xsT"], s.lin(1, 1))
                wait(pe, done["cs"], s.lin(1, -1))
                for c in range(TILES):
                    ins = pe.matmul(tile(ps_ps[k], c), tile(xsT[k], c), weight, start=True, stop=True)
                ins.then_inc(done["psr"], 1)

            def dst_product(s):
                k = s.slot()
                pe.wait_ge(done["sT"], s.lin(1, 1))
                wait(pe, done["cd"], s.lin(1, -1))
                for c in range(TILES):
                    ins = pe.matmul(tile(ps_pd[k], c), tile(sT[k], c), weight, start=True, stop=True)
                ins.then_inc(done["pd"], 1)

            run_groups(pe, ng, 2, [(0, turns), (0, dst_product)] if last else [(0, turns), (0, src_product), (0, dst_product)])

        @block.vector
        def _(v):
            def collect(s):
                k = s.slot()
                v.wait_ge(flags_in[k], s.lin(16, 16, div=2))
                v.wait_ge(done["turns"] if last else done["xsT"], s.lin(1, 1))
                rows = ps_s[k] if last else xsT[k]
                v.tensor_tensor(ws[k][:, :], rows[:, :], flags[k][:, 1, :], ALU.mult).then_inc(done["ws"], 1)
                v.wait_ge(done["ws"], s.lin(1, 1))
                wait(v, done["sum"], s.lin())
                first = s.fixed and s.lin() == 0
                v.tensor_tensor_scan(aT[k][:, :], flags[k][:, 0, :], ws[k][:, :],
                                     0.0 if first else aT[1 - k][:, G - 1:G], ALU.mult, ALU.add).then_inc(done["sum"], 1)
                v.wait_ge(done["sum"], s.lin(1, 1))
                v.wait_ge(done["turnd"], s.lin(1, 1))
                wait(v, done["pd"], s.lin(1, -1))
                v.tensor_tensor(sT[k][:, :], aT[k][:, :], ps_d[k][:, :], ALU.add).then_inc(done["sT"], 1)

            def src_bias(s):
                k = s.slot()
                v.wait_ge(done["psr"], s.lin(1, 1))
                v.tensor_tensor(tiles3(c_s[k]), tiles3(ps_ps[k]), over_tiles(bias), ALU.add).then_inc(done["cs"], 1)

            def dst_bias(s):
                k = s.slot()
                dinv = rec[k][:, DINV:DINV + TILES].bitcast(F32)
                v.wait_ge(rec_in[k], s.lin(16, 16, div=2))
                v.wait_ge(done["pd"], s.lin(1, 1))
                for c in range(TILES):
                    ins = v.scalar_tensor_tensor(out=tile(c_d[k], c), in0=tile(ps_pd[k], c), scalar=dinv[:, c:c + 1],
                                                 in1=bias, op0=ALU.mult, op1=ALU.add)
                ins.then_inc(done["cd"], 1)

            def affine(s, norm, r, h, o, normed, scaled):
                k = s.slot()
                norm.finish(v, s, r[k], h[k], normed)
                v.wait_ge(normed, s.lin(1, 1))
                v.tensor_tensor(tiles3(h[k]), tiles3(h[k]), over_tiles(w.row("gamma")), ALU.mult).then_inc(scaled, 1)
                v.wait_ge(scaled, s.lin(1, 1))

            def src_stats(s):
                v.wait_ge(done["rs"], s.lin(1, 1))
                ns.stats(v, s, r_s[s.slot()])

            def src_out(s):
                k = s.slot()
                affine(s, ns, r_s, h_s, o_s, done["hs"], done["sg"])
                wait(v, os_out[k], s.lin(16, 0, div=2))
                v.tensor_tensor(tiles3(o_s[k]), tiles3(h_s[k]), over_tiles(w.row("beta")), ALU.add).then_inc(done["os"], 1)

            def dst_stats(s):
                v.wait_ge(done["rd"], s.lin(1, 1))
                nd.stats(v, s, r_d[s.slot()])

            def dst_out(s):
                k = s.slot()
                dinv = rec[k][:, DINV:DINV + TILES].bitcast(F32)
                affine(s, nd, r_d, h_d, o_d, done["hd"], done["hg"])
                v.tensor_tensor(tiles3(h_d[k]), tiles3(h_d[k]), over_tiles(w.row("beta")), ALU.add).then_inc(done["hb"], 1)
                v.wait_ge(done["hb"], s.lin(1, 1))
                wait(v, od_out[k], s.lin(16, 0, div=2))
                for c in range(TILES):
                    ins = v.tensor_scalar(tile(o_d[k], c), tile(h_d[k], c), dinv[:, c:c + 1], None, ALU.mult)
                ins.then_inc(done["od"], 1)

            def last_stats(s):
                k = s.slot()
                v.wait_ge(done["cd"], s.lin(1, 1))
                v.wait_ge(x3_in[k], s.lin(16, 16, div=2))
                v.tensor_tensor(r_d[k][:, :], c_d[k][:, :], x3[k][:, :], ALU.add).then_inc(done["rd"], 1)
                v.wait_ge(done["rd"], s.lin(1, 1))
                nd.stats(v, s, r_d[k])

            def last_out(s):
                k = s.slot()
                nd.finish(v, s, r_d[k], o_d[k], done["od"], out_free=lambda: wait(v, od_out[k], s.lin(64, 0, div=2)))

            if last:
                run_groups(v, ng, 2, [(1, dst_bias), (0, collect), (1, last_stats), (1, last_out)])
            else:
                run_groups(v, ng, 2, [(1, dst_bias), (1, src_bias), (0, collect), (1, dst_stats), (1, src_stats),
                                      (1, dst_out), (1, src_out)])

        @block.scalar
        def _(a):
            def copy_src(s):
                k = s.slot()
                wait(a, done["psr"], s.lin(1, -1))
                wait(a, done["ws"], s.lin(1, -1))
                a.wait_ge(done["turns"], s.lin(1, 1))
                a.copy(xsT[k][:, :], ps_s[k][:, :]).then_inc(done["xsT"], 1)

            def relus(s):
                k = s.slot()
                a.wait_ge(done["cd"], s.lin(1, 1))
                a.activation(r_d[k][:, :], c_d[k][:, :], ACT.Relu).then_inc(done["rd"], 1)
                a.wait_ge(done["cs"], s.lin(1, 1))
                a.activation(r_s[k][:, :], c_s[k][:, :], ACT.Relu).then_inc(done["rs"], 1)

            if last:
                run_groups(a, ng, 2, [(1, lambda s: nd.root(a, s))])
            else:
                run_groups(a, ng, 2, [(0, copy_src), (1, relus), (1, lambda s: nd.root(a, s)), (1, lambda s: ns.root(a, s))])


def build(nc, x, ints, ew, edge_attr, mats, cols, rows, wrow, out):
    nodes = x.shape[0]
    ng = ew.shape[0]

    def table(name, shape, dt=F32):
        return nc.dram_tensor(name, shape, dt).ap()

    facts = table("facts", [P, ng * REC], I32)
    along = table("along", [ng, 4, G])
    slots = table("slots", [nodes, 2], I32)
    mapped = table("mapped", [P, ng * 2 * TILES], I32)
    t1, s1 = table("t1", [ng * G, D]), table("s1", [ng * G, D])
    t2 = table("t2", [nodes + ng * G, D])
    t3, s3, d3 = table("t3", [ng * G, D]), table("s3", [ng * G, D]), table("d3", [ng * G, D])
    th, sh = table("th", [ng * G, D]), table("sh", [ng * G, D])
    with ExitStack() as ctx:
        w = Weights(Room(nc, ctx, "w"))
        prepare_weights(nc, w, mats, cols, rows, wrow)
        prepare_edges(nc, w, ng, nodes, ints, ew, along, facts.rearrange("p (g r) -> p g r", r=REC), slots)
        dense_pass(nc, w, ng, nodes, x, out, t2, facts, slots, mapped)
        sum_layer(nc, w, ng, nodes, x, facts, along, t1, s1)
        max_layer(nc, w, ng, nodes, facts, along, ew, mapped, t1, s1, t2)
        attention_layer(nc, w, ng, nodes, facts, along, edge_attr, mapped, t2, t3, s3, d3)
        gcn_layer(nc, w, ng, nodes, facts, along, mapped, t3, s3, False, next_t=th, next_s=sh)
        gcn_layer(nc, w, ng, nodes, facts, along, mapped, th, sh, True, d3=d3, out=out)


def kernel(**inputs):
    import numpy as np
    import concourse.bacc as bacc
    from concourse.bass_utils import run_bass_kernel_spmd as run

    a = {k: np.ascontiguousarray(v) for k, v in inputs.items()}
    nodes, d = a["x"].shape
    edges = a["src"].shape[0]
    ng = -(-edges // G)
    pad = ng * G - edges
    fill = np.full((pad,), nodes, np.int32)
    src = np.concatenate([a["src"], np.zeros((pad,), np.int32)])
    dst = np.concatenate([a["dst"], fill])
    before = np.concatenate([np.full((1,), nodes + 1, np.int32), dst[:-1]])
    after = np.concatenate([dst[1:], np.full((1,), nodes + 1, np.int32)])
    m1 = a["L1_gnn_W1"]
    u1 = a["L1_gnn_U1"]
    mats = [a["L0_gnn_W"], a["L2_gnn_Wq"], a["L2_gnn_Wk"], a["L2_gnn_We"], a["L2_gnn_Wv"], m1[:d], m1[d:2 * d],
            a["L1_gnn_W2"], u1[:d], u1[d:], a["L1_gnn_U2"], a["L3_gnn_W1"], a["L3_gnn_W2"]]
    vecs = [a[k] for k in ("L0_gnn_b", "L1_gnn_b1", "L1_gnn_b2", "L1_gnn_c1", "L1_gnn_c2", "L2_gnn_bq", "L2_gnn_bk",
                           "L2_gnn_be", "L2_gnn_bv", "L3_gnn_b1", "L3_gnn_g1", "L3_gnn_beta1", "L3_gnn_b2")]
    arrays = {
        "x": a["x"],
        "ints": np.stack([src, dst, before, after]).reshape(4, ng, G),
        "ew": np.concatenate([a["edge_weight"], np.zeros((pad,), np.float32)]).reshape(ng, G),
        "edge_attr": np.concatenate([a["edge_attr_128"], np.zeros((pad, d), np.float32)]),
        "mats": np.ascontiguousarray(np.concatenate(mats, axis=1)),
        "cols": np.ascontiguousarray(np.stack(vecs, axis=1)),
        "rows": np.stack(vecs),
        "wrow": np.ascontiguousarray(m1[2 * d:]),
    }
    nc = bacc.Bacc("TRN2", target_bir_lowering=False, num_devices=1)
    aps = [nc.dram_tensor(k, v.shape, mybir.dt.from_np(v.dtype), kind="ExternalInput").ap() for k, v in arrays.items()]
    out = nc.dram_tensor("out", (nodes, d), F32, kind="ExternalOutput").ap()
    build(nc, *aps, out)
    result = run(nc, [arrays], core_ids=[0])
    return result.results[0]["out"]
```

```python
from contextlib import ExitStack

import concourse.bass as bass
from concourse import mybir

F32 = mybir.dt.float32
I32 = mybir.dt.int32
BF16 = mybir.dt.bfloat16
ALU = mybir.AluOpType
ACT = mybir.ActivationFunctionType

P = 128
D = 128
TILES = 4
G = P * TILES
EPS = 1e-5
NO_ROW = 1 << 20
BIG = 3.0e38

SRC, DSTC, SCAT, PAY, LAST, FIRST, DINV, WROW = 0, 4, 8, 12, 20, 24, 28, 32
REC = 36
PEN_B, KEEP_B, KEEP_F, W_F = 0, 1, 2, 3

WEIGHTS = ["W0", "Wq", "Wk", "We", "Wv", "M1S", "M1D", "M2", "U1X", "U1A", "U2", "G1", "G2"]
VECTORS = ["b0", "mb1", "mb2", "c1", "c2", "bq", "bk", "be", "bv", "gb1", "gamma", "beta", "gb2"]


class Step:

    def __init__(self, j, unroll, off):
        self.j, self.unroll, self.off = j, unroll, off
        self.fixed = isinstance(j, int)

    def lin(self, mult=1, add=0, div=1):
        return self.j * (mult * (self.unroll // div)) + (mult * (self.off // div) + add)

    def slot(self, count=2):
        return self.off % count


def wait(eng, sem, value):
    if isinstance(value, int) and value <= 0:
        return
    eng.wait_ge(sem, value)


def uses(count, k, ring):
    return (count + ring - 1 - k) // ring


def run_groups(eng, count, unroll, stages):
    deepest = max(lag for lag, _ in stages)
    first = -(-(deepest + 4) // unroll)
    last = (count - 1) // unroll

    def at(j, u):
        for lag, work in stages:
            step = Step(j, unroll, u - lag)
            if step.fixed and not 0 <= step.lin() < count:
                continue
            work(step)

    for t in range(first * unroll):
        at(t // unroll, t % unroll)
    with eng.Fori(first, last) as j:
        for u in range(unroll):
            at(j, u)
    for t in range(last * unroll, count + deepest):
        at(t // unroll, t % unroll)


class Room:

    def __init__(self, nc, ctx, name):
        self.nc, self.ctx, self.name = nc, ctx, name
        self.counts = []
        self.passed = self.sem("passed")

    def hold(self, eng, sem, value):
        if isinstance(value, int):
            wait(eng, sem, value)
            return
        eng.wait_ge(sem, value)
        eng.sem_inc(self.passed, 1)

    def sb(self, name, shape, dt=F32):
        return self.ctx.enter_context(self.nc.sbuf_tensor(f"{self.name}_{name}", shape, dt))

    def two(self, name, shape, dt=F32, count=2):
        return [self.sb(f"{name}{i}", shape, dt) for i in range(count)]

    def bank(self, name):
        return self.ctx.enter_context(self.nc.psum_tensor(f"{self.name}_bank_{name}", [P, G], F32))

    def sem(self, name):
        self.counts.append(self.ctx.enter_context(self.nc.semaphore(f"{self.name}_{name}")))
        return self.counts[-1]

    def sem2(self, name, count=2):
        return [self.sem(f"{name}{i}") for i in range(count)]

    def swdge2(self, name, count=2):
        return [self.nc.alloc_semaphore(f"{self.name}_{name}{i}") for i in range(count)]

    def block(self):
        self.ctx.callback(self.clear)
        return self.ctx.enter_context(self.nc.Block())

    def clear(self):
        numbers = sorted(sem.num for sem in self.counts)
        start = 0
        for i, number in enumerate(numbers):
            if i + 1 == len(numbers) or numbers[i + 1] != number + 1:
                self.nc.gpsimd.sem_clear(range(numbers[start], number + 1))
                start = i + 1
        self.nc.all_engine_barrier()


def tile(buf, c):
    return buf[:, c * D:(c + 1) * D]


def tiles3(buf):
    return buf[:, :].rearrange("p (c d) -> p c d", c=TILES)


def cols_of(table, g, width):
    return table[:, bass.ds(g * width, width)]


def flat(along, g, what):
    return along[bass.ds(g, 1), what, :].rearrange("a g -> (a g)").partition_broadcast(P)


def edge_rows(table, g, base=0):
    return table[bass.ds(g * G + base, G), :].rearrange("(c p) d -> p c d", p=P)


def over_tiles(row):
    return row.unsqueeze(1).broadcast_to([P, TILES, D])


class Norm:

    def __init__(self, room, name, eps_col):
        self.st = room.two(f"{name}_st", [P, 6 * TILES], count=4)
        self.mv = room.two(f"{name}_mv", [P, 2 * TILES], count=4)
        self.sd, self.rs, self.rm = (room.two(f"{name}_{k}", [P, TILES], count=4) for k in ("sd", "rs", "rm"))
        self.st_done, self.settled, self.mv_done, self.sd_done, self.rs_done, self.rm_done = (
            room.sem(f"{name}_{k}") for k in ("st_done", "st_settled", "mv_done", "sd_done", "rs_done", "rm_done"))
        self.eps = eps_col

    def stats(self, v, s, rows, ready=None):
        k = s.slot(4)
        if ready is not None:
            v.wait_ge(ready, s.lin(1, 1))
        for c in range(TILES):
            ins = v.bn_stats(self.st[k][:, 6 * c:6 * c + 6], tile(rows, c))
        ins.then_inc(self.st_done, 1)

    def moments(self, v, s):
        k = s.slot(4)
        v.wait_ge(self.st_done, s.lin(1, 1))
        v.sem_inc(self.settled, 1)
        for c in range(TILES):
            ins = v.bn_aggr(self.mv[k][:, 2 * c:2 * c + 2], self.st[k][:, 6 * c:6 * c + 6])
        ins.then_inc(self.mv_done, 1)

    def root(self, a, s):
        k = s.slot(4)
        a.wait_ge(self.mv_done, s.lin(1, 1))
        a.activation(self.sd[k][:, :], self.mv[k][:, 1::2], ACT.Sqrt, bias=self.eps).then_inc(self.sd_done, 1)

    def invert(self, v, s):
        k = s.slot(4)
        v.wait_ge(self.sd_done, s.lin(1, 1))
        v.reciprocal(self.rs[k][:, :], self.sd[k][:, :]).then_inc(self.rs_done, 1)

    def masked(self, v, s, mask):
        k = s.slot(4)
        v.wait_ge(self.rs_done, s.lin(1, 1))
        v.tensor_tensor(self.rm[k][:, :], self.rs[k][:, :], mask, ALU.mult).then_inc(self.rm_done, 1)

    def offset(self, v, s):
        k = s.slot(4)
        v.wait_ge(self.rs_done, s.lin(1, 1))
        v.scalar_tensor_tensor(out=self.rm[k][:, :], in0=self.mv[k][:, 0::2], scalar=-1.0, in1=self.rs[k][:, :],
                               op0=ALU.mult, op1=ALU.mult).then_inc(self.rm_done, 1)

    def scale(self, v, s, rows, out, out_done, masked=False):
        k = s.slot(4)
        v.wait_ge(self.rm_done if masked else self.rs_done, s.lin(1, 1))
        factor = self.rm[k] if masked else self.rs[k]
        for c in range(TILES):
            ins = v.tensor_scalar(tile(out, c), tile(rows, c), self.mv[k][:, 2 * c:2 * c + 1],
                                  factor[:, c:c + 1], ALU.subtract, ALU.mult)
        ins.then_inc(out_done, 1)

    def scale_a(self, a, s, rows, out, out_done):
        k = s.slot(4)
        a.wait_ge(self.rm_done, s.lin(1, 1))
        for c in range(TILES):
            ins = a.activation(tile(out, c), tile(rows, c), ACT.Identity, bias=self.rm[k][:, c:c + 1],
                               scale=self.rs[k][:, c:c + 1])
        ins.then_inc(out_done, 1)


class Weights:

    def __init__(self, room):
        n = len(WEIGHTS)
        self.mats = room.sb("mats", [P, n * D])
        self.turned = room.sb("turned", [P, 5 * D])
        self.cols = room.sb("cols", [P, len(VECTORS)])
        self.rows = room.sb("rows", [P, len(VECTORS) * D])
        self.wrow = room.sb("wrow", [1, D])
        self.ident = room.sb("ident", [P, P])
        self.center = room.sb("center", [P, P])
        self.heads = room.sb("heads", [P, P])
        self.mean_col = room.sb("mean_col", [P, 1])
        self.eps = room.sb("eps", [P, 1])
        self.eps2 = room.sb("eps2", [P, 1])
        self.u1c = room.sb("u1c", [P, D])
        self.g1c = room.sb("g1c", [P, D])
        self.u2c = room.sb("u2c", [P, D])
        self.g2c = room.sb("g2c", [P, D])
        self.c2c = room.sb("c2c", [P, D])
        self.gb2c = room.sb("gb2c", [P, D])
        self.negc2 = room.sb("negc2", [P, 1])
        self.neggb2 = room.sb("neggb2", [P, 1])
        self.c1b = room.sb("c1b", [P, 1])
        self.ones16 = room.sb("ones16", [P, P], BF16)
        self.gb1s = room.sb("gb1s", [P, D], BF16)
        self.c2s = room.sb("c2s", [P, D], BF16)

    def mat(self, name):
        i = WEIGHTS.index(name)
        return self.mats[:, i * D:(i + 1) * D]

    def t(self, i):
        return self.turned[:, i * D:(i + 1) * D]

    def col(self, name):
        i = VECTORS.index(name)
        return self.cols[:, i:i + 1]

    def row(self, name):
        i = VECTORS.index(name)
        return self.rows[:, i * D:(i + 1) * D]


def prepare_weights(nc, w, mats_in, vec_cols, vec_rows, wrow_in):
    with ExitStack() as ctx:
        room = Room(nc, ctx, "prep")
        ps_turn = [room.bank(f"ps_turn{i}") for i in range(2)]
        ps_mats = room.bank("ps_mats")
        ps_cols = room.bank("ps_cols")
        gw2 = room.sb("gw2", [P, D])
        gw2l = room.sb("gw2l", [P, D])
        gb2full = room.sb("gb2full", [P, D])
        sums = room.sb("sums", [P, 4])
        beta_b = room.sb("beta_b", [P, P])
        rest = room.sb("rest", [P, D])
        part = room.sb("part", [P, D], BF16)
        loaded = room.sem("loaded")
        const = room.sem("const")
        ident_ok = room.sem("ident_ok")
        turned = room.sem("turned")
        kept = room.sem("kept")
        v1 = room.sem("v1")
        prod = room.sem("prod")
        back = room.sem("back")
        block = room.block()

        @block.sync
        def _(sp):
            sp.dma_start(w.mats[:, :], mats_in).then_inc(loaded, 16)
            sp.dma_start(w.cols[:, :], vec_cols).then_inc(loaded, 16)
            sp.dma_start(w.rows[:, :], vec_rows.rearrange("k d -> (k d)").partition_broadcast(P)).then_inc(loaded, 16)
            sp.dma_start(w.wrow[:, :], wrow_in).then_inc(loaded, 16)

        @block.gpsimd
        def _(pool):
            nc.gpsimd.memset(w.ident[:, :], 0.0).then_inc(const, 1)
            nc.gpsimd.memset(w.center[:, :], -1.0 / P).then_inc(const, 1)
            nc.gpsimd.memset(w.heads[:, :], 0.25).then_inc(const, 1)
            nc.gpsimd.memset(w.mean_col[:, :], 1.0 / P).then_inc(const, 1)
            nc.gpsimd.memset(w.eps[:, :], EPS).then_inc(const, 1)
            nc.gpsimd.memset(w.eps2[:, :], EPS * EPS).then_inc(const, 1)
            pool.wait_ge(const, 6)
            nc.gpsimd.affine_select(out=w.ident[:, :], in_=w.ident[:, :], compare_op=ALU.not_equal, fill=1.0,
                                    base=0, pattern=[[-1, P]], channel_multiplier=1).then_inc(ident_ok, 1)
            nc.gpsimd.affine_select(out=w.center[:, :], in_=w.center[:, :], compare_op=ALU.not_equal,
                                    fill=1.0 - 1.0 / P, base=0, pattern=[[-1, P]], channel_multiplier=1).then_inc(ident_ok, 1)
            heads3 = w.heads[:, :].rearrange("p (h d) -> p h d", d=16)
            nc.gpsimd.affine_select(out=heads3, in_=heads3, compare_op=ALU.is_ge, fill=0.0, base=0,
                                    pattern=[[-16, 8], [0, 16]], channel_multiplier=1).then_inc(ident_ok, 1)
            pool.wait_ge(ident_ok, 3)
            nc.gpsimd.affine_select(out=heads3, in_=heads3, compare_op=ALU.is_ge, fill=0.0, base=15,
                                    pattern=[[16, 8], [0, 16]], channel_multiplier=-1).then_inc(ident_ok, 1)

        @block.tensor
        def _(pe):
            pe.wait_ge(ident_ok, 4)
            pe.wait_ge(loaded, 64)
            for i in range(5):
                ins = pe.transpose(ps_turn[i // 4][:, (i % 4) * D:(i % 4 + 1) * D], w.mats[:, i * D:(i + 1) * D], w.ident[:, :])
            ins.then_inc(turned, 1)
            pe.matmul(ps_mats[:, 0:D], w.center[:, :], w.mat("U1X"), start=True, stop=True)
            pe.matmul(ps_mats[:, D:2 * D], w.center[:, :], w.mat("G1"), start=True, stop=True)
            pe.wait_ge(v1, 1)
            pe.matmul(ps_mats[:, 2 * D:3 * D], w.center[:, :], gw2[:, :], start=True, stop=True)
            pe.wait_ge(v1, 2)
            pe.matmul(ps_mats[:, 3 * D:4 * D], beta_b[:, :], w.mat("G2"), start=True, stop=True)
            pe.matmul(ps_cols[:, 0:1], w.mat("U1A"), w.col("mb2"), start=True, stop=True).then_inc(prod, 1)
            pe.wait_ge(v1, 3)
            pe.transpose(ps_turn[0][:, 0:128], w.c2c[:, :], w.ident[:, :])
            pe.transpose(ps_turn[0][:, 128:256], w.gb2c[:, :], w.ident[:, :]).then_inc(back, 1)

        @block.vector
        def _(v):
            n = [0]

            def keep(ins):
                n[0] += 1
                ins.then_inc(kept, 1)
                v.wait_ge(kept, n[0])

            v.wait_ge(loaded, 64)
            v.tensor_scalar(gw2[:, :], w.mat("G2"), w.col("gamma"), None, ALU.mult).then_inc(v1, 1)
            v.wait_ge(const, 6)
            v.wait_ge(ident_ok, 4)
            keep(v.memset(beta_b[:, :], 0.0))
            v.tensor_scalar(beta_b[:, :], beta_b[:, :], w.col("beta"), None, ALU.add).then_inc(v1, 1)
            v.wait_ge(turned, 1)
            v.tensor_copy(w.turned[:, 0:4 * D], ps_turn[0][:, :])
            v.tensor_copy(w.turned[:, 4 * D:5 * D], ps_turn[1][:, 0:D])
            keep(v.reduce_sum(sums[:, 0:1], w.mat("U2"), mybir.AxisListType.X))
            keep(v.tensor_scalar(sums[:, 0:1], sums[:, 0:1], 1.0 / P, None, ALU.mult))
            v.tensor_scalar(w.u2c[:, :], w.mat("U2"), sums[:, 0:1], None, ALU.subtract)
            keep(v.reduce_sum(sums[:, 1:2], w.row("c2"), mybir.AxisListType.X))
            keep(v.tensor_scalar(sums[:, 1:2], sums[:, 1:2], 1.0 / P, None, ALU.mult))
            keep(v.tensor_scalar(w.c2c[:, :], w.row("c2"), sums[:, 1:2], None, ALU.subtract))
            v.wait_ge(prod, 1)
            v.tensor_copy(w.u1c[:, :], ps_mats[:, 0:D])
            v.tensor_copy(w.g1c[:, :], ps_mats[:, D:2 * D])
            keep(v.tensor_copy(gw2l[:, :], ps_mats[:, 2 * D:3 * D]))
            keep(v.reduce_sum(sums[:, 2:3], gw2l[:, :], mybir.AxisListType.X))
            keep(v.tensor_scalar(sums[:, 2:3], sums[:, 2:3], 1.0 / P, None, ALU.mult))
            v.tensor_scalar(w.g2c[:, :], gw2l[:, :], sums[:, 2:3], None, ALU.subtract)
            keep(v.tensor_tensor(gb2full[:, :], ps_mats[:, 3 * D:4 * D], w.row("gb2"), ALU.add))
            keep(v.reduce_sum(sums[:, 3:4], gb2full[:, :], mybir.AxisListType.X))
            keep(v.tensor_scalar(sums[:, 3:4], sums[:, 3:4], 1.0 / P, None, ALU.mult))
            v.tensor_scalar(w.gb2c[:, :], gb2full[:, :], sums[:, 3:4], None, ALU.subtract).then_inc(v1, 1)
            v.tensor_tensor(w.c1b[:, :], ps_cols[:, 0:1], w.col("c1"), ALU.add)
            v.wait_ge(back, 1)
            v.tensor_scalar(w.negc2[:, :], ps_turn[0][:, 0:1], -1.0, None, ALU.mult)
            keep(v.tensor_scalar(w.neggb2[:, :], ps_turn[0][:, 128:129], -1.0, None, ALU.mult))

            def split(row, parts):
                keep(v.memset(parts[:, :], 0.0))
                keep(v.tensor_copy(rest[:, :], row))
                for i in range(3):
                    keep(v.tensor_copy(part[:, :], rest[:, :]))
                    at = slice(32 * i, 32 * i + 1)
                    keep(v.tensor_copy(parts[at, :], part[at, :]))
                    keep(v.tensor_tensor(rest[:, :], rest[:, :], part[:, :], ALU.subtract))

            keep(v.memset(w.ones16[:, :], 1.0))
            split(w.c2c[:, :], w.c2s)
            split(w.row("gb1"), w.gb1s)


def prepare_edges(nc, w, ng, nodes, ints_in, ew_in, along, facts, slots):
    with ExitStack() as ctx:
        room = Room(nc, ctx, "edges")
        I = {k: room.sb(k, [ng, G], I32) for k in ("src", "dst", "dprev", "dnext")}
        f = {k: room.sb("f_" + k, [ng, G]) for k in ("dst", "dprev", "dnext", "last", "first", "w", "pos", "carry",
                                                      "degsum", "begin", "deg", "scat", "dstc", "src", "dinv", "pay")}
        al = room.sb("along", [ng, 4, G])
        ends = room.sb("ends", [ng, 4])
        erow = room.sb("erow", [1, 4, 64])
        crow = room.sb("crow", [1, 2, 64])
        ccol = room.sb("ccol", [ng, 2])
        rec = room.sb("rec", [P, ng, REC], I32)
        iota_id = room.sb("iota_id", [125, nodes // 125, 2], I32)
        ps_e = room.bank("ps_e")
        ps = [room.bank(f"ps{i}") for i in range(7)]
        loaded, kept, posed, ended, ends_back, carried, col_back, turned, evac, rooted, stored = (
            room.sem(x) for x in ("loaded", "kept", "posed", "ended", "ends_back", "carried", "col_back", "turned",
                                  "evac", "rooted", "stored"))
        ready = room.sem("ready")
        alongs = room.sem("alongs")
        rec_ok = room.sem("rec_ok")
        ids = room.sem("ids")
        TURN = [("src", SRC), ("dstc", DSTC), ("scat", SCAT), ("last", LAST), ("first", FIRST), ("dinv", DINV), ("w", WROW)]
        block = room.block()

        @block.sync
        def _(sp):
            for i, k in enumerate(("src", "dst", "dprev", "dnext")):
                sp.dma_start(I[k][:, :], ints_in[i]).then_inc(loaded, 16)
            sp.dma_start(f["w"][:, :], ew_in).then_inc(loaded, 16)
            sp.wait_ge(ids, 2)
            sp.dma_start(slots.rearrange("(a b) c -> a b c", a=125), iota_id[:, :, :]).then_inc(stored, 16)
            sp.wait_ge(alongs, 1)
            sp.dma_start(along, al[:, :, :]).then_inc(stored, 16)
            sp.wait_ge(rec_ok, 1)
            sp.dma_start(facts, rec[:, :, :]).then_inc(stored, 16)
            sp.wait_ge(stored, 48)

        @block.gpsimd
        def _(pool):
            nc.gpsimd.iota(iota_id[:, :, 1], pattern=[[1, nodes // 125]], base=0,
                           channel_multiplier=nodes // 125).then_inc(ids, 1)
            nc.gpsimd.memset(iota_id[:, :, 0], NO_ROW).then_inc(ids, 1)
            nc.gpsimd.iota(f["pos"][:, :], pattern=[[1, G]], base=0, channel_multiplier=G,
                           allow_small_or_imprecise_dtypes=True).then_inc(posed, 1)
            nc.gpsimd.iota(rec[:, :, PAY:PAY + 2 * TILES:2], pattern=[[G, ng], [P, TILES]], base=0,
                           channel_multiplier=1).then_inc(posed, 1)

        @block.vector
        def _(v):
            n = [0]

            def keep(ins):
                n[0] += 1
                ins.then_inc(kept, 1)
                v.wait_ge(kept, n[0])

            v.wait_ge(loaded, 80)
            v.tensor_copy(f["dst"][:, :], I["dst"][:, :])
            v.tensor_copy(f["src"][:, :], I["src"][:, :])
            v.tensor_copy(f["dprev"][:, :], I["dprev"][:, :])
            keep(v.tensor_copy(f["dnext"][:, :], I["dnext"][:, :]))
            v.tensor_tensor(al[:, KEEP_F, :], f["dst"][:, :], f["dprev"][:, :], ALU.is_equal)
            keep(v.tensor_tensor(al[:, KEEP_B, :], f["dst"][:, :], f["dnext"][:, :], ALU.is_equal))
            v.tensor_scalar(al[:, PEN_B, :], al[:, KEEP_B, :], BIG, BIG, ALU.mult, ALU.subtract)
            v.tensor_copy(al[:, W_F, :], f["w"][:, :]).then_inc(alongs, 1)
            v.tensor_scalar(f["last"][:, :], al[:, KEEP_B, :], -1.0, 1.0, ALU.mult, ALU.add)
            keep(v.tensor_scalar(f["first"][:, :], al[:, KEEP_F, :], -1.0, 1.0, ALU.mult, ALU.add))
            v.tensor_scalar(f["dstc"][:, :], f["dst"][:, :], float(nodes - 1), None, ALU.min)
            v.scalar_tensor_tensor(out=f["scat"][:, :], in0=al[:, KEEP_B, :], scalar=float(NO_ROW), in1=f["dst"][:, :],
                                   op0=ALU.mult, op1=ALU.add)
            v.wait_ge(posed, 1)
            keep(v.tensor_tensor(f["pos"][:, :], f["pos"][:, :], f["first"][:, :], ALU.mult))
            v.tensor_tensor_scan(f["degsum"][:, :], al[:, KEEP_F, :], f["w"][:, :], 0.0, ALU.mult, ALU.add)
            v.tensor_tensor_scan(f["begin"][:, :], al[:, KEEP_F, :], f["pos"][:, :], 0.0, ALU.mult, ALU.add)
            keep(v.memset(f["deg"][:, :], 0.0))
            keep(v.tensor_tensor_scan(f["carry"][:, :], al[:, KEEP_F, :], f["deg"][:, :], 1.0, ALU.mult, ALU.add))
            v.tensor_copy(ends[:, 0:1], f["carry"][:, G - 1:G])
            v.tensor_copy(ends[:, 1:2], f["degsum"][:, G - 1:G])
            v.tensor_copy(ends[:, 2:3], f["begin"][:, G - 1:G]).then_inc(ended, 1)
            v.wait_ge(ends_back, 1)
            keep(v.tensor_copy(erow[:, 0:3, 0:ng], ps_e[0:1, 0:3 * 64].rearrange("p (k n) -> p k n", k=3)[:, :, 0:ng]))
            v.tensor_tensor_scan(crow[:, 0, 1:ng + 1], erow[:, 0, 0:ng], erow[:, 1, 0:ng], 0.0, ALU.mult, ALU.add)
            keep(v.tensor_tensor_scan(crow[:, 1, 1:ng + 1], erow[:, 0, 0:ng], erow[:, 2, 0:ng], 0.0, ALU.mult, ALU.add))
            keep(v.memset(crow[:, :, 0:1], 0.0))
            v.sem_inc(carried, 1)
            v.wait_ge(col_back, 1)
            keep(v.tensor_copy(ccol[:, :], ps_e[0:ng, 256:258]))
            keep(v.scalar_tensor_tensor(out=f["deg"][:, :], in0=f["carry"][:, :], scalar=ccol[:, 0:1],
                                        in1=f["degsum"][:, :], op0=ALU.mult, op1=ALU.add))
            keep(v.scalar_tensor_tensor(out=f["pay"][:, :], in0=f["carry"][:, :], scalar=ccol[:, 1:2],
                                        in1=f["begin"][:, :], op0=ALU.mult, op1=ALU.add))
            v.tensor_scalar(f["pay"][:, :], f["pay"][:, :], float(nodes), None, ALU.add)
            keep(v.tensor_scalar(f["deg"][:, :], f["deg"][:, :], 1.0, None, ALU.add))
            v.tensor_scalar(f["carry"][:, :], f["deg"][:, :], 0.0, None, ALU.is_gt)
            keep(v.tensor_scalar(f["deg"][:, :], f["deg"][:, :], 1e-30, None, ALU.max))
            v.sem_inc(ready, 1)
            v.wait_ge(rooted, 1)
            keep(v.reciprocal(f["dinv"][:, :], f["begin"][:, :]))
            keep(v.tensor_tensor(f["dinv"][:, :], f["dinv"][:, :], f["carry"][:, :], ALU.mult))
            v.sem_inc(ready, 1)
            fl = rec[:, :, :].bitcast(F32)
            v.wait_ge(turned, 1)
            v.wait_ge(posed, 2)
            for i, (k, at) in enumerate(TURN):
                out = fl if at >= LAST else rec
                v.tensor_copy(out[:, :, at:at + TILES], ps[i][:, 0:TILES * ng].rearrange("p (c g) -> p g c", c=TILES))
            v.tensor_copy(rec[:, :, PAY + 1:PAY + 2 * TILES:2],
                          ps[0][:, TILES * ng:2 * TILES * ng].rearrange("p (c g) -> p g c", c=TILES)).then_inc(rec_ok, 1)

        @block.scalar
        def _(a):
            a.wait_ge(ready, 1)
            a.activation(f["begin"][:, :], f["deg"][:, :], ACT.Sqrt).then_inc(rooted, 1)

        @block.tensor
        def _(pe):
            pe.wait_ge(ended, 1)
            for k in range(3):
                ins = pe.transpose(ps_e[0:1, 64 * k:64 * k + ng], ends[:, k:k + 1], w.ident[0:ng, 0:ng])
            ins.then_inc(ends_back, 1)
            pe.wait_ge(carried, 1)
            for k in range(2):
                ins = pe.transpose(ps_e[0:ng, 256 + k:257 + k], crow[:, k, 0:ng], w.ident[0:1, 0:1])
            ins.then_inc(col_back, 1)
            pe.wait_ge(ready, 2)
            for i, (k, at) in enumerate(TURN):
                for c in range(TILES):
                    pe.transpose(ps[i][:, c * ng:(c + 1) * ng], f[k][:, c * P:(c + 1) * P], w.ident[0:ng, 0:ng])
            for c in range(TILES):
                ins = pe.transpose(ps[0][:, (TILES + c) * ng:(TILES + c + 1) * ng], f["pay"][:, c * P:(c + 1) * P],
                                   w.ident[0:ng, 0:ng])
            ins.then_inc(turned, 1)


def dense_pass(nc, w, ng, nodes, x, out, t2, facts, slots, mapped):
    count = -(-nodes // G)
    half = -(-(count // 2) // 4) * 4
    with ExitStack() as ctx:
        room = Room(nc, ctx, "dense")
        xin, u, z, x2, x3b, z4, o = (room.two(k, [P, G], count=4) for k in "xin u z x2 x3b z4 o".split())
        x1T, rT, x3T, hT, hsq = (room.two(k, [P, G]) for k in "x1T rT x3T hT hsq".split())
        junk2 = room.sb("junk2", [P, G])
        junk4 = room.sb("junk4", [P, G])
        st = room.two("st", [P, 6 * TILES])
        mv = room.two("mv", [P, 2 * TILES])
        sd23, rs23, hst = (room.two(k, [P, 2 * TILES]) for k in "sd23 rs23 hst".split())
        sd1, rs1, sq2, hm2, hvar, sdh, rsh, sq4, sd4, rs4 = (
            room.two(k, [P, TILES]) for k in "sd1 rs1 sq2 hm2 hvar sdh rsh sq4 sd4 rs4".split())
        rec = room.two("rec", [P, REC], I32)
        got = room.two("got", [P, 2 * TILES], I32)
        ps_t1, ps_t3, ps_u, ps_w, ps_z, ps_h = (room.bank(k) for k in ("t1", "t3", "u", "w", "z", "h"))
        ps_p = [room.bank("p0"), room.bank("p1")]
        names = ("y st settled mv sd1 rs1 u t1 x1T ua rT zp z sq2 sd23 rs23 x2 x3b t3 x3T wa hT hsq pp hst hm2 "
                 "hvar0 hvar sdh rsh z4 sq4 sd4 rs4 o").split()
        done = {k: room.sem(k + "_done") for k in names}
        x_in, x2_out, o_out = room.sem2("x_in", 4), room.sem2("x2_out", 4), room.sem2("o_out", 4)
        rec_in, put, found, kept = (room.swdge2(k) for k in ("rec_in", "put", "found", "kept"))

        def rows(table, s):
            at = min(s.lin(G), nodes - G) if s.fixed else s.lin(G)
            return table[bass.ds(at, G), :].rearrange("(p c) d -> p (c d)", c=TILES)

        def each_tile(factors):
            return factors.unsqueeze(2).broadcast_to([P, TILES, D])

        block = room.block()

        @block.sync
        def _(sp):
            def load(s):
                k = s.slot(4)
                room.hold(sp, done["u"], s.lin(1, -3))
                sp.dma_start(xin[k][:, :], rows(x, s)).then_inc(x_in[k], 16)

            def store(s, table, buf, written, landed):
                k = s.slot(4)
                if s.fixed and s.lin() == count - 1:
                    sp.wait_ge(landed[(count - 2) % 4], 16 * ((count - 2) // 4 + 1))
                room.hold(sp, written, s.lin(1, 1))
                sp.dma_start(rows(table, s), buf[k][:, :]).then_inc(landed[k], 16)

            run_groups(sp, count, 4, [(0, load), (8, lambda s: store(s, t2, x2, done["x2"], x2_out)),
                                      (13, lambda s: store(s, out, o, done["o"], o_out))])
            for k in range(4):
                sp.wait_ge(x2_out[k], 16 * uses(count, k, 4))
                sp.wait_ge(o_out[k], 16 * uses(count, k, 4))

        @block.vector
        def _(v):
            def stats1(s):
                k = s.slot()
                v.wait_ge(done["y"], s.lin(1, 1))
                for c in range(TILES):
                    ins = v.bn_stats(st[k][:, 6 * c:6 * c + 6], tile(xin[s.slot(4)], c))
                ins.then_inc(done["st"], 1)

            def moments1(s):
                k = s.slot()
                v.wait_ge(done["st"], s.lin(1, 1))
                v.sem_inc(done["settled"], 1)
                for c in range(TILES):
                    ins = v.bn_aggr(mv[k][:, 2 * c:2 * c + 2], st[k][:, 6 * c:6 * c + 6])
                ins.then_inc(done["mv"], 1)

            def invert1(s):
                k = s.slot()
                v.wait_ge(done["sd1"], s.lin(1, 1))
                v.reciprocal(rs1[k][:, :], sd1[k][:, :]).then_inc(done["rs1"], 1)

            def scale1(s):
                k, k4 = s.slot(), s.slot(4)
                v.wait_ge(done["rs1"], s.lin(1, 1))
                for c in range(TILES):
                    ins = v.tensor_scalar(tile(u[k4], c), tile(xin[k4], c), mv[k][:, 2 * c:2 * c + 1],
                                          rs1[k][:, c:c + 1], ALU.subtract, ALU.mult)
                ins.then_inc(done["u"], 1)

            def add_mlp(s):
                k4 = s.slot(4)
                v.wait_ge(done["zp"], s.lin(1, 1))
                v.tensor_tensor(z[k4][:, :], ps_z[:, :], u[k4][:, :], ALU.add).then_inc(done["z"], 1)

            def invert23(s):
                k = s.slot()
                v.wait_ge(done["sd23"], s.lin(1, 1))
                v.reciprocal(rs23[k][:, :], sd23[k][:, :]).then_inc(done["rs23"], 1)

            def scale3(s):
                k, k4 = s.slot(), s.slot(4)
                v.wait_ge(done["rs23"], s.lin(1, 1))
                for c in range(TILES):
                    ins = v.scalar_tensor_tensor(out=tile(x3b[k4], c), in0=tile(z[k4], c),
                                                 scalar=rs23[k][:, TILES + c:TILES + c + 1], in1=w.gb2c[:, :],
                                                 op0=ALU.mult, op1=ALU.add)
                ins.then_inc(done["x3b"], 1)

            def scale2(s):
                k, k4 = s.slot(), s.slot(4)
                wait(v, x2_out[k4], s.lin(16, 0, div=4))
                v.tensor_tensor(tiles3(x2[k4]), tiles3(z[k4]), each_tile(rs23[k][:, 0:TILES]), ALU.mult).then_inc(done["x2"], 1)

            def moments_h(s):
                k = s.slot()
                v.wait_ge(done["pp"], s.lin(1, 1))
                v.tensor_copy(hst[k][:, :], ps_h[:, 0:2 * TILES]).then_inc(done["hst"], 1)

            def square_h(s):
                k = s.slot()
                v.wait_ge(done["hst"], s.lin(1, 1))
                v.tensor_tensor(hm2[k][:, :], hst[k][:, TILES:2 * TILES], hst[k][:, TILES:2 * TILES], ALU.mult).then_inc(done["hm2"], 1)

            def var_h(s):
                k = s.slot()
                v.wait_ge(done["hm2"], s.lin(1, 1))
                v.tensor_tensor(hvar[k][:, :], hst[k][:, 0:TILES], hm2[k][:, :], ALU.subtract).then_inc(done["hvar0"], 1)

            def clamp_h(s):
                k = s.slot()
                v.wait_ge(done["hvar0"], s.lin(1, 1))
                v.tensor_scalar(hvar[k][:, :], hvar[k][:, :], 0.0, None, ALU.max).then_inc(done["hvar"], 1)

            def invert_h(s):
                k = s.slot()
                v.wait_ge(done["sdh"], s.lin(1, 1))
                v.reciprocal(rsh[k][:, :], sdh[k][:, :]).then_inc(done["rsh"], 1)

            def add_gcn(s):
                k, k4 = s.slot(), s.slot(4)
                v.wait_ge(done["rsh"], s.lin(1, 1))
                for c in range(TILES):
                    ins = v.scalar_tensor_tensor(out=tile(z4[k4], c), in0=tile(ps_p[k], c), scalar=rsh[k][:, c:c + 1],
                                                 in1=tile(x3b[k4], c), op0=ALU.mult, op1=ALU.add)
                ins.then_inc(done["z4"], 1)

            def invert4(s):
                k = s.slot()
                v.wait_ge(done["sd4"], s.lin(1, 1))
                v.reciprocal(rs4[k][:, :], sd4[k][:, :]).then_inc(done["rs4"], 1)

            def scale4(s):
                k, k4 = s.slot(), s.slot(4)
                v.wait_ge(done["rs4"], s.lin(1, 1))
                wait(v, o_out[k4], s.lin(16, 0, div=4))
                v.tensor_tensor(tiles3(o[k4]), tiles3(z4[k4]), each_tile(rs4[k][:, :]), ALU.mult).then_inc(done["o"], 1)

            run_groups(v, count, 4, [(8, moments_h), (1, invert1), (5, invert23), (8, square_h), (5, scale3),
                                     (8, var_h), (1, scale1), (8, clamp_h), (3, add_mlp), (5, scale2), (10, invert4),
                                     (0, stats1), (10, scale4), (0, moments1), (8, invert_h), (8, add_gcn)])

        @block.scalar
        def _(a):
            def root1(s):
                k = s.slot()
                a.wait_ge(done["mv"], s.lin(1, 1))
                a.activation(sd1[k][:, :], mv[k][:, 1::2], ACT.Sqrt, bias=w.eps[:, :]).then_inc(done["sd1"], 1)

            def mlp_in(s):
                k = s.slot()
                a.wait_ge(done["t1"], s.lin(1, 1))
                a.copy(x1T[k][:, :], ps_t1[:, :]).then_inc(done["x1T"], 1)

            def mlp_mid(s):
                k = s.slot()
                a.wait_ge(done["ua"], s.lin(1, 1))
                a.activation(rT[k][:, :], ps_u[:, :], ACT.Relu, bias=w.col("c1")).then_inc(done["rT"], 1)

            def squares2(s):
                k, k4 = s.slot(), s.slot(4)
                a.wait_ge(done["z"], s.lin(1, 1))
                for c in range(TILES):
                    ins = a.activation(tile(junk2, c), tile(z[k4], c), ACT.Square, accum_out=sq2[k][:, c:c + 1])
                ins.then_inc(done["sq2"], 1)

            def root23(s):
                k = s.slot()
                a.wait_ge(done["sq2"], s.lin(1, 1))
                a.activation(sd23[k][:, 0:TILES], sq2[k][:, :], ACT.Sqrt, bias=w.eps[:, :], scale=1.0 / D)
                a.activation(sd23[k][:, TILES:2 * TILES], sq2[k][:, :], ACT.Sqrt, bias=w.eps2[:, :],
                             scale=(1.0 + EPS) / D).then_inc(done["sd23"], 1)

            def gcn_in(s):
                k = s.slot()
                a.wait_ge(done["t3"], s.lin(1, 1))
                a.activation(x3T[k][:, :], ps_t3[:, :], ACT.Identity, bias=w.neggb2[:, :]).then_inc(done["x3T"], 1)

            def gcn_mid(s):
                k = s.slot()
                a.wait_ge(done["wa"], s.lin(1, 1))
                wait(a, done["pp"], s.lin(1, -1))
                a.activation(hT[k][:, :], ps_w[:, :], ACT.Relu, bias=w.col("gb1")).then_inc(done["hT"], 1)

            def square_h(s):
                k = s.slot()
                a.wait_ge(done["hT"], s.lin(1, 1))
                a.activation(hsq[k][:, :], hT[k][:, :], ACT.Square).then_inc(done["hsq"], 1)

            def root_h(s):
                k = s.slot()
                a.wait_ge(done["hvar"], s.lin(1, 1))
                a.activation(sdh[k][:, :], hvar[k][:, :], ACT.Sqrt, bias=w.eps[:, :]).then_inc(done["sdh"], 1)

            def squares4(s):
                k, k4 = s.slot(), s.slot(4)
                a.wait_ge(done["z4"], s.lin(1, 1))
                for c in range(TILES):
                    ins = a.activation(tile(junk4, c), tile(z4[k4], c), ACT.Square, accum_out=sq4[k][:, c:c + 1])
                ins.then_inc(done["sq4"], 1)

            def root4(s):
                k = s.slot()
                a.wait_ge(done["sq4"], s.lin(1, 1))
                a.activation(sd4[k][:, :], sq4[k][:, :], ACT.Sqrt, bias=w.eps[:, :], scale=1.0 / D).then_inc(done["sd4"], 1)

            run_groups(a, count, 4, [(4, squares2), (2, mlp_mid), (4, root23), (6, gcn_mid), (9, squares4), (6, square_h),
                                     (9, root4), (8, root_h), (5, gcn_in), (1, mlp_in), (0, root1)])

        @block.tensor
        def _(pe):
            def turn1(s):
                pe.wait_ge(done["u"], s.lin(1, 1))
                wait(pe, done["x1T"], s.lin())
                for c in range(TILES):
                    ins = pe.transpose(tile(ps_t1, c), tile(u[s.slot(4)], c), w.ident[:, :])
                ins.then_inc(done["t1"], 1)

            def mlp1(s):
                k = s.slot()
                pe.wait_ge(done["x1T"], s.lin(1, 1))
                wait(pe, done["rT"], s.lin())
                pe.matmul(ps_u[:, :], w.u1c[:, :], x1T[k][:, :], start=True, stop=True).then_inc(done["ua"], 1)

            def mlp2(s):
                k = s.slot()
                pe.wait_ge(done["rT"], s.lin(1, 1))
                wait(pe, done["z"], s.lin())
                for c in range(TILES):
                    pe.matmul(tile(ps_z, c), w.ones16[:, :], w.c2s[:, :], start=True, stop=False)
                    ins = pe.matmul(tile(ps_z, c), tile(rT[k], c), w.u2c[:, :], start=False, stop=True)
                ins.then_inc(done["zp"], 1)

            def turn3(s):
                pe.wait_ge(done["x3b"], s.lin(1, 1))
                wait(pe, done["x3T"], s.lin())
                for c in range(TILES):
                    ins = pe.transpose(tile(ps_t3, c), tile(x3b[s.slot(4)], c), w.ident[:, :])
                ins.then_inc(done["t3"], 1)

            def gcn1(s):
                k = s.slot()
                pe.wait_ge(done["x3T"], s.lin(1, 1))
                wait(pe, done["hT"], s.lin())
                pe.matmul(ps_w[:, :], w.g1c[:, :], x3T[k][:, :], start=True, stop=True).then_inc(done["wa"], 1)

            def gcn2(s):
                k = s.slot()
                pe.wait_ge(done["hT"], s.lin(1, 1))
                wait(pe, done["z4"], s.lin(1, -1))
                for c in range(TILES):
                    pe.matmul(tile(ps_p[k], c), tile(hT[k], c), w.g2c[:, :], start=True, stop=True)
                wait(pe, done["hst"], s.lin())
                for c in range(TILES):
                    pe.matmul(ps_h[:, TILES + c:TILES + c + 1], tile(hT[k], c), w.mean_col[:, :], start=True, stop=True)
                pe.wait_ge(done["hsq"], s.lin(1, 1))
                for c in range(TILES):
                    ins = pe.matmul(ps_h[:, c:c + 1], tile(hsq[k], c), w.mean_col[:, :], start=True, stop=True)
                ins.then_inc(done["pp"], 1)

            run_groups(pe, count, 4, [(2, mlp1), (6, gcn1), (3, mlp2), (7, gcn2), (5, turn3), (1, turn1)])

        @block.gpsimd
        def _(pool):
            top = pool.to_reg(nodes - 1)

            def add_b0(s):
                k4 = s.slot(4)
                pool.wait_ge(x_in[k4], s.lin(16, 16, div=4))
                pool.tensor_tensor(tiles3(xin[k4]), tiles3(xin[k4]), over_tiles(w.row("b0")), ALU.add).then_inc(done["y"], 1)

            def after(base):
                return lambda s: add_b0(Step(s.j, s.unroll, s.off + base))

            def put_load(s):
                k = s.slot()
                room.hold(pool, put[k], s.lin(16 * TILES, 0, div=2))
                pool.dma_start(rec[k][:, :], cols_of(facts, s.lin(), REC)).then_inc(rec_in[k], 16)

            def put_slots(s):
                k = s.slot()
                room.hold(pool, rec_in[k], s.lin(16, 16, div=2))
                for c in range(TILES):
                    pool.indirect_dma_start(slots, bass.IndirectOffsetOnAxis(rec[k][:, SCAT + c:SCAT + c + 1], 0),
                                            rec[k][:, PAY + 2 * c:PAY + 2 * c + 2], None, bounds_check=top,
                                            oob_is_err=False).then_inc(put[k], 16)

            def find_load(s):
                k = s.slot()
                room.hold(pool, found[k], s.lin(16 * TILES, 0, div=2))
                pool.dma_start(rec[k][:, :], cols_of(facts, s.lin(), REC)).then_inc(rec_in[k], 16)

            def find_slots(s):
                k = s.slot()
                room.hold(pool, kept[k], s.lin(16, 0, div=2))
                room.hold(pool, rec_in[k], s.lin(16, 16 * (uses(ng, k, 2) + 1), div=2))
                for c in range(TILES):
                    pool.indirect_dma_start(got[k][:, 2 * c:2 * c + 2], None, slots,
                                            bass.IndirectOffsetOnAxis(rec[k][:, SRC + c:SRC + c + 1], 0),
                                            bounds_check=top, oob_is_err=False).then_inc(found[k], 16)

            def keep_slots(s):
                k = s.slot()
                room.hold(pool, found[k], s.lin(16 * TILES, 16 * TILES, div=2))
                pool.dma_start(cols_of(mapped, s.lin(), 2 * TILES),
                               got[k][:, :]).then_inc(kept[k], 16)

            def paced(base, groups, loops, stages):
                def dense_at(s, part):
                    n = Step(s.j, 4, 2 * s.off + part + base) if not s.fixed else Step(0, 4, 2 * s.lin() + part + base)
                    if n.fixed and not base <= n.lin() < base + groups:
                        return
                    add_b0(n)
                run_groups(pool, loops, 2, stages + [(0, lambda s: dense_at(s, 0)), (0, lambda s: dense_at(s, 1))])
                for n in range(base + 2 * loops, base + groups):
                    add_b0(Step(0, 4, n))

            paced(0, half, ng, [(1, put_slots), (0, put_load)])
            for k in range(2):
                pool.wait_ge(put[k], 16 * TILES * uses(ng, k, 2))
            paced(half, count - half, ng, [(2, keep_slots), (1, find_slots), (0, find_load)])
            for k in range(2):
                pool.wait_ge(kept[k], 16 * uses(ng, k, 2))


def sum_layer(nc, w, ng, nodes, x, facts, along, t1, s1):
    with ExitStack() as ctx:
        room = Room(nc, ctx, "sum")
        keep, xs, xd, ys, yd, hT, x1, x1s = (room.two(k, [P, G], count=4) for k in "keep xs xd ys yd hT x1 x1s".split())
        rec = room.two("rec", [P, REC], I32, count=4)
        mask = room.two("mask", [P, TILES], I32, count=4)
        ps_t = [room.bank(f"t{i}") for i in range(2)]
        ps_w = [room.bank(f"w{i}") for i in range(2)]
        nd = Norm(room, "nd", w.eps[:, :])
        ns = Norm(room, "ns", w.eps[:, :])
        done = {k: room.sem(k + "_done") for k in "turn scan wsum ys yd ydb x1 x1s".split()}
        rec_in, keep_in, mask_in, x1_out, x1s_out = (
            room.sem2(k, 4) for k in ("rec_in", "keep_in", "mask_in", "x1_out", "x1s_out"))
        x_in = room.swdge2("x_in", 4)
        block = room.block()

        @block.sync
        def _(sp):
            def load(s):
                k = s.slot(4)
                room.hold(sp, x_in[k], s.lin(128, 0, div=4))
                sp.dma_start(rec[k][:, :], cols_of(facts, s.lin(), REC)).then_inc(rec_in[k], 16)
                room.hold(sp, done["scan"], s.lin(1, -3))
                sp.dma_start(keep[k][:, :], flat(along, s.lin(), KEEP_F)).then_inc(keep_in[k], 16)
                room.hold(sp, done["x1"], s.lin(1, -3))
                sp.dma_start(mask[k][:, :], facts[:, bass.ds(s.lin(REC, LAST), TILES)]).then_inc(mask_in[k], 16)

            def store(s):
                k = s.slot(4)
                room.hold(sp, done["x1s"], s.lin(1, 1))
                sp.dma_start(edge_rows(s1, s.lin()), tiles3(x1s[k])).then_inc(x1s_out[k], 16)
                room.hold(sp, done["x1"], s.lin(1, 1))
                sp.dma_start(edge_rows(t1, s.lin()), tiles3(x1[k])).then_inc(x1_out[k], 16)

            run_groups(sp, ng, 4, [(0, load), (4, store)])
            for k in range(4):
                sp.wait_ge(x1_out[k], 16 * uses(ng, k, 4))
                sp.wait_ge(x1s_out[k], 16 * uses(ng, k, 4))

        @block.gpsimd
        def _(pool):
            top = pool.to_reg(nodes - 1)

            def gather(s):
                k = s.slot(4)
                room.hold(pool, done["turn"], s.lin(1, -3))
                room.hold(pool, done["ys"], s.lin(1, -3))
                room.hold(pool, done["yd"], s.lin(1, -3))
                room.hold(pool, rec_in[k], s.lin(16, 16, div=4))
                for c in range(TILES):
                    for buf, at in ((xs, SRC), (xd, DSTC)):
                        pool.indirect_dma_start(tile(buf[k], c), None, x,
                                                bass.IndirectOffsetOnAxis(rec[k][:, at + c:at + c + 1], 0),
                                                bounds_check=top, oob_is_err=False).then_inc(x_in[k], 16)

            run_groups(pool, ng, 4, [(0, gather)])

        @block.tensor
        def _(pe):
            def turn(s):
                k, k4 = s.slot(), s.slot(4)
                pe.wait_ge(x_in[k4], s.lin(128, 128, div=4))
                wait(pe, done["scan"], s.lin(1, -1))
                for c in range(TILES):
                    ins = pe.transpose(tile(ps_t[k], c), tile(xs[k4], c), w.ident[:, :])
                ins.then_inc(done["turn"], 1)

            def product(s):
                k = s.slot()
                pe.wait_ge(done["scan"], s.lin(1, 1))
                wait(pe, done["yd"], s.lin(1, -1))
                for c in range(TILES):
                    ins = pe.matmul(tile(ps_w[k], c), tile(hT[s.slot(4)], c), w.t(0), start=True, stop=True)
                ins.then_inc(done["wsum"], 1)

            run_groups(pe, ng, 4, [(1, product), (0, turn)])

        @block.vector
        def _(v):
            def scan(s):
                k, k4 = s.slot(), s.slot(4)
                wait(v, done["wsum"], s.lin(1, -3))
                v.wait_ge(keep_in[k4], s.lin(16, 16, div=4))
                v.wait_ge(done["turn"], s.lin(1, 1))
                wait(v, done["scan"], s.lin())
                first = s.fixed and s.lin() == 0
                v.tensor_tensor_scan(hT[k4][:, :], keep[k4][:, :], ps_t[k][:, :],
                                     0.0 if first else hT[k4 - 1][:, G - 1:G], ALU.mult, ALU.add).then_inc(done["scan"], 1)

            def src_add(s):
                k = s.slot(4)
                v.wait_ge(x_in[k], s.lin(128, 128, div=4))
                v.tensor_tensor(tiles3(ys[k]), tiles3(xs[k]), over_tiles(w.row("b0")), ALU.add).then_inc(done["ys"], 1)

            def dst_add(s):
                k, k4 = s.slot(), s.slot(4)
                v.wait_ge(done["wsum"], s.lin(1, 1))
                v.tensor_tensor(yd[k4][:, :], ps_w[k][:, :], xd[k4][:, :], ALU.add).then_inc(done["yd"], 1)

            def dst_bias(s):
                k = s.slot(4)
                v.wait_ge(done["yd"], s.lin(1, 1))
                v.tensor_tensor(tiles3(yd[k]), tiles3(yd[k]), over_tiles(w.row("b0")), ALU.add).then_inc(done["ydb"], 1)

            def src_out(s):
                k = s.slot(4)
                wait(v, x1s_out[k], s.lin(16, 0, div=4))
                ns.scale(v, s, ys[k], x1s[k], done["x1s"])

            def dst_mask(s):
                k = s.slot(4)
                v.wait_ge(mask_in[k], s.lin(16, 16, div=4))
                nd.masked(v, s, mask[k][:, :].bitcast(F32))

            def dst_out(s):
                k = s.slot(4)
                wait(v, x1_out[k], s.lin(16, 0, div=4))
                nd.scale(v, s, yd[k], x1[k], done["x1"], masked=True)

            run_groups(v, ng, 4, [(1, lambda s: ns.invert(v, s)), (2, lambda s: nd.invert(v, s)), (0, scan),
                                  (2, dst_mask), (1, src_out), (1, dst_add), (2, dst_out), (1, dst_bias), (0, src_add),
                                  (1, lambda s: nd.stats(v, s, yd[s.slot(4)], done["ydb"])),
                                  (0, lambda s: ns.stats(v, s, ys[s.slot(4)], done["ys"])),
                                  (1, lambda s: nd.moments(v, s)), (0, lambda s: ns.moments(v, s))])

        @block.scalar
        def _(a):
            run_groups(a, ng, 4, [(1, lambda s: nd.root(a, s)), (0, lambda s: ns.root(a, s))])


def max_layer(nc, w, ng, nodes, facts, along, ew_row, mapped, t1, s1, t2):
    rows_all = ng * G
    with ExitStack() as ctx:
        room = Room(nc, ctx, "max")
        mask = room.two("mask", [P, TILES], I32, count=4)
        mi = room.two("mi", [P, 2 * TILES], I32, count=4)
        flags = room.two("flags", [P, 2, G], count=4)
        wr = room.two("wr", [1, G], count=4)
        xs, xd, xdT, ag, x2, z = (room.two(k, [P, G], count=4) for k in "xs xd xdT ag x2 z".split())
        xsT, hT, rT = (room.two(k, [P, G]) for k in "xsT hT rT".split())
        ps_d, ps_s, ps_h, ps_m, ps_r = (room.bank(k) for k in "dshmr")
        ps_z = [room.bank("z0"), room.bank("z1")]
        nz = Norm(room, "nz", w.eps[:, :])
        done = {k: room.sem(k + "_done") for k in "turnd turns xsT spread ha hT ma max ra rT zp z x2".split()}
        mask_in, mi_in, flags_in, wr_in, xd_in, xs_in, x2_out = (
            room.sem2(k, 4) for k in ("mask_in", "mi_in", "flags_in", "wr_in", "xd_in", "xs_in", "x2_out"))
        over_in = room.swdge2("over_in", 4)
        block = room.block()

        def group(s):
            return (ng - 1) - s.lin() if s.fixed else s.lin(-1, ng - 1)

        @block.sync
        def _(sp):
            def load(s):
                k = s.slot(4)
                g = group(s)
                room.hold(sp, done["turns"], s.lin(1, -3))
                sp.dma_start(mi[k][:, :], cols_of(mapped, g, 2 * TILES)).then_inc(mi_in[k], 16)
                sp.dma_start(tiles3(xs[k]), edge_rows(s1, g)).then_inc(xs_in[k], 16)
                room.hold(sp, done["turnd"], s.lin(1, -3))
                sp.dma_start(tiles3(xd[k]), edge_rows(t1, g)).then_inc(xd_in[k], 16)
                room.hold(sp, done["ha"], s.lin(1, -3))
                sp.dma_start(wr[k][:, :], ew_row[bass.ds(g, 1), :]).then_inc(wr_in[k], 16)
                room.hold(sp, done["max"], s.lin(1, -3))
                sp.dma_start(flags[k][:, :, :], along[bass.ds(g, 1), PEN_B:KEEP_B + 1, :]
                             .rearrange("a k g -> (a k) g").partition_broadcast(P)).then_inc(flags_in[k], 16)

            def load_mask(s):
                k = s.slot(4)
                room.hold(sp, done["x2"], s.lin(1, -3))
                at = group(s) * REC + FIRST
                sp.dma_start(mask[k][:, :], facts[:, bass.ds(at, TILES)]).then_inc(mask_in[k], 16)

            def store(s):
                k = s.slot(4)
                room.hold(sp, done["x2"], s.lin(1, 1))
                sp.dma_start(edge_rows(t2, group(s), nodes), tiles3(x2[k])).then_inc(x2_out[k], 16)

            run_groups(sp, ng, 4, [(0, load), (3, load_mask), (7, store)])
            for k in range(4):
                sp.wait_ge(x2_out[k], 16 * uses(ng, k, 4))

        @block.gpsimd
        def _(pool):
            top = pool.to_reg(rows_all - 1)

            def overlay(s):
                k = s.slot(4)
                room.hold(pool, xs_in[k], s.lin(16, 16, div=4))
                room.hold(pool, mi_in[k], s.lin(16, 16, div=4))
                for c in range(TILES):
                    pool.indirect_dma_start(tile(xs[k], c), None, t1,
                                            bass.IndirectOffsetOnAxis(mi[k][:, 2 * c:2 * c + 1], 0),
                                            bounds_check=top, oob_is_err=False).then_inc(over_in[k], 16)

            run_groups(pool, ng, 4, [(0, overlay)])

        @block.tensor
        def _(pe):
            def turns(s):
                k4 = s.slot(4)
                pe.wait_ge(xd_in[k4], s.lin(16, 16, div=4))
                wait(pe, done["spread"], s.lin())
                for c in range(TILES):
                    ins = pe.transpose(tile(ps_d, c), tile(xd[k4], c), w.ident[:, :])
                ins.then_inc(done["turnd"], 1)
                pe.wait_ge(over_in[k4], s.lin(64, 64, div=4))
                wait(pe, done["xsT"], s.lin())
                for c in range(TILES):
                    ins = pe.transpose(tile(ps_s, c), tile(xs[k4], c), w.ident[:, :])
                ins.then_inc(done["turns"], 1)

            def hidden(s):
                k, k4 = s.slot(), s.slot(4)
                wait(pe, done["hT"], s.lin())
                pe.wait_ge(wr_in[k4], s.lin(16, 16, div=4))
                pe.matmul(ps_h[:, :], w.wrow[:, :], wr[k4][:, :], start=True, stop=False)
                pe.wait_ge(done["spread"], s.lin(1, 1))
                pe.matmul(ps_h[:, :], w.mat("M1D"), xdT[k4][:, :], start=False, stop=False)
                pe.wait_ge(done["xsT"], s.lin(1, 1))
                pe.matmul(ps_h[:, :], w.mat("M1S"), xsT[k][:, :], start=False, stop=True).then_inc(done["ha"], 1)

            def message(s):
                k = s.slot()
                pe.wait_ge(done["hT"], s.lin(1, 1))
                wait(pe, done["max"], s.lin())
                pe.matmul(ps_m[:, :], w.mat("M2"), hT[k][:, :], start=True, stop=True).then_inc(done["ma"], 1)

            def update1(s):
                k4 = s.slot(4)
                wait(pe, done["rT"], s.lin())
                pe.matmul(ps_r[:, :], w.mat("U1X"), xdT[k4][:, :], start=True, stop=False)
                pe.wait_ge(done["max"], s.lin(1, 1))
                pe.matmul(ps_r[:, :], w.mat("U1A"), ag[k4][:, :], start=False, stop=True).then_inc(done["ra"], 1)

            def update2(s):
                k, k4 = s.slot(), s.slot(4)
                wait(pe, done["z"], s.lin(1, -1))
                pe.wait_ge(done["rT"], s.lin(1, 1))
                for c in range(TILES):
                    pe.matmul(tile(ps_z[k], c), tile(xdT[k4], c), w.ident[:, :], start=True, stop=False)
                    ins = pe.matmul(tile(ps_z[k], c), tile(rT[k], c), w.mat("U2"), start=False, stop=True)
                ins.then_inc(done["zp"], 1)

            run_groups(pe, ng, 4, [(2, message), (3, update1), (4, update2), (1, hidden), (0, turns)])

        @block.vector
        def _(v):
            def spread(s):
                k4 = s.slot(4)
                wait(v, done["zp"], s.lin(1, -3))
                v.wait_ge(flags_in[k4], s.lin(16, 16, div=4))
                v.wait_ge(done["turnd"], s.lin(1, 1))
                wait(v, done["spread"], s.lin())
                first = s.fixed and s.lin() == 0
                v.tensor_tensor_scan(xdT[k4][:, ::-1], flags[k4][:, 1, ::-1], ps_d[:, ::-1],
                                     0.0 if first else xdT[k4 - 1][:, 0:1], ALU.mult, ALU.add).then_inc(done["spread"], 1)

            def maximum(s):
                k4 = s.slot(4)
                wait(v, done["ra"], s.lin(1, -3))
                v.wait_ge(done["ma"], s.lin(1, 1))
                wait(v, done["max"], s.lin())
                first = s.fixed and s.lin() == 0
                v.tensor_tensor_scan(ag[k4][:, ::-1], flags[k4][:, 0, ::-1], ps_m[:, ::-1],
                                     0.0 if first else ag[k4 - 1][:, 0:1], ALU.add, ALU.max).then_inc(done["max"], 1)

            def add_bias(s):
                k, k4 = s.slot(), s.slot(4)
                v.wait_ge(done["zp"], s.lin(1, 1))
                v.tensor_tensor(tiles3(z[k4]), tiles3(ps_z[k]), over_tiles(w.row("c2")), ALU.add).then_inc(done["z"], 1)

            def mask_factors(s):
                k = s.slot(4)
                v.wait_ge(mask_in[k], s.lin(16, 16, div=4))
                nz.masked(v, s, mask[k][:, :].bitcast(F32))

            def finish(s):
                k = s.slot(4)
                wait(v, x2_out[k], s.lin(16, 0, div=4))
                nz.scale(v, s, z[k], x2[k], done["x2"], masked=True)

            run_groups(v, ng, 4, [(5, lambda s: nz.invert(v, s)), (2, maximum), (5, mask_factors), (5, finish),
                                  (4, add_bias), (4, lambda s: nz.stats(v, s, z[s.slot(4)], done["z"])),
                                  (4, lambda s: nz.moments(v, s)), (0, spread)])

        @block.scalar
        def _(a):
            def copy_src(s):
                k = s.slot()
                wait(a, done["ha"], s.lin(1, -1))
                a.wait_ge(done["turns"], s.lin(1, 1))
                a.copy(xsT[k][:, :], ps_s[:, :]).then_inc(done["xsT"], 1)

            def relu1(s):
                k = s.slot()
                wait(a, done["ma"], s.lin(1, -1))
                a.wait_ge(done["ha"], s.lin(1, 1))
                a.activation(hT[k][:, :], ps_h[:, :], ACT.Relu, bias=w.col("mb1")).then_inc(done["hT"], 1)

            def relu2(s):
                k = s.slot()
                wait(a, done["zp"], s.lin(1, -1))
                a.wait_ge(done["ra"], s.lin(1, 1))
                a.activation(rT[k][:, :], ps_r[:, :], ACT.Relu, bias=w.c1b[:, :]).then_inc(done["rT"], 1)

            run_groups(a, ng, 4, [(3, relu2), (1, relu1), (0, copy_src), (4, lambda s: nz.root(a, s))])


def attention_layer(nc, w, ng, nodes, facts, along, edge_attr, mapped, t2, t3, s3, d3):
    rows_all = nodes + ng * G
    with ExitStack() as ctx:
        room = Room(nc, ctx, "att")
        rec = room.two("rec", [P, REC], I32, count=4)
        mi = room.two("mi", [P, 2 * TILES], I32, count=4)
        keep, ea, xs, xd, xsT, xdT, x3, x3n, x3s = (
            room.two(k, [P, G], count=4) for k in "keep ea xs xd xsT xdT x3 x3n x3s".split())
        eT, q, ev, qk, qke, sc, pr, m, wv, zT = (
            room.two(k, [P, G]) for k in "eT q ev qk qke sc pr m wv zT".split())
        ps_d, ps_s, ps_q, ps_e, ps_k, ps_v, ps_sc, ps_z = (room.bank(k) for k in ("d", "s", "q", "e", "k", "v", "sc", "z"))
        nz = Norm(room, "nz", w.eps[:, :])
        ns = Norm(room, "ns", w.eps[:, :])
        done = {k: room.sem(k + "_done") for k in
                ("turnd turns turne xsT eT spread qa q eva ev ka qk qke sca sc pr va m sum zT turnz x3 x3n x3s").split()}
        rec_in, mi_in, keep_in, ea_in, xd_in, x3_out, x3n_out, x3s_out = (
            room.sem2(k, 4) for k in ("rec_in", "mi_in", "keep_in", "ea_in", "xd_in", "x3_out", "x3n_out", "x3s_out"))
        xs_in = room.swdge2("xs_in", 4)
        block = room.block()

        @block.sync
        def _(sp):
            def load(s):
                k = s.slot(4)
                g = s.lin()
                room.hold(sp, xs_in[k], s.lin(64, 0, div=4))
                sp.dma_start(mi[k][:, :], cols_of(mapped, g, 2 * TILES)).then_inc(mi_in[k], 16)
                room.hold(sp, done["turnd"], s.lin(1, -3))
                sp.dma_start(tiles3(xd[k]), edge_rows(t2, g, nodes)).then_inc(xd_in[k], 16)
                room.hold(sp, done["turne"], s.lin(1, -3))
                sp.dma_start(tiles3(ea[k]), edge_rows(edge_attr, g)).then_inc(ea_in[k], 16)
                room.hold(sp, done["sum"], s.lin(1, -3))
                sp.dma_start(keep[k][:, :], flat(along, g, KEEP_F)).then_inc(keep_in[k], 16)

            def load_facts(s):
                k = s.slot(4)
                room.hold(sp, done["x3n"], s.lin(1, -3))
                sp.dma_start(rec[k][:, :], cols_of(facts, s.lin(), REC)).then_inc(rec_in[k], 16)

            def store(s):
                k = s.slot(4)
                g = s.lin()
                room.hold(sp, done["x3s"], s.lin(1, 1))
                sp.dma_start(edge_rows(s3, g), tiles3(x3s[k])).then_inc(x3s_out[k], 16)

            def store_dst(s):
                k = s.slot(4)
                g = s.lin()
                room.hold(sp, done["x3"], s.lin(1, 1))
                sp.dma_start(edge_rows(d3, g), tiles3(x3[k])).then_inc(x3_out[k], 16)
                room.hold(sp, done["x3n"], s.lin(1, 1))
                sp.dma_start(edge_rows(t3, g), tiles3(x3n[k])).then_inc(x3n_out[k], 16)

            run_groups(sp, ng, 4, [(0, load), (3, load_facts), (3, store), (7, store_dst)])
            for k in range(4):
                for sem in (x3_out, x3n_out, x3s_out):
                    sp.wait_ge(sem[k], 16 * uses(ng, k, 4))

        @block.gpsimd
        def _(pool):
            top = pool.to_reg(rows_all - 1)

            def gather(s):
                k = s.slot(4)
                room.hold(pool, done["turns"], s.lin(1, -3))
                room.hold(pool, done["x3s"], s.lin(1, -3))
                room.hold(pool, mi_in[k], s.lin(16, 16, div=4))
                for c in range(TILES):
                    pool.indirect_dma_start(tile(xs[k], c), None, t2,
                                            bass.IndirectOffsetOnAxis(mi[k][:, 2 * c + 1:2 * c + 2], 0),
                                            bounds_check=top, oob_is_err=False).then_inc(xs_in[k], 16)

            def multiply_edge(s):
                k = s.slot()
                pool.wait_ge(done["qk"], s.lin(1, 1))
                pool.wait_ge(done["ev"], s.lin(1, 1))
                wait(pool, done["sca"], s.lin(1, -1))
                pool.tensor_tensor(qke[k][:, :], qk[k][:, :], ev[k][:, :], ALU.mult).then_inc(done["qke"], 1)

            def add_own(s):
                k, k4 = s.slot(), s.slot(4)
                pool.wait_ge(done["sum"], s.lin(1, 1))
                pool.wait_ge(done["spread"], s.lin(1, 1))
                wait(pool, done["turnz"], s.lin(1, -1))
                pool.tensor_tensor(zT[k][:, :], wv[k][:, :], xdT[k4][:, :], ALU.add).then_inc(done["zT"], 1)

            run_groups(pool, ng, 4, [(3, multiply_edge), (5, add_own), (0, gather)])

        @block.tensor
        def _(pe):
            def turn(s, buf, bank, arrived, per, freed, over):
                k = s.slot(4)
                pe.wait_ge(arrived[k], s.lin(per, per, div=4))
                wait(pe, freed, s.lin())
                for c in range(TILES):
                    ins = pe.transpose(tile(bank, c), tile(buf[k], c), w.ident[:, :])
                ins.then_inc(over, 1)

            def turns(s):
                wait(pe, done["ev"], s.lin())
                turn(s, ea, ps_e, ea_in, 16, done["eT"], done["turne"])
                turn(s, xd, ps_d, xd_in, 16, done["spread"], done["turnd"])
                turn(s, xs, ps_s, xs_in, 64, done["xsT"], done["turns"])

            def products(s):
                k, k4 = s.slot(), s.slot(4)
                pe.wait_ge(done["eT"], s.lin(1, 1))
                pe.matmul(ps_e[:, :], w.t(3), eT[k][:, :], start=True, stop=True).then_inc(done["eva"], 1)
                pe.wait_ge(done["spread"], s.lin(1, 1))
                wait(pe, done["q"], s.lin())
                pe.matmul(ps_q[:, :], w.t(1), xdT[k4][:, :], start=True, stop=True).then_inc(done["qa"], 1)
                pe.wait_ge(done["xsT"], s.lin(1, 1))
                wait(pe, done["qk"], s.lin())
                pe.matmul(ps_k[:, :], w.t(2), xsT[k4][:, :], start=True, stop=True).then_inc(done["ka"], 1)

            def values(s):
                pe.wait_ge(done["xsT"], s.lin(1, 1))
                wait(pe, done["m"], s.lin())
                pe.matmul(ps_v[:, :], w.t(4), xsT[s.slot(4)][:, :], start=True, stop=True).then_inc(done["va"], 1)

            def scores(s):
                k = s.slot()
                pe.wait_ge(done["qke"], s.lin(1, 1))
                wait(pe, done["sc"], s.lin())
                pe.matmul(ps_sc[:, :], w.heads[:, :], qke[k][:, :], start=True, stop=True).then_inc(done["sca"], 1)

            def turn_z(s):
                k = s.slot()
                pe.wait_ge(done["zT"], s.lin(1, 1))
                wait(pe, done["x3"], s.lin())
                for c in range(TILES):
                    ins = pe.transpose(tile(ps_z, c), tile(zT[k], c), w.ident[:, :])
                ins.then_inc(done["turnz"], 1)

            run_groups(pe, ng, 4, [(1, products), (3, values), (2, scores), (4, turn_z), (0, turns)])

        @block.vector
        def _(v):
            def spread(s):
                k4 = s.slot(4)
                wait(v, done["qa"], s.lin(1, -3))
                wait(v, done["zT"], s.lin(1, -3))
                v.wait_ge(keep_in[k4], s.lin(16, 16, div=4))
                v.wait_ge(done["turnd"], s.lin(1, 1))
                wait(v, done["spread"], s.lin())
                first = s.fixed and s.lin() == 0
                v.tensor_tensor_scan(xdT[k4][:, :], keep[k4][:, :], ps_d[:, :],
                                     0.0 if first else xdT[k4 - 1][:, G - 1:G], ALU.mult, ALU.add).then_inc(done["spread"], 1)

            def src_stats(s):
                k = s.slot(4)
                v.wait_ge(xs_in[k], s.lin(64, 64, div=4))
                ns.stats(v, s, xs[k])

            def multiply(s):
                k = s.slot()
                v.wait_ge(done["q"], s.lin(1, 1))
                v.wait_ge(done["ka"], s.lin(1, 1))
                wait(v, done["qke"], s.lin(1, -1))
                v.scalar_tensor_tensor(out=qk[k][:, :], in0=ps_k[:, :], scalar=w.col("bk"), in1=q[k][:, :],
                                       op0=ALU.add, op1=ALU.mult).then_inc(done["qk"], 1)

            def clip(s):
                k = s.slot()
                v.wait_ge(done["sca"], s.lin(1, 1))
                wait(v, done["pr"], s.lin(1, -1))
                v.tensor_scalar(sc[k][:, :], ps_sc[:, :], -5.0, 5.0, ALU.max, ALU.min).then_inc(done["sc"], 1)

            def weigh(s):
                k = s.slot()
                v.wait_ge(done["pr"], s.lin(1, 1))
                v.wait_ge(done["va"], s.lin(1, 1))
                v.scalar_tensor_tensor(out=m[k][:, :], in0=ps_v[:, :], scalar=w.col("bv"), in1=pr[k][:, :],
                                       op0=ALU.add, op1=ALU.mult).then_inc(done["m"], 1)

            def sum_up(s):
                k = s.slot()
                v.wait_ge(done["m"], s.lin(1, 1))
                wait(v, done["zT"], s.lin(1, -1))
                wait(v, done["sum"], s.lin())
                first = s.fixed and s.lin() == 0
                v.tensor_tensor_scan(wv[k][:, :], keep[s.slot(4)][:, :], m[k][:, :],
                                     0.0 if first else wv[1 - k][:, G - 1:G], ALU.mult, ALU.add).then_inc(done["sum"], 1)

            def mask_factors(s):
                k = s.slot(4)
                v.wait_ge(rec_in[k], s.lin(16, 16, div=4))
                nz.masked(v, s, rec[k][:, LAST:LAST + TILES].bitcast(F32))

            def dst_out(s):
                k = s.slot(4)
                wait(v, x3_out[k], s.lin(16, 0, div=4))
                wait(v, done["x3n"], s.lin(1, -3))
                nz.scale(v, s, ps_z, x3[k], done["x3"], masked=True)

            run_groups(v, ng, 4, [(5, lambda s: nz.invert(v, s)), (1, lambda s: ns.invert(v, s)), (3, weigh),
                                  (5, mask_factors), (1, lambda s: ns.offset(v, s)), (5, dst_out), (0, src_stats),
                                  (3, sum_up), (1, multiply), (0, lambda s: ns.moments(v, s)), (2, clip),
                                  (4, lambda s: nz.stats(v, s, ps_z, done["turnz"])), (0, spread),
                                  (4, lambda s: nz.moments(v, s))])

        @block.scalar
        def _(a):
            def out_of(s, out, bank, before, over, bias=None):
                a.wait_ge(before, s.lin(1, 1))
                if bias is None:
                    a.copy(out[:, :], bank[:, :]).then_inc(over, 1)
                else:
                    a.activation(out[:, :], bank[:, :], ACT.Identity, bias=bias).then_inc(over, 1)

            def edge_in(s):
                wait(a, done["eva"], s.lin(1, -1))
                out_of(s, eT[s.slot()], ps_e, done["turne"], done["eT"])

            def src_in(s):
                wait(a, done["ka"], s.lin(1, -3))
                wait(a, done["va"], s.lin(1, -3))
                out_of(s, xsT[s.slot(4)], ps_s, done["turns"], done["xsT"])

            def factors(s):
                wait(a, done["qke"], s.lin(1, -1))
                out_of(s, ev[s.slot()], ps_e, done["eva"], done["ev"], w.col("be"))
                wait(a, done["qk"], s.lin(1, -1))
                out_of(s, q[s.slot()], ps_q, done["qa"], done["q"], w.col("bq"))

            def src_out(s):
                k = s.slot(4)
                wait(a, x3s_out[k], s.lin(16, 0, div=4))
                a.wait_ge(xs_in[k], s.lin(64, 64, div=4))
                ns.scale_a(a, s, xs[k], x3s[k], done["x3s"])

            def own_scaled(s):
                k = s.slot(4)
                a.wait_ge(rec_in[k], s.lin(16, 16, div=4))
                a.wait_ge(done["x3"], s.lin(1, 1))
                wait(a, x3n_out[k], s.lin(16, 0, div=4))
                dinv = rec[k][:, DINV:DINV + TILES].bitcast(F32)
                for c in range(TILES):
                    ins = a.activation(tile(x3n[k], c), tile(x3[k], c), ACT.Copy, scale=dinv[:, c:c + 1])
                ins.then_inc(done["x3n"], 1)

            def exponent(s):
                k = s.slot()
                a.wait_ge(done["sc"], s.lin(1, 1))
                wait(a, done["m"], s.lin(1, -1))
                a.activation(pr[k][:, :], sc[k][:, :], ACT.Exp).then_inc(done["pr"], 1)

            run_groups(a, ng, 4, [(1, factors), (1, src_out), (5, own_scaled), (2, exponent),
                                  (0, lambda s: ns.root(a, s)), (0, edge_in), (0, src_in),
                                  (4, lambda s: nz.root(a, s))])


def gcn_layer(nc, w, ng, nodes, facts, along, mapped, own_t, src_t, last, next_t=None, next_s=None, d3=None, out=None):
    with ExitStack() as ctx:
        room = Room(nc, ctx, "gcn2" if last else "gcn1")
        rec = room.two("rec", [P, REC], I32, count=4)
        mi = room.two("mi", [P, 2 * TILES], I32, count=4)
        flags = room.two("flags", [P, 2, G], count=4)
        xs, xd, o_d = (room.two(k, [P, G], count=4) for k in "xs xd o_d".split())
        xsT, ws, aT, sT, c_d, r_d, h_d, g_d = (room.two(k, [P, G]) for k in "xsT ws aT sT c_d r_d h_d g_d".split())
        x3 = room.two("x3", [P, G], count=4) if last else None
        r_s, h_s, g_s = (None, None, None) if last else (room.two(k, [P, G]) for k in "r_s h_s g_s".split())
        o_s = None if last else room.two("o_s", [P, G], count=4)
        ps_s = [room.bank("s0"), room.bank("s1")]
        ps_d = [room.bank("d0"), room.bank("d1")]
        ps_pd = [room.bank("pd0"), room.bank("pd1")]
        ps_ps = [room.bank("ps0"), room.bank("ps1")]
        nd = Norm(room, "nd", w.eps[:, :])
        ns = None if last else Norm(room, "ns", w.eps[:, :])
        weight = w.mat("G2") if last else w.mat("G1")
        bias = w.row("gb2") if last else w.row("gb1")
        done = {k: room.sem(k + "_done") for k in
                "turns turnd xsT ws sum sT pd psr cd rd hd hg hb od rs hs sg os".split()}
        rec_in, mi_in, flags_in, xd_in, xs_in, x3_in, os_out = (
            room.sem2(k, 4) for k in ("rec_in", "mi_in", "flags_in", "xd_in", "xs_in", "x3_in", "os_out"))
        over_in = room.swdge2("over_in", 4)
        od_out = room.swdge2("od_out", 4) if last else room.sem2("od_out", 4)
        block = room.block()

        @block.sync
        def _(sp):
            def load(s):
                k = s.slot(4)
                g = s.lin()
                room.hold(sp, done["turns"], s.lin(1, -3))
                sp.dma_start(mi[k][:, :], cols_of(mapped, g, 2 * TILES)).then_inc(mi_in[k], 16)
                sp.dma_start(tiles3(xs[k]), edge_rows(src_t, g)).then_inc(xs_in[k], 16)
                room.hold(sp, done["turnd"], s.lin(1, -3))
                sp.dma_start(tiles3(xd[k]), edge_rows(own_t, g)).then_inc(xd_in[k], 16)
                room.hold(sp, done["sum"], s.lin(1, -3))
                sp.dma_start(flags[k][:, :, :], along[bass.ds(g, 1), KEEP_F:W_F + 1, :]
                             .rearrange("a k g -> (a k) g").partition_broadcast(P)).then_inc(flags_in[k], 16)

            def load_facts(s):
                k = s.slot(4)
                g = s.lin()
                room.hold(sp, done["od"], s.lin(1, -3))
                if last:
                    room.hold(sp, od_out[k], s.lin(16 * TILES, 0, div=4))
                sp.dma_start(rec[k][:, :], cols_of(facts, g, REC)).then_inc(rec_in[k], 16)
                if last:
                    sp.dma_start(tiles3(x3[k]), edge_rows(d3, g)).then_inc(x3_in[k], 16)

            def store(s):
                k = s.slot(4)
                g = s.lin()
                room.hold(sp, done["os"], s.lin(1, 1))
                sp.dma_start(edge_rows(next_s, g), tiles3(o_s[k])).then_inc(os_out[k], 16)
                room.hold(sp, done["od"], s.lin(1, 1))
                sp.dma_start(edge_rows(next_t, g), tiles3(o_d[k])).then_inc(od_out[k], 16)

            if last:
                run_groups(sp, ng, 4, [(0, load), (1, load_facts)])
            else:
                run_groups(sp, ng, 4, [(0, load), (1, load_facts), (6, store)])
                for k in range(4):
                    sp.wait_ge(os_out[k], 16 * uses(ng, k, 4))
                    sp.wait_ge(od_out[k], 16 * uses(ng, k, 4))

        @block.gpsimd
        def _(pool):
            top = pool.to_reg(ng * G - 1)
            top_node = pool.to_reg(nodes - 1)

            def overlay(s):
                k = s.slot(4)
                room.hold(pool, xs_in[k], s.lin(16, 16, div=4))
                room.hold(pool, mi_in[k], s.lin(16, 16, div=4))
                for c in range(TILES):
                    pool.indirect_dma_start(tile(xs[k], c), None, own_t,
                                            bass.IndirectOffsetOnAxis(mi[k][:, 2 * c:2 * c + 1], 0),
                                            bounds_check=top, oob_is_err=False).then_inc(over_in[k], 16)

            def weigh(s):
                k = s.slot()
                pool.wait_ge(done["xsT"], s.lin(1, 1))
                pool.wait_ge(flags_in[s.slot(4)], s.lin(16, 16, div=4))
                wait(pool, done["sum"], s.lin(1, -1))
                pool.tensor_tensor(ws[k][:, :], xsT[k][:, :], flags[s.slot(4)][:, 1, :], ALU.mult).then_inc(done["ws"], 1)

            def src_gamma(s):
                k = s.slot()
                pool.wait_ge(done["hs"], s.lin(1, 1))
                wait(pool, done["os"], s.lin(1, -1))
                pool.tensor_tensor(tiles3(g_s[k]), tiles3(h_s[k]), over_tiles(w.row("gamma")), ALU.mult).then_inc(done["sg"], 1)

            def scatter(s):
                k = s.slot(4)
                room.hold(pool, done["od"], s.lin(1, 1))
                for c in range(TILES):
                    pool.indirect_dma_start(out, bass.IndirectOffsetOnAxis(rec[k][:, SCAT + c:SCAT + c + 1], 0),
                                            tile(o_d[k], c), None, bounds_check=top_node,
                                            oob_is_err=False).then_inc(od_out[k], 16)

            if last:
                run_groups(pool, ng, 4, [(0, overlay), (3, scatter)])
                for k in range(4):
                    pool.wait_ge(od_out[k], 16 * TILES * uses(ng, k, 4))
            else:
                run_groups(pool, ng, 4, [(2, weigh), (4, src_gamma), (0, overlay)])

        @block.tensor
        def _(pe):
            def turns(s):
                k, k4 = s.slot(), s.slot(4)
                pe.wait_ge(over_in[k4], s.lin(64, 64, div=4))
                wait(pe, done["ws"] if last else done["xsT"], s.lin(1, -1))
                for c in range(TILES):
                    ins = pe.transpose(tile(ps_s[k], c), tile(xs[k4], c), w.ident[:, :])
                ins.then_inc(done["turns"], 1)
                pe.wait_ge(xd_in[k4], s.lin(16, 16, div=4))
                wait(pe, done["sT"], s.lin(1, -1))
                for c in range(TILES):
                    ins = pe.transpose(tile(ps_d[k], c), tile(xd[k4], c), w.ident[:, :])
                ins.then_inc(done["turnd"], 1)

            def src_product(s):
                k = s.slot()
                pe.wait_ge(done["xsT"], s.lin(1, 1))
                wait(pe, done["rs"], s.lin(1, -1))
                for c in range(TILES):
                    pe.matmul(tile(ps_ps[k], c), w.ones16[:, :], w.gb1s[:, :], start=True, stop=False)
                    ins = pe.matmul(tile(ps_ps[k], c), tile(xsT[k], c), weight, start=False, stop=True)
                ins.then_inc(done["psr"], 1)

            def dst_product(s):
                k = s.slot()
                pe.wait_ge(done["sT"], s.lin(1, 1))
                wait(pe, done["cd"], s.lin(1, -1))
                for c in range(TILES):
                    ins = pe.matmul(tile(ps_pd[k], c), tile(sT[k], c), weight, start=True, stop=True)
                ins.then_inc(done["pd"], 1)

            if last:
                run_groups(pe, ng, 4, [(1, dst_product), (0, turns)])
            else:
                run_groups(pe, ng, 4, [(2, dst_product), (1, src_product), (0, turns)])

        @block.vector
        def _(v):
            def weigh(s):
                k = s.slot()
                v.wait_ge(flags_in[s.slot(4)], s.lin(16, 16, div=4))
                v.wait_ge(done["turns"], s.lin(1, 1))
                v.tensor_tensor(ws[k][:, :], ps_s[k][:, :], flags[s.slot(4)][:, 1, :], ALU.mult).then_inc(done["ws"], 1)

            def sum_up(s):
                k = s.slot()
                v.wait_ge(flags_in[s.slot(4)], s.lin(16, 16, div=4))
                v.wait_ge(done["ws"], s.lin(1, 1))
                wait(v, done["sum"], s.lin())
                first = s.fixed and s.lin() == 0
                v.tensor_tensor_scan(aT[k][:, :], flags[s.slot(4)][:, 0, :], ws[k][:, :],
                                     0.0 if first else aT[1 - k][:, G - 1:G], ALU.mult, ALU.add).then_inc(done["sum"], 1)

            def add_own(s):
                k = s.slot()
                v.wait_ge(done["sum"], s.lin(1, 1))
                v.wait_ge(done["turnd"], s.lin(1, 1))
                wait(v, done["pd"], s.lin(1, -1))
                v.tensor_tensor(sT[k][:, :], aT[k][:, :], ps_d[k][:, :], ALU.add).then_inc(done["sT"], 1)

            def dst_bias(s):
                k, k4 = s.slot(), s.slot(4)
                dinv = rec[k4][:, DINV:DINV + TILES].bitcast(F32)
                v.wait_ge(rec_in[k4], s.lin(16, 16, div=4))
                v.wait_ge(done["pd"], s.lin(1, 1))
                wait(v, done["rd"], s.lin(1, -1))
                for c in range(TILES):
                    ins = v.scalar_tensor_tensor(out=tile(c_d[k], c), in0=tile(ps_pd[k], c), scalar=dinv[:, c:c + 1],
                                                 in1=bias, op0=ALU.mult, op1=ALU.add)
                ins.then_inc(done["cd"], 1)

            def dst_norm(s):
                nd.scale(v, s, r_d[s.slot()], h_d[s.slot()], done["hd"])

            def dst_gamma(s):
                k = s.slot()
                v.wait_ge(done["hd"], s.lin(1, 1))
                v.tensor_tensor(tiles3(g_d[k]), tiles3(h_d[k]), over_tiles(w.row("gamma")), ALU.mult).then_inc(done["hg"], 1)

            def dst_beta(s):
                k = s.slot()
                v.wait_ge(done["hg"], s.lin(1, 1))
                v.tensor_tensor(tiles3(g_d[k]), tiles3(g_d[k]), over_tiles(w.row("beta")), ALU.add).then_inc(done["hb"], 1)

            def src_beta(s):
                k, k4 = s.slot(), s.slot(4)
                v.wait_ge(done["sg"], s.lin(1, 1))
                wait(v, os_out[k4], s.lin(16, 0, div=4))
                v.tensor_tensor(tiles3(o_s[k4]), tiles3(g_s[k]), over_tiles(w.row("beta")), ALU.add).then_inc(done["os"], 1)

            def add_x3(s):
                k, k4 = s.slot(), s.slot(4)
                v.wait_ge(done["cd"], s.lin(1, 1))
                v.wait_ge(x3_in[k4], s.lin(16, 16, div=4))
                v.tensor_tensor(r_d[k][:, :], c_d[k][:, :], x3[k4][:, :], ALU.add).then_inc(done["rd"], 1)

            def last_out(s):
                k4 = s.slot(4)
                wait(v, od_out[k4], s.lin(64, 0, div=4))
                nd.scale(v, s, r_d[s.slot()], o_d[k4], done["od"])

            dst_stats = lambda s: nd.stats(v, s, r_d[s.slot()], done["rd"])
            dst_moments = lambda s: nd.moments(v, s)
            if last:
                run_groups(v, ng, 4, [(2, lambda s: nd.invert(v, s)), (0, weigh), (1, dst_bias), (0, sum_up), (2, last_out),
                                      (1, add_x3), (0, add_own), (1, dst_stats), (1, dst_moments)])
            else:
                run_groups(v, ng, 4, [(3, lambda s: nd.invert(v, s)), (2, lambda s: ns.invert(v, s)), (1, sum_up),
                                      (3, dst_norm), (2, lambda s: ns.offset(v, s)), (1, add_own), (3, dst_gamma),
                                      (2, dst_bias), (1, lambda s: ns.stats(v, s, r_s[s.slot()], done["rs"])),
                                      (3, dst_beta), (1, lambda s: ns.moments(v, s)), (3, src_beta),
                                      (2, dst_stats), (2, dst_moments)])

        @block.scalar
        def _(a):
            def copy_src(s):
                k = s.slot()
                wait(a, done["psr"], s.lin(1, -1))
                wait(a, done["ws"], s.lin(1, -1))
                a.wait_ge(done["turns"], s.lin(1, 1))
                a.copy(xsT[k][:, :], ps_s[k][:, :]).then_inc(done["xsT"], 1)

            def dst_relu(s):
                k = s.slot()
                a.wait_ge(done["cd"], s.lin(1, 1))
                wait(a, done["hd"], s.lin(1, -1))
                a.activation(r_d[k][:, :], c_d[k][:, :], ACT.Relu).then_inc(done["rd"], 1)

            def src_relu(s):
                k = s.slot()
                a.wait_ge(done["psr"], s.lin(1, 1))
                wait(a, done["hs"], s.lin(1, -1))
                a.activation(r_s[k][:, :], ps_ps[k][:, :], ACT.Relu).then_inc(done["rs"], 1)

            def src_norm(s):
                wait(a, done["sg"], s.lin(1, -1))
                ns.scale_a(a, s, r_s[s.slot()], h_s[s.slot()], done["hs"])

            def dst_scaled(s):
                k, k4 = s.slot(), s.slot(4)
                a.wait_ge(done["hb"], s.lin(1, 1))
                wait(a, od_out[k4], s.lin(16, 0, div=4))
                dinv = rec[k4][:, DINV:DINV + TILES].bitcast(F32)
                for c in range(TILES):
                    ins = a.activation(tile(o_d[k4], c), tile(g_d[k], c), ACT.Copy, scale=dinv[:, c:c + 1])
                ins.then_inc(done["od"], 1)

            if last:
                run_groups(a, ng, 4, [(1, lambda s: nd.root(a, s))])
            else:
                run_groups(a, ng, 4, [(1, src_relu), (2, src_norm), (4, dst_scaled), (2, dst_relu), (0, copy_src),
                                      (1, lambda s: ns.root(a, s)), (2, lambda s: nd.root(a, s))])


def build(nc, x, ints, ew, edge_attr, mats, cols, rows, wrow, out):
    nodes = x.shape[0]
    ng = ew.shape[0]

    def table(name, shape, dt=F32):
        return nc.dram_tensor(name, shape, dt).ap()

    facts = table("facts", [P, ng * REC], I32)
    along = table("along", [ng, 4, G])
    slots = table("slots", [nodes, 2], I32)
    mapped = table("mapped", [P, ng * 2 * TILES], I32)
    t1, s1 = table("t1", [ng * G, D]), table("s1", [ng * G, D])
    t2 = table("t2", [nodes + ng * G, D])
    t3, s3, d3 = table("t3", [ng * G, D]), table("s3", [ng * G, D]), table("d3", [ng * G, D])
    th, sh = table("th", [ng * G, D]), table("sh", [ng * G, D])
    with ExitStack() as ctx:
        w = Weights(Room(nc, ctx, "w"))
        prepare_weights(nc, w, mats, cols, rows, wrow)
        prepare_edges(nc, w, ng, nodes, ints, ew, along, facts.rearrange("p (g r) -> p g r", r=REC), slots)
        dense_pass(nc, w, ng, nodes, x, out, t2, facts, slots, mapped)
        sum_layer(nc, w, ng, nodes, x, facts, along, t1, s1)
        max_layer(nc, w, ng, nodes, facts, along, ew, mapped, t1, s1, t2)
        attention_layer(nc, w, ng, nodes, facts, along, edge_attr, mapped, t2, t3, s3, d3)
        gcn_layer(nc, w, ng, nodes, facts, along, mapped, t3, s3, False, next_t=th, next_s=sh)
        gcn_layer(nc, w, ng, nodes, facts, along, mapped, th, sh, True, d3=d3, out=out)


def kernel(**inputs):
    import numpy as np
    import concourse.bacc as bacc
    from concourse.bass_utils import run_bass_kernel_spmd as run

    a = {k: np.ascontiguousarray(v) for k, v in inputs.items()}
    nodes, d = a["x"].shape
    edges = a["src"].shape[0]
    ng = -(-edges // G)
    pad = ng * G - edges
    fill = np.full((pad,), nodes, np.int32)
    src = np.concatenate([a["src"], np.zeros((pad,), np.int32)])
    dst = np.concatenate([a["dst"], fill])
    before = np.concatenate([np.full((1,), nodes + 1, np.int32), dst[:-1]])
    after = np.concatenate([dst[1:], np.full((1,), nodes + 1, np.int32)])
    m1 = a["L1_gnn_W1"]
    u1 = a["L1_gnn_U1"]
    mats = [a["L0_gnn_W"], a["L2_gnn_Wq"], a["L2_gnn_Wk"], a["L2_gnn_We"], a["L2_gnn_Wv"], m1[:d], m1[d:2 * d],
            a["L1_gnn_W2"], u1[:d], u1[d:], a["L1_gnn_U2"], a["L3_gnn_W1"], a["L3_gnn_W2"]]
    vecs = [a[k] for k in ("L0_gnn_b", "L1_gnn_b1", "L1_gnn_b2", "L1_gnn_c1", "L1_gnn_c2", "L2_gnn_bq", "L2_gnn_bk",
                           "L2_gnn_be", "L2_gnn_bv", "L3_gnn_b1", "L3_gnn_g1", "L3_gnn_beta1", "L3_gnn_b2")]
    arrays = {
        "x": a["x"],
        "ints": np.stack([src, dst, before, after]).reshape(4, ng, G),
        "ew": np.concatenate([a["edge_weight"], np.zeros((pad,), np.float32)]).reshape(ng, G),
        "edge_attr": np.concatenate([a["edge_attr_128"], np.zeros((pad, d), np.float32)]),
        "mats": np.ascontiguousarray(np.concatenate(mats, axis=1)),
        "cols": np.ascontiguousarray(np.stack(vecs, axis=1)),
        "rows": np.stack(vecs),
        "wrow": np.ascontiguousarray(m1[2 * d:]),
    }
    nc = bacc.Bacc("TRN2", target_bir_lowering=False, num_devices=1)
    aps = [nc.dram_tensor(k, v.shape, mybir.dt.from_np(v.dtype), kind="ExternalInput").ap() for k, v in arrays.items()]
    out = nc.dram_tensor("out", (nodes, d), F32, kind="ExternalOutput").ap()
    build(nc, *aps, out)
    result = run(nc, [arrays], core_ids=[0])
    return result.results[0]["out"]
```

```python
from contextlib import ExitStack

import concourse.bass as bass
from concourse import mybir

F32 = mybir.dt.float32
I32 = mybir.dt.int32
BF16 = mybir.dt.bfloat16
ALU = mybir.AluOpType
ACT = mybir.ActivationFunctionType

P = 128
D = 128
TILES = 4
G = P * TILES
EPS = 1e-5
X2_LAG, O_LAG = 7, 12
NO_ROW = 1 << 20
BIG = 3.0e38

SRC, DSTC, SCAT, PAY, LAST, FIRST, DINV, WROW = 0, 4, 8, 12, 20, 24, 28, 32
REC = 36
PEN_B, KEEP_B, KEEP_F, W_F = 0, 1, 2, 3

WEIGHTS = ["W0", "Wq", "Wk", "We", "Wv", "M1S", "M1D", "M2", "U1X", "U1A", "U2", "G1", "G2"]
VECTORS = ["b0", "mb1", "mb2", "c1", "c2", "bq", "bk", "be", "bv", "gb1", "gamma", "beta", "gb2"]


class Step:

    def __init__(self, j, unroll, off):
        self.j, self.unroll, self.off = j, unroll, off
        self.fixed = isinstance(j, int)

    def lin(self, mult=1, add=0, div=1):
        return self.j * (mult * (self.unroll // div)) + (mult * (self.off // div) + add)

    def slot(self, count=2):
        return self.off % count


def wait(eng, sem, value):
    if isinstance(value, int) and value <= 0:
        return
    eng.wait_ge(sem, value)


def uses(count, k, ring):
    return (count + ring - 1 - k) // ring


def run_groups(eng, count, unroll, stages, first=0):
    deepest = max(lag for lag, _ in stages)
    first = max(first, -(-(deepest + 4) // unroll))
    last = (count - 1) // unroll

    def at(j, u):
        for lag, work in stages:
            step = Step(j, unroll, u - lag)
            if step.fixed and not 0 <= step.lin() < count:
                continue
            work(step)

    for t in range(first * unroll):
        at(t // unroll, t % unroll)
    with eng.Fori(first, last) as j:
        for u in range(unroll):
            at(j, u)
    for t in range(last * unroll, count + deepest):
        at(t // unroll, t % unroll)


class Lone(Step):

    def slot(self, count=2):
        return 0


class Beside:

    def __init__(self, late, work):
        self.late, self.work = late, work


def run_beside(eng, count, stages):
    def placed(b):
        def stage(s):
            if s.off % 4 != b.late % 4:
                return
            m = Lone(s.j, 1, -(b.late // 4))
            if not m.fixed or m.lin() >= 0:
                b.work(m)
        return stage

    run_groups(eng, count, 4, [(0, placed(b)) if isinstance(b, Beside) else b for b in stages])
    rounds = -(-count // 4)
    rest = [(4 * m + b.late, i, b, m) for i, b in enumerate(stages) if isinstance(b, Beside)
            for m in range(rounds) if 4 * m + b.late >= count]
    for _, _, b, m in sorted(rest, key=lambda r: r[:2]):
        b.work(Lone(0, 1, m))


class Room:

    def __init__(self, nc, ctx, name):
        self.nc, self.ctx, self.name = nc, ctx, name
        self.counts = []
        self.passed = self.sem("passed")

    def hold(self, eng, sem, value):
        if isinstance(value, int):
            wait(eng, sem, value)
            return
        eng.wait_ge(sem, value)
        eng.sem_inc(self.passed, 1)

    def sb(self, name, shape, dt=F32):
        return self.ctx.enter_context(self.nc.sbuf_tensor(f"{self.name}_{name}", shape, dt))

    def two(self, name, shape, dt=F32, count=2):
        return [self.sb(f"{name}{i}", shape, dt) for i in range(count)]

    def bank(self, name):
        return self.ctx.enter_context(self.nc.psum_tensor(f"{self.name}_bank_{name}", [P, G], F32))

    def sem(self, name):
        self.counts.append(self.ctx.enter_context(self.nc.semaphore(f"{self.name}_{name}")))
        return self.counts[-1]

    def sem2(self, name, count=2):
        return [self.sem(f"{name}{i}") for i in range(count)]

    def swdge2(self, name, count=2):
        return [self.nc.alloc_semaphore(f"{self.name}_{name}{i}") for i in range(count)]

    def block(self):
        self.ctx.callback(self.clear)
        return self.ctx.enter_context(self.nc.Block())

    def clear(self):
        numbers = sorted(sem.num for sem in self.counts)
        start = 0
        for i, number in enumerate(numbers):
            if i + 1 == len(numbers) or numbers[i + 1] != number + 1:
                self.nc.gpsimd.sem_clear(range(numbers[start], number + 1))
                start = i + 1
        self.nc.all_engine_barrier()


def tile(buf, c):
    return buf[:, c * D:(c + 1) * D]


def tiles3(buf):
    return buf[:, :].rearrange("p (c d) -> p c d", c=TILES)


def cols_of(table, g, width):
    return table[:, bass.ds(g * width, width)]


def flat(along, g, what):
    return along[bass.ds(g, 1), what, :].rearrange("a g -> (a g)").partition_broadcast(P)


def edge_rows(table, g, base=0):
    return table[bass.ds(g * G + base, G), :].rearrange("(c p) d -> p c d", p=P)


def over_tiles(row):
    return row.unsqueeze(1).broadcast_to([P, TILES, D])


class Norm:

    def __init__(self, room, name, eps_col, ring=4):
        self.st = room.two(f"{name}_st", [P, 6 * TILES], count=ring)
        self.mv = room.two(f"{name}_mv", [P, 2 * TILES], count=ring)
        self.sd, self.rs, self.rm = (room.two(f"{name}_{k}", [P, TILES], count=ring) for k in ("sd", "rs", "rm"))
        self.st_done, self.settled, self.mv_done, self.sd_done, self.rs_done, self.rm_done = (
            room.sem(f"{name}_{k}") for k in ("st_done", "st_settled", "mv_done", "sd_done", "rs_done", "rm_done"))
        self.eps = eps_col

    def stats(self, v, s, rows, ready=None):
        k = s.slot(4)
        if ready is not None:
            v.wait_ge(ready, s.lin(1, 1))
        for c in range(TILES):
            ins = v.bn_stats(self.st[k][:, 6 * c:6 * c + 6], tile(rows, c))
        ins.then_inc(self.st_done, 1)

    def moments(self, v, s):
        k = s.slot(4)
        v.wait_ge(self.st_done, s.lin(1, 1))
        v.sem_inc(self.settled, 1)
        for c in range(TILES):
            ins = v.bn_aggr(self.mv[k][:, 2 * c:2 * c + 2], self.st[k][:, 6 * c:6 * c + 6])
        ins.then_inc(self.mv_done, 1)

    def root(self, a, s):
        k = s.slot(4)
        a.wait_ge(self.mv_done, s.lin(1, 1))
        a.activation(self.sd[k][:, :], self.mv[k][:, 1::2], ACT.Sqrt, bias=self.eps).then_inc(self.sd_done, 1)

    def invert(self, v, s):
        k = s.slot(4)
        v.wait_ge(self.sd_done, s.lin(1, 1))
        v.reciprocal(self.rs[k][:, :], self.sd[k][:, :]).then_inc(self.rs_done, 1)

    def masked(self, v, s, mask):
        k = s.slot(4)
        v.wait_ge(self.rs_done, s.lin(1, 1))
        v.tensor_tensor(self.rm[k][:, :], self.rs[k][:, :], mask, ALU.mult).then_inc(self.rm_done, 1)

    def offset(self, v, s):
        k = s.slot(4)
        v.wait_ge(self.rs_done, s.lin(1, 1))
        v.scalar_tensor_tensor(out=self.rm[k][:, :], in0=self.mv[k][:, 0::2], scalar=-1.0, in1=self.rs[k][:, :],
                               op0=ALU.mult, op1=ALU.mult).then_inc(self.rm_done, 1)

    def scale(self, v, s, rows, out, out_done, masked=False):
        k = s.slot(4)
        v.wait_ge(self.rm_done if masked else self.rs_done, s.lin(1, 1))
        factor = self.rm[k] if masked else self.rs[k]
        for c in range(TILES):
            ins = v.tensor_scalar(tile(out, c), tile(rows, c), self.mv[k][:, 2 * c:2 * c + 1],
                                  factor[:, c:c + 1], ALU.subtract, ALU.mult)
        ins.then_inc(out_done, 1)

    def scale_a(self, a, s, rows, out, out_done):
        k = s.slot(4)
        a.wait_ge(self.rm_done, s.lin(1, 1))
        for c in range(TILES):
            ins = a.activation(tile(out, c), tile(rows, c), ACT.Identity, bias=self.rm[k][:, c:c + 1],
                               scale=self.rs[k][:, c:c + 1])
        ins.then_inc(out_done, 1)


class Weights:

    def __init__(self, room):
        n = len(WEIGHTS)
        self.mats = room.sb("mats", [P, n * D])
        self.turned = room.sb("turned", [P, 5 * D])
        self.cols = room.sb("cols", [P, len(VECTORS)])
        self.rows = room.sb("rows", [P, len(VECTORS) * D])
        self.wcol = room.sb("wcol", [P, 1])
        self.ident = room.sb("ident", [P, P])
        self.center = room.sb("center", [P, P])
        self.heads = room.sb("heads", [P, P])
        self.mean_col = room.sb("mean_col", [P, 1])
        self.eps = room.sb("eps", [P, 1])
        self.eps2 = room.sb("eps2", [P, 1])
        self.u1c = room.sb("u1c", [P, D])
        self.g1c = room.sb("g1c", [P, D])
        self.u2c = room.sb("u2c", [P, D])
        self.g2c = room.sb("g2c", [P, D])
        self.c2c = room.sb("c2c", [P, D])
        self.gb2c = room.sb("gb2c", [P, D])
        self.negc2 = room.sb("negc2", [P, 1])
        self.neggb2 = room.sb("neggb2", [P, 1])
        self.c1b = room.sb("c1b", [P, 1])
        self.ones16 = room.sb("ones16", [P, P], BF16)
        self.gb1s = room.sb("gb1s", [P, D], BF16)
        self.c2s = room.sb("c2s", [P, D], BF16)

    def mat(self, name):
        i = WEIGHTS.index(name)
        return self.mats[:, i * D:(i + 1) * D]

    def t(self, i):
        return self.turned[:, i * D:(i + 1) * D]

    def col(self, name):
        i = VECTORS.index(name)
        return self.cols[:, i:i + 1]

    def row(self, name):
        i = VECTORS.index(name)
        return self.rows[:, i * D:(i + 1) * D]


def prepare_weights(nc, w, mats_in, vec_cols, vec_rows, wrow_in):
    with ExitStack() as ctx:
        room = Room(nc, ctx, "prep")
        ps_turn = [room.bank(f"ps_turn{i}") for i in range(2)]
        ps_mats = room.bank("ps_mats")
        ps_cols = room.bank("ps_cols")
        gw2 = room.sb("gw2", [P, D])
        gw2l = room.sb("gw2l", [P, D])
        gb2full = room.sb("gb2full", [P, D])
        sums = room.sb("sums", [P, 4])
        beta_b = room.sb("beta_b", [P, P])
        rest = room.sb("rest", [P, D])
        part = room.sb("part", [P, D], BF16)
        loaded = room.sem("loaded")
        const = room.sem("const")
        ident_ok = room.sem("ident_ok")
        turned = room.sem("turned")
        kept = room.sem("kept")
        v1 = room.sem("v1")
        prod = room.sem("prod")
        back = room.sem("back")
        block = room.block()

        @block.sync
        def _(sp):
            sp.dma_start(w.mats[:, :], mats_in).then_inc(loaded, 16)
            sp.dma_start(w.cols[:, :], vec_cols).then_inc(loaded, 16)
            sp.dma_start(w.rows[:, :], vec_rows.rearrange("k d -> (k d)").partition_broadcast(P)).then_inc(loaded, 16)
            sp.dma_start(w.wcol[:, :], wrow_in).then_inc(loaded, 16)

        @block.gpsimd
        def _(pool):
            nc.gpsimd.memset(w.ident[:, :], 0.0).then_inc(const, 1)
            nc.gpsimd.memset(w.center[:, :], -1.0 / P).then_inc(const, 1)
            nc.gpsimd.memset(w.heads[:, :], 0.25).then_inc(const, 1)
            nc.gpsimd.memset(w.mean_col[:, :], 1.0 / P).then_inc(const, 1)
            nc.gpsimd.memset(w.eps[:, :], EPS).then_inc(const, 1)
            nc.gpsimd.memset(w.eps2[:, :], EPS * EPS).then_inc(const, 1)
            pool.wait_ge(const, 6)
            nc.gpsimd.affine_select(out=w.ident[:, :], in_=w.ident[:, :], compare_op=ALU.not_equal, fill=1.0,
                                    base=0, pattern=[[-1, P]], channel_multiplier=1).then_inc(ident_ok, 1)
            nc.gpsimd.affine_select(out=w.center[:, :], in_=w.center[:, :], compare_op=ALU.not_equal,
                                    fill=1.0 - 1.0 / P, base=0, pattern=[[-1, P]], channel_multiplier=1).then_inc(ident_ok, 1)
            heads3 = w.heads[:, :].rearrange("p (h d) -> p h d", d=16)
            nc.gpsimd.affine_select(out=heads3, in_=heads3, compare_op=ALU.is_ge, fill=0.0, base=0,
                                    pattern=[[-16, 8], [0, 16]], channel_multiplier=1).then_inc(ident_ok, 1)
            pool.wait_ge(ident_ok, 3)
            nc.gpsimd.affine_select(out=heads3, in_=heads3, compare_op=ALU.is_ge, fill=0.0, base=15,
                                    pattern=[[16, 8], [0, 16]], channel_multiplier=-1).then_inc(ident_ok, 1)

        @block.tensor
        def _(pe):
            pe.wait_ge(ident_ok, 4)
            pe.wait_ge(loaded, 64)
            for i in range(5):
                ins = pe.transpose(ps_turn[i // 4][:, (i % 4) * D:(i % 4 + 1) * D], w.mats[:, i * D:(i + 1) * D], w.ident[:, :])
            ins.then_inc(turned, 1)
            pe.matmul(ps_mats[:, 0:D], w.center[:, :], w.mat("U1X"), start=True, stop=True)
            pe.matmul(ps_mats[:, D:2 * D], w.center[:, :], w.mat("G1"), start=True, stop=True)
            pe.wait_ge(v1, 1)
            pe.matmul(ps_mats[:, 2 * D:3 * D], w.center[:, :], gw2[:, :], start=True, stop=True)
            pe.wait_ge(v1, 2)
            pe.matmul(ps_mats[:, 3 * D:4 * D], beta_b[:, :], w.mat("G2"), start=True, stop=True)
            pe.matmul(ps_cols[:, 0:1], w.mat("U1A"), w.col("mb2"), start=True, stop=True).then_inc(prod, 1)
            pe.wait_ge(v1, 3)
            pe.transpose(ps_turn[0][:, 0:128], w.c2c[:, :], w.ident[:, :])
            pe.transpose(ps_turn[0][:, 128:256], w.gb2c[:, :], w.ident[:, :]).then_inc(back, 1)

        @block.vector
        def _(v):
            n = [0]

            def keep(ins):
                n[0] += 1
                ins.then_inc(kept, 1)
                v.wait_ge(kept, n[0])

            v.wait_ge(loaded, 64)
            v.tensor_scalar(gw2[:, :], w.mat("G2"), w.col("gamma"), None, ALU.mult).then_inc(v1, 1)
            v.wait_ge(const, 6)
            v.wait_ge(ident_ok, 4)
            keep(v.memset(beta_b[:, :], 0.0))
            v.tensor_scalar(beta_b[:, :], beta_b[:, :], w.col("beta"), None, ALU.add).then_inc(v1, 1)
            v.wait_ge(turned, 1)
            v.tensor_copy(w.turned[:, 0:4 * D], ps_turn[0][:, :])
            v.tensor_copy(w.turned[:, 4 * D:5 * D], ps_turn[1][:, 0:D])
            keep(v.reduce_sum(sums[:, 0:1], w.mat("U2"), mybir.AxisListType.X))
            keep(v.tensor_scalar(sums[:, 0:1], sums[:, 0:1], 1.0 / P, None, ALU.mult))
            v.tensor_scalar(w.u2c[:, :], w.mat("U2"), sums[:, 0:1], None, ALU.subtract)
            keep(v.reduce_sum(sums[:, 1:2], w.row("c2"), mybir.AxisListType.X))
            keep(v.tensor_scalar(sums[:, 1:2], sums[:, 1:2], 1.0 / P, None, ALU.mult))
            keep(v.tensor_scalar(w.c2c[:, :], w.row("c2"), sums[:, 1:2], None, ALU.subtract))
            v.wait_ge(prod, 1)
            v.tensor_copy(w.u1c[:, :], ps_mats[:, 0:D])
            v.tensor_copy(w.g1c[:, :], ps_mats[:, D:2 * D])
            keep(v.tensor_copy(gw2l[:, :], ps_mats[:, 2 * D:3 * D]))
            keep(v.reduce_sum(sums[:, 2:3], gw2l[:, :], mybir.AxisListType.X))
            keep(v.tensor_scalar(sums[:, 2:3], sums[:, 2:3], 1.0 / P, None, ALU.mult))
            v.tensor_scalar(w.g2c[:, :], gw2l[:, :], sums[:, 2:3], None, ALU.subtract)
            keep(v.tensor_tensor(gb2full[:, :], ps_mats[:, 3 * D:4 * D], w.row("gb2"), ALU.add))
            keep(v.reduce_sum(sums[:, 3:4], gb2full[:, :], mybir.AxisListType.X))
            keep(v.tensor_scalar(sums[:, 3:4], sums[:, 3:4], 1.0 / P, None, ALU.mult))
            v.tensor_scalar(w.gb2c[:, :], gb2full[:, :], sums[:, 3:4], None, ALU.subtract).then_inc(v1, 1)
            v.tensor_tensor(w.c1b[:, :], ps_cols[:, 0:1], w.col("c1"), ALU.add)
            v.wait_ge(back, 1)
            v.tensor_scalar(w.negc2[:, :], ps_turn[0][:, 0:1], -1.0, None, ALU.mult)
            keep(v.tensor_scalar(w.neggb2[:, :], ps_turn[0][:, 128:129], -1.0, None, ALU.mult))

            def split(row, parts):
                keep(v.memset(parts[:, :], 0.0))
                keep(v.tensor_copy(rest[:, :], row))
                for i in range(3):
                    keep(v.tensor_copy(part[:, :], rest[:, :]))
                    at = slice(32 * i, 32 * i + 1)
                    keep(v.tensor_copy(parts[at, :], part[at, :]))
                    keep(v.tensor_tensor(rest[:, :], rest[:, :], part[:, :], ALU.subtract))

            keep(v.memset(w.ones16[:, :], 1.0))
            split(w.c2c[:, :], w.c2s)
            split(w.row("gb1"), w.gb1s)


def prepare_edges(nc, w, ng, nodes, ints_in, ew_in, along, facts, slots):
    with ExitStack() as ctx:
        room = Room(nc, ctx, "edges")
        I = {k: room.sb(k, [ng, G], I32) for k in ("src", "dst", "dprev", "dnext")}
        f = {k: room.sb("f_" + k, [ng, G]) for k in ("dst", "dprev", "dnext", "last", "first", "w", "pos", "carry",
                                                      "degsum", "begin", "deg", "scat", "dstc", "src", "dinv", "pay")}
        al = room.sb("along", [ng, 4, G])
        ends = room.sb("ends", [ng, 4])
        erow = room.sb("erow", [1, 4, 64])
        crow = room.sb("crow", [1, 2, 64])
        ccol = room.sb("ccol", [ng, 2])
        rec = room.sb("rec", [P, ng, REC], I32)
        iota_id = room.sb("iota_id", [125, nodes // 125, 2], I32)
        ps_e = room.bank("ps_e")
        ps = [room.bank(f"ps{i}") for i in range(7)]
        loaded, kept, posed, ended, ends_back, carried, col_back, turned, evac, rooted, stored = (
            room.sem(x) for x in ("loaded", "kept", "posed", "ended", "ends_back", "carried", "col_back", "turned",
                                  "evac", "rooted", "stored"))
        ready = room.sem("ready")
        alongs = room.sem("alongs")
        rec_ok = room.sem("rec_ok")
        ids = room.sem("ids")
        TURN = [("src", SRC), ("dstc", DSTC), ("scat", SCAT), ("last", LAST), ("first", FIRST), ("dinv", DINV), ("w", WROW)]
        block = room.block()

        @block.sync
        def _(sp):
            for i, k in enumerate(("src", "dst", "dprev", "dnext")):
                sp.dma_start(I[k][:, :], ints_in[i]).then_inc(loaded, 16)
            sp.dma_start(f["w"][:, :], ew_in).then_inc(loaded, 16)
            sp.wait_ge(ids, 2)
            sp.dma_start(slots.rearrange("(a b) c -> a b c", a=125), iota_id[:, :, :]).then_inc(stored, 16)
            sp.wait_ge(alongs, 1)
            sp.dma_start(along, al[:, :, :]).then_inc(stored, 16)
            sp.wait_ge(rec_ok, 1)
            sp.dma_start(facts, rec[:, :, :]).then_inc(stored, 16)
            sp.wait_ge(stored, 48)

        @block.gpsimd
        def _(pool):
            nc.gpsimd.iota(iota_id[:, :, 1], pattern=[[1, nodes // 125]], base=0,
                           channel_multiplier=nodes // 125).then_inc(ids, 1)
            nc.gpsimd.memset(iota_id[:, :, 0], NO_ROW).then_inc(ids, 1)
            nc.gpsimd.iota(f["pos"][:, :], pattern=[[1, G]], base=0, channel_multiplier=G,
                           allow_small_or_imprecise_dtypes=True).then_inc(posed, 1)
            nc.gpsimd.iota(rec[:, :, PAY:PAY + 2 * TILES:2], pattern=[[G, ng], [P, TILES]], base=0,
                           channel_multiplier=1).then_inc(posed, 1)

        @block.vector
        def _(v):
            n = [0]

            def keep(ins):
                n[0] += 1
                ins.then_inc(kept, 1)
                v.wait_ge(kept, n[0])

            v.wait_ge(loaded, 80)
            v.tensor_copy(f["dst"][:, :], I["dst"][:, :])
            v.tensor_copy(f["src"][:, :], I["src"][:, :])
            v.tensor_copy(f["dprev"][:, :], I["dprev"][:, :])
            keep(v.tensor_copy(f["dnext"][:, :], I["dnext"][:, :]))
            v.tensor_tensor(al[:, KEEP_F, :], f["dst"][:, :], f["dprev"][:, :], ALU.is_equal)
            keep(v.tensor_tensor(al[:, KEEP_B, :], f["dst"][:, :], f["dnext"][:, :], ALU.is_equal))
            v.tensor_scalar(al[:, PEN_B, :], al[:, KEEP_B, :], BIG, BIG, ALU.mult, ALU.subtract)
            v.tensor_copy(al[:, W_F, :], f["w"][:, :]).then_inc(alongs, 1)
            v.tensor_scalar(f["last"][:, :], al[:, KEEP_B, :], -1.0, 1.0, ALU.mult, ALU.add)
            keep(v.tensor_scalar(f["first"][:, :], al[:, KEEP_F, :], -1.0, 1.0, ALU.mult, ALU.add))
            v.tensor_scalar(f["dstc"][:, :], f["dst"][:, :], float(nodes - 1), None, ALU.min)
            v.scalar_tensor_tensor(out=f["scat"][:, :], in0=al[:, KEEP_B, :], scalar=float(NO_ROW), in1=f["dst"][:, :],
                                   op0=ALU.mult, op1=ALU.add)
            v.wait_ge(posed, 1)
            keep(v.tensor_tensor(f["pos"][:, :], f["pos"][:, :], f["first"][:, :], ALU.mult))
            v.tensor_tensor_scan(f["degsum"][:, :], al[:, KEEP_F, :], f["w"][:, :], 0.0, ALU.mult, ALU.add)
            v.tensor_tensor_scan(f["begin"][:, :], al[:, KEEP_F, :], f["pos"][:, :], 0.0, ALU.mult, ALU.add)
            keep(v.memset(f["deg"][:, :], 0.0))
            keep(v.tensor_tensor_scan(f["carry"][:, :], al[:, KEEP_F, :], f["deg"][:, :], 1.0, ALU.mult, ALU.add))
            v.tensor_copy(ends[:, 0:1], f["carry"][:, G - 1:G])
            v.tensor_copy(ends[:, 1:2], f["degsum"][:, G - 1:G])
            v.tensor_copy(ends[:, 2:3], f["begin"][:, G - 1:G]).then_inc(ended, 1)
            v.wait_ge(ends_back, 1)
            keep(v.tensor_copy(erow[:, 0:3, 0:ng], ps_e[0:1, 0:3 * 64].rearrange("p (k n) -> p k n", k=3)[:, :, 0:ng]))
            v.tensor_tensor_scan(crow[:, 0, 1:ng + 1], erow[:, 0, 0:ng], erow[:, 1, 0:ng], 0.0, ALU.mult, ALU.add)
            keep(v.tensor_tensor_scan(crow[:, 1, 1:ng + 1], erow[:, 0, 0:ng], erow[:, 2, 0:ng], 0.0, ALU.mult, ALU.add))
            keep(v.memset(crow[:, :, 0:1], 0.0))
            v.sem_inc(carried, 1)
            v.wait_ge(col_back, 1)
            keep(v.tensor_copy(ccol[:, :], ps_e[0:ng, 256:258]))
            keep(v.scalar_tensor_tensor(out=f["deg"][:, :], in0=f["carry"][:, :], scalar=ccol[:, 0:1],
                                        in1=f["degsum"][:, :], op0=ALU.mult, op1=ALU.add))
            keep(v.scalar_tensor_tensor(out=f["pay"][:, :], in0=f["carry"][:, :], scalar=ccol[:, 1:2],
                                        in1=f["begin"][:, :], op0=ALU.mult, op1=ALU.add))
            v.tensor_scalar(f["pay"][:, :], f["pay"][:, :], float(nodes), None, ALU.add)
            keep(v.tensor_scalar(f["deg"][:, :], f["deg"][:, :], 1.0, None, ALU.add))
            v.tensor_scalar(f["carry"][:, :], f["deg"][:, :], 0.0, None, ALU.is_gt)
            keep(v.tensor_scalar(f["deg"][:, :], f["deg"][:, :], 1e-30, None, ALU.max))
            v.sem_inc(ready, 1)
            v.wait_ge(rooted, 1)
            keep(v.reciprocal(f["dinv"][:, :], f["begin"][:, :]))
            keep(v.tensor_tensor(f["dinv"][:, :], f["dinv"][:, :], f["carry"][:, :], ALU.mult))
            v.sem_inc(ready, 1)
            fl = rec[:, :, :].bitcast(F32)
            v.wait_ge(turned, 1)
            v.wait_ge(posed, 2)
            for i, (k, at) in enumerate(TURN):
                out = fl if at >= LAST else rec
                v.tensor_copy(out[:, :, at:at + TILES], ps[i][:, 0:TILES * ng].rearrange("p (c g) -> p g c", c=TILES))
            v.tensor_copy(rec[:, :, PAY + 1:PAY + 2 * TILES:2],
                          ps[0][:, TILES * ng:2 * TILES * ng].rearrange("p (c g) -> p g c", c=TILES)).then_inc(rec_ok, 1)

        @block.scalar
        def _(a):
            a.wait_ge(ready, 1)
            a.activation(f["begin"][:, :], f["deg"][:, :], ACT.Sqrt).then_inc(rooted, 1)

        @block.tensor
        def _(pe):
            pe.wait_ge(ended, 1)
            for k in range(3):
                ins = pe.transpose(ps_e[0:1, 64 * k:64 * k + ng], ends[:, k:k + 1], w.ident[0:ng, 0:ng])
            ins.then_inc(ends_back, 1)
            pe.wait_ge(carried, 1)
            for k in range(2):
                ins = pe.transpose(ps_e[0:ng, 256 + k:257 + k], crow[:, k, 0:ng], w.ident[0:1, 0:1])
            ins.then_inc(col_back, 1)
            pe.wait_ge(ready, 2)
            for i, (k, at) in enumerate(TURN):
                for c in range(TILES):
                    pe.transpose(ps[i][:, c * ng:(c + 1) * ng], f[k][:, c * P:(c + 1) * P], w.ident[0:ng, 0:ng])
            for c in range(TILES):
                ins = pe.transpose(ps[0][:, (TILES + c) * ng:(TILES + c + 1) * ng], f["pay"][:, c * P:(c + 1) * P],
                                   w.ident[0:ng, 0:ng])
            ins.then_inc(turned, 1)


def dense_pass(nc, w, ng, nodes, x, out, t2, facts, along, slots, mapped, t1, s1):
    count = -(-nodes // G)
    rounds = -(-count // 4)
    assert rounds == ng
    half = -(-(count // 2) // 4) * 4
    with ExitStack() as ctx:
        room = Room(nc, ctx, "dense")
        xin, u, z, x2, x3b, z4, o = (room.two(k, [P, G], count=4) for k in "xin u z x2 x3b z4 o".split())
        x1T, rT, x3T, hT, hsq = (room.two(k, [P, G]) for k in "x1T rT x3T hT hsq".split())
        junk2 = room.sb("junk2", [P, G])
        junk4 = room.sb("junk4", [P, G])
        st = room.two("st", [P, 6 * TILES])
        mv = room.two("mv", [P, 2 * TILES])
        sd23, hst = (room.two(k, [P, 2 * TILES]) for k in "sd23 hst".split())
        rs23 = room.two("rs23", [P, 2 * TILES], count=4)
        rs4 = room.two("rs4", [P, TILES], count=4)
        sd1, rs1, sq2, hm2, hvar, sdh, rsh, sq4, sd4 = (
            room.two(k, [P, TILES]) for k in "sd1 rs1 sq2 hm2 hvar sdh rsh sq4 sd4".split())
        rec = room.two("rec", [P, REC], I32)
        got = room.two("got", [P, 2 * TILES], I32)
        ps_t1, ps_t3, ps_u, ps_w, ps_z, ps_h = (room.bank(k) for k in ("t1", "t3", "u", "w", "z", "h"))
        ps_p = [room.bank("p0"), room.bank("p1")]
        names = ("y st settled mv sd1 rs1 u t1 x1T ua rT zp z sq2 sd23 rs23 x2 x3b t3 x3T wa hT hsq pp hst hm2 "
                 "hvar0 hvar sdh rsh z4 sq4 sd4 rs4").split()
        e_rec = room.sb("e_rec", [P, REC], I32)
        e_mask = room.sb("e_mask", [P, TILES], I32)
        e_keep, e_xs, e_xd, e_ys, e_yd, e_hT, e_x1, e_x1s = (
            room.sb("e_" + k, [P, G]) for k in "keep xs xd ys yd hT x1 x1s".split())
        e_state = room.sb("e_state", [P, 1])
        e_nd = Norm(room, "e_nd", w.eps[:, :], ring=1)
        e_ns = Norm(room, "e_ns", w.eps[:, :], ring=1)
        edge = {k: room.sem("e_" + k) for k in
                "rec_in keep_in mask_in turn scan state wsum ys yd ydb x1 x1s x1_out x1s_out".split()}
        e_xs_in, e_xd_in = room.swdge2("e_x_in")
        done = {k: room.sem(k + "_done") for k in names}
        o_done = room.sem2("o_done", 4)
        x_in, x2_out, o_out = room.sem2("x_in", 4), room.sem2("x2_out", 4), room.sem2("o_out", 4)
        rec_in, put, found, kept = (room.swdge2(k) for k in ("rec_in", "put", "found", "kept"))

        def rows(table, s):
            at = min(s.lin(G), nodes - G) if s.fixed else s.lin(G)
            return table[bass.ds(at, G), :].rearrange("(p c) d -> p (c d)", c=TILES)

        def each_tile(factors):
            return factors.unsqueeze(2).broadcast_to([P, TILES, D])

        def scale4(eng, s):
            k4 = s.slot(4)
            eng.wait_ge(done["rs4"], s.lin(1, 1))
            wait(eng, o_out[k4], s.lin(16, 0, div=4))
            eng.tensor_tensor(tiles3(o[k4]), tiles3(z4[k4]), each_tile(rs4[k4][:, :]), ALU.mult).then_inc(o_done[k4], 1)

        block = room.block()

        @block.sync
        def _(sp):
            def load(s):
                k = s.slot(4)
                room.hold(sp, done["u"], s.lin(1, -3))
                sp.dma_start(xin[k][:, :], rows(x, s)).then_inc(x_in[k], 16)

            def store(s, table, buf, written, count_then, landed):
                k = s.slot(4)
                if s.fixed and s.lin() == count - 1:
                    sp.wait_ge(landed[(count - 2) % 4], 16 * ((count - 2) // 4 + 1))
                room.hold(sp, written, count_then)
                sp.dma_start(rows(table, s), buf[k][:, :]).then_inc(landed[k], 16)

            def load_edges(m):
                room.hold(sp, e_xd_in, m.lin(64))
                sp.dma_start(e_rec[:, :], cols_of(facts, m.lin(), REC)).then_inc(edge["rec_in"], 16)

            def load_keep(m):
                room.hold(sp, edge["scan"], m.lin())
                sp.dma_start(e_keep[:, :], flat(along, m.lin(), KEEP_F)).then_inc(edge["keep_in"], 16)

            def load_mask(m):
                room.hold(sp, edge["x1"], m.lin())
                sp.dma_start(e_mask[:, :], facts[:, bass.ds(m.lin(REC, LAST), TILES)]).then_inc(edge["mask_in"], 16)

            def store_src(m):
                room.hold(sp, edge["x1s"], m.lin(1, 1))
                sp.dma_start(edge_rows(s1, m.lin()), tiles3(e_x1s)).then_inc(edge["x1s_out"], 16)

            def store_dst(m):
                room.hold(sp, edge["x1"], m.lin(1, 1))
                sp.dma_start(edge_rows(t1, m.lin()), tiles3(e_x1)).then_inc(edge["x1_out"], 16)

            run_beside(sp, count, [(0, load), (8, lambda s: store(s, t2, x2, done["x2"], s.lin(1, 1), x2_out)),
                                   (13, lambda s: store(s, out, o, o_done[s.slot(4)], s.lin(1, 1, div=4), o_out)),
                                   Beside(0, load_edges), Beside(1, load_keep), Beside(5, load_mask),
                                   Beside(9, store_src), Beside(10, store_dst)])
            sp.wait_ge(edge["x1s_out"], 16 * ng)
            sp.wait_ge(edge["x1_out"], 16 * ng)
            for k in range(4):
                sp.wait_ge(x2_out[k], 16 * uses(count, k, 4))
                sp.wait_ge(o_out[k], 16 * uses(count, k, 4))

        @block.vector
        def _(v):
            def stats1(s):
                k = s.slot()
                v.wait_ge(done["y"], s.lin(1, 1))
                for c in range(TILES):
                    ins = v.bn_stats(st[k][:, 6 * c:6 * c + 6], tile(xin[s.slot(4)], c))
                ins.then_inc(done["st"], 1)

            def moments1(s):
                k = s.slot()
                v.wait_ge(done["st"], s.lin(1, 1))
                v.sem_inc(done["settled"], 1)
                for c in range(TILES):
                    ins = v.bn_aggr(mv[k][:, 2 * c:2 * c + 2], st[k][:, 6 * c:6 * c + 6])
                ins.then_inc(done["mv"], 1)

            def invert1(s):
                k = s.slot()
                v.wait_ge(done["sd1"], s.lin(1, 1))
                v.reciprocal(rs1[k][:, :], sd1[k][:, :]).then_inc(done["rs1"], 1)

            def scale1(s):
                k, k4 = s.slot(), s.slot(4)
                v.wait_ge(done["rs1"], s.lin(1, 1))
                for c in range(TILES):
                    ins = v.tensor_scalar(tile(u[k4], c), tile(xin[k4], c), mv[k][:, 2 * c:2 * c + 1],
                                          rs1[k][:, c:c + 1], ALU.subtract, ALU.mult)
                ins.then_inc(done["u"], 1)

            def add_mlp(s):
                k4 = s.slot(4)
                v.wait_ge(done["zp"], s.lin(1, 1))
                wait(v, done["x2"], s.lin(1, -3))
                v.tensor_tensor(z[k4][:, :], ps_z[:, :], u[k4][:, :], ALU.add).then_inc(done["z"], 1)

            def invert23(s):
                k = s.slot()
                v.wait_ge(done["sd23"], s.lin(1, 1))
                wait(v, done["x2"], s.lin(1, -3))
                v.reciprocal(rs23[s.slot(4)][:, :], sd23[k][:, :]).then_inc(done["rs23"], 1)

            def scale3(s):
                k, k4 = s.slot(), s.slot(4)
                v.wait_ge(done["rs23"], s.lin(1, 1))
                for c in range(TILES):
                    ins = v.scalar_tensor_tensor(out=tile(x3b[k4], c), in0=tile(z[k4], c),
                                                 scalar=rs23[k4][:, TILES + c:TILES + c + 1], in1=w.gb2c[:, :],
                                                 op0=ALU.mult, op1=ALU.add)
                ins.then_inc(done["x3b"], 1)

            def moments_h(s):
                k = s.slot()
                v.wait_ge(done["pp"], s.lin(1, 1))
                v.tensor_copy(hst[k][:, :], ps_h[:, 0:2 * TILES]).then_inc(done["hst"], 1)

            def square_h(s):
                k = s.slot()
                v.wait_ge(done["hst"], s.lin(1, 1))
                v.tensor_tensor(hm2[k][:, :], hst[k][:, TILES:2 * TILES], hst[k][:, TILES:2 * TILES], ALU.mult).then_inc(done["hm2"], 1)

            def var_h(s):
                k = s.slot()
                v.wait_ge(done["hm2"], s.lin(1, 1))
                v.tensor_tensor(hvar[k][:, :], hst[k][:, 0:TILES], hm2[k][:, :], ALU.subtract).then_inc(done["hvar0"], 1)

            def clamp_h(s):
                k = s.slot()
                v.wait_ge(done["hvar0"], s.lin(1, 1))
                v.tensor_scalar(hvar[k][:, :], hvar[k][:, :], 0.0, None, ALU.max).then_inc(done["hvar"], 1)

            def invert_h(s):
                k = s.slot()
                v.wait_ge(done["sdh"], s.lin(1, 1))
                v.reciprocal(rsh[k][:, :], sdh[k][:, :]).then_inc(done["rsh"], 1)

            def add_gcn(s):
                k, k4 = s.slot(), s.slot(4)
                v.wait_ge(done["rsh"], s.lin(1, 1))
                wait(v, o_done[s.slot(4)], s.lin(1, 0, div=4))
                for c in range(TILES):
                    ins = v.scalar_tensor_tensor(out=tile(z4[k4], c), in0=tile(ps_p[k], c), scalar=rsh[k][:, c:c + 1],
                                                 in1=tile(x3b[k4], c), op0=ALU.mult, op1=ALU.add)
                ins.then_inc(done["z4"], 1)

            def invert4(s):
                k = s.slot()
                v.wait_ge(done["sd4"], s.lin(1, 1))
                wait(v, o_done[s.slot(4)], s.lin(1, 0, div=4))
                v.reciprocal(rs4[s.slot(4)][:, :], sd4[k][:, :]).then_inc(done["rs4"], 1)

            def edge_scan(m):
                v.wait_ge(edge["keep_in"], m.lin(16, 16))
                v.wait_ge(edge["turn"], m.lin(1, 1))
                wait(v, edge["wsum"], m.lin())
                wait(v, edge["state"], m.lin())
                first = m.fixed and m.lin() == 0
                v.tensor_tensor_scan(e_hT[:, :], e_keep[:, :], ps_t1[:, :], 0.0 if first else e_state[:, :],
                                     ALU.mult, ALU.add).then_inc(edge["scan"], 1)

            def edge_state(m):
                v.wait_ge(edge["scan"], m.lin(1, 1))
                v.tensor_copy(e_state[:, :], e_hT[:, G - 1:G]).then_inc(edge["state"], 1)

            def edge_src_add(m):
                v.wait_ge(e_xs_in, m.lin(64, 64))
                wait(v, edge["x1s"], m.lin())
                v.tensor_tensor(tiles3(e_ys), tiles3(e_xs), over_tiles(w.row("b0")), ALU.add).then_inc(edge["ys"], 1)

            def edge_dst_add(m):
                v.wait_ge(e_xd_in, m.lin(64, 64))
                v.wait_ge(edge["wsum"], m.lin(1, 1))
                v.tensor_tensor(e_yd[:, :], ps_t3[:, :], e_xd[:, :], ALU.add).then_inc(edge["yd"], 1)

            def edge_dst_bias(m):
                v.wait_ge(edge["yd"], m.lin(1, 1))
                v.tensor_tensor(tiles3(e_yd), tiles3(e_yd), over_tiles(w.row("b0")), ALU.add).then_inc(edge["ydb"], 1)

            def edge_mask(m):
                v.wait_ge(edge["mask_in"], m.lin(16, 16))
                e_nd.masked(v, m, e_mask[:, :].bitcast(F32))

            def edge_dst_out(m):
                wait(v, edge["x1_out"], m.lin(16))
                e_nd.scale(v, m, e_yd, e_x1, edge["x1"], masked=True)

            def scale4_v(s):
                if s.slot(4) == 1:
                    scale4(v, s)

            run_beside(v, count, [
                (8, moments_h), (5, invert23), (8, square_h), Beside(6, lambda m: e_nd.invert(v, m)),
                (5, scale3), (8, var_h), Beside(6, edge_mask), (1, invert1), (8, clamp_h), Beside(4, edge_dst_bias),
                (1, scale1), (0, stats1), (11, scale4_v), (10, invert4), Beside(5, lambda m: e_ns.invert(v, m)), (3, add_mlp), (0, moments1),
                Beside(4, lambda m: e_nd.stats(v, m, e_yd, edge["ydb"])), Beside(5, lambda m: e_ns.offset(v, m)),
                Beside(6, edge_dst_out), (8, invert_h), (8, add_gcn), Beside(4, lambda m: e_nd.moments(v, m)),
                Beside(2, edge_src_add), Beside(2, edge_scan), Beside(3, edge_state),
                Beside(3, lambda m: e_ns.stats(v, m, e_ys, edge["ys"])), Beside(3, edge_dst_add),
                Beside(3, lambda m: e_ns.moments(v, m))])

        @block.scalar
        def _(a):
            def root1(s):
                k = s.slot()
                a.wait_ge(done["mv"], s.lin(1, 1))
                a.activation(sd1[k][:, :], mv[k][:, 1::2], ACT.Sqrt, bias=w.eps[:, :]).then_inc(done["sd1"], 1)

            def mlp_in(s):
                k = s.slot()
                a.wait_ge(done["t1"], s.lin(1, 1))
                a.copy(x1T[k][:, :], ps_t1[:, :]).then_inc(done["x1T"], 1)

            def mlp_mid(s):
                k = s.slot()
                a.wait_ge(done["ua"], s.lin(1, 1))
                a.activation(rT[k][:, :], ps_u[:, :], ACT.Relu, bias=w.col("c1")).then_inc(done["rT"], 1)

            def squares2(s):
                k, k4 = s.slot(), s.slot(4)
                a.wait_ge(done["z"], s.lin(1, 1))
                for c in range(TILES):
                    ins = a.activation(tile(junk2, c), tile(z[k4], c), ACT.Square, accum_out=sq2[k][:, c:c + 1])
                ins.then_inc(done["sq2"], 1)

            def root23(s):
                k = s.slot()
                a.wait_ge(done["sq2"], s.lin(1, 1))
                a.activation(sd23[k][:, 0:TILES], sq2[k][:, :], ACT.Sqrt, bias=w.eps[:, :], scale=1.0 / D)
                a.activation(sd23[k][:, TILES:2 * TILES], sq2[k][:, :], ACT.Sqrt, bias=w.eps2[:, :],
                             scale=(1.0 + EPS) / D).then_inc(done["sd23"], 1)

            def gcn_in(s):
                k = s.slot()
                a.wait_ge(done["t3"], s.lin(1, 1))
                a.activation(x3T[k][:, :], ps_t3[:, :], ACT.Identity, bias=w.neggb2[:, :]).then_inc(done["x3T"], 1)

            def gcn_mid(s):
                k = s.slot()
                a.wait_ge(done["wa"], s.lin(1, 1))
                wait(a, done["pp"], s.lin(1, -1))
                a.activation(hT[k][:, :], ps_w[:, :], ACT.Relu, bias=w.col("gb1")).then_inc(done["hT"], 1)

            def square_h(s):
                k = s.slot()
                a.wait_ge(done["hT"], s.lin(1, 1))
                a.activation(hsq[k][:, :], hT[k][:, :], ACT.Square).then_inc(done["hsq"], 1)

            def root_h(s):
                k = s.slot()
                a.wait_ge(done["hvar"], s.lin(1, 1))
                a.activation(sdh[k][:, :], hvar[k][:, :], ACT.Sqrt, bias=w.eps[:, :]).then_inc(done["sdh"], 1)

            def squares4(s):
                k, k4 = s.slot(), s.slot(4)
                a.wait_ge(done["z4"], s.lin(1, 1))
                for c in range(TILES):
                    ins = a.activation(tile(junk4, c), tile(z4[k4], c), ACT.Square, accum_out=sq4[k][:, c:c + 1])
                ins.then_inc(done["sq4"], 1)

            def root4(s):
                k = s.slot()
                a.wait_ge(done["sq4"], s.lin(1, 1))
                a.activation(sd4[k][:, :], sq4[k][:, :], ACT.Sqrt, bias=w.eps[:, :], scale=1.0 / D).then_inc(done["sd4"], 1)

            def scale4_a(s):
                k4 = s.slot(4)
                if k4 == 3:
                    a.wait_ge(done["rs4"], s.lin(1, 1))
                    wait(a, o_out[k4], s.lin(16, 0, div=4))
                    for c in range(TILES):
                        ins = a.activation(tile(o[k4], c), tile(z4[k4], c), ACT.Copy, scale=rs4[k4][:, c:c + 1])
                    ins.then_inc(o_done[k4], 1)

            def edge_src_out(m):
                wait(a, edge["x1s_out"], m.lin(16))
                e_ns.scale_a(a, m, e_ys, e_x1s, edge["x1s"])

            run_beside(a, count, [(6, gcn_in), (2, mlp_in), (11, scale4_a), (4, squares2), (8, root_h), (4, root23), (9, squares4),
                                  (2, mlp_mid), (9, root4), (6, gcn_mid), (0, root1), (6, square_h),
                                  Beside(4, lambda m: e_ns.root(a, m)), Beside(5, lambda m: e_nd.root(a, m)),
                                  Beside(5, edge_src_out)])

        @block.tensor
        def _(pe):
            def turn1(s):
                pe.wait_ge(done["u"], s.lin(1, 1))
                wait(pe, done["x1T"], s.lin())
                if s.off % 4 == 1:
                    pe.wait_ge(edge["scan"], s.lin(1, 1, div=4))
                for c in range(TILES):
                    ins = pe.transpose(tile(ps_t1, c), tile(u[s.slot(4)], c), w.ident[:, :])
                ins.then_inc(done["t1"], 1)

            def mlp1(s):
                k = s.slot()
                pe.wait_ge(done["x1T"], s.lin(1, 1))
                wait(pe, done["rT"], s.lin())
                pe.matmul(ps_u[:, :], w.u1c[:, :], x1T[k][:, :], start=True, stop=True).then_inc(done["ua"], 1)

            def mlp2(s):
                k = s.slot()
                pe.wait_ge(done["rT"], s.lin(1, 1))
                wait(pe, done["z"], s.lin())
                for c in range(TILES):
                    pe.matmul(tile(ps_z, c), w.ones16[:, :], w.c2s[:, :], start=True, stop=False)
                    ins = pe.matmul(tile(ps_z, c), tile(rT[k], c), w.u2c[:, :], start=False, stop=True)
                ins.then_inc(done["zp"], 1)

            def turn3(s):
                pe.wait_ge(done["x3b"], s.lin(1, 1))
                wait(pe, done["x3T"], s.lin())
                if s.fixed and s.lin() == 0:
                    pe.wait_ge(edge["yd"], 1)
                if s.off % 4 == 2 and not (s.fixed and s.lin(1, 2, div=4) > ng):
                    pe.wait_ge(edge["yd"], s.lin(1, 2, div=4))
                for c in range(TILES):
                    ins = pe.transpose(tile(ps_t3, c), tile(x3b[s.slot(4)], c), w.ident[:, :])
                ins.then_inc(done["t3"], 1)

            def gcn1(s):
                k = s.slot()
                pe.wait_ge(done["x3T"], s.lin(1, 1))
                wait(pe, done["hT"], s.lin())
                pe.matmul(ps_w[:, :], w.g1c[:, :], x3T[k][:, :], start=True, stop=True).then_inc(done["wa"], 1)

            def gcn2(s):
                k = s.slot()
                pe.wait_ge(done["hT"], s.lin(1, 1))
                wait(pe, done["z4"], s.lin(1, -1))
                for c in range(TILES):
                    pe.matmul(tile(ps_p[k], c), tile(hT[k], c), w.g2c[:, :], start=True, stop=True)
                wait(pe, done["hst"], s.lin())
                for c in range(TILES):
                    pe.matmul(ps_h[:, TILES + c:TILES + c + 1], tile(hT[k], c), w.mean_col[:, :], start=True, stop=True)
                pe.wait_ge(done["hsq"], s.lin(1, 1))
                for c in range(TILES):
                    ins = pe.matmul(ps_h[:, c:c + 1], tile(hsq[k], c), w.mean_col[:, :], start=True, stop=True)
                ins.then_inc(done["pp"], 1)

            def edge_turn(m):
                pe.wait_ge(e_xs_in, m.lin(64, 64))
                wait(pe, done["x1T"], m.lin(4, 1))
                for c in range(TILES):
                    ins = pe.transpose(tile(ps_t1, c), tile(e_xs, c), w.ident[:, :])
                ins.then_inc(edge["turn"], 1)

            def edge_product(m):
                pe.wait_ge(edge["scan"], m.lin(1, 1))
                wait(pe, done["x3T"], m.lin(4, -2))
                for c in range(TILES):
                    ins = pe.matmul(tile(ps_t3, c), tile(e_hT, c), w.t(0), start=True, stop=True)
                ins.then_inc(edge["wsum"], 1)

            run_beside(pe, count, [(6, turn3), (2, turn1), (3, mlp2), (2, mlp1), Beside(2, edge_turn), (7, gcn2),
                                   Beside(3, edge_product), (6, gcn1)])

        @block.gpsimd
        def _(pool):
            top = pool.to_reg(nodes - 1)

            def add_b0(s):
                k4 = s.slot(4)
                pool.wait_ge(x_in[k4], s.lin(16, 16, div=4))
                pool.tensor_tensor(tiles3(xin[k4]), tiles3(xin[k4]), over_tiles(w.row("b0")), ALU.add).then_inc(done["y"], 1)

            def scale2(s):
                k4 = s.slot(4)
                pool.wait_ge(done["rs23"], s.lin(1, 1))
                wait(pool, x2_out[k4], s.lin(16, 0, div=4))
                pool.tensor_tensor(tiles3(x2[k4]), tiles3(z[k4]), each_tile(rs23[k4][:, 0:TILES]), ALU.mult).then_inc(done["x2"], 1)

            def scale4_pool(s):
                if s.slot() == 0:
                    scale4(pool, s)

            works = [(X2_LAG, scale2), (O_LAG, scale4_pool), (0, add_b0)]

            def gather_edges(m, part):
                if part == 0:
                    room.hold(pool, edge["rec_in"], m.lin(16, 16))
                    room.hold(pool, edge["turn"], m.lin())
                    room.hold(pool, edge["ys"], m.lin())
                if part == 2:
                    room.hold(pool, edge["yd"], m.lin())
                buf, at, arrived = ((e_xs, SRC, e_xs_in), (e_xd, DSTC, e_xd_in))[part // 2]
                for c in range(2 * (part % 2), 2 * (part % 2) + 2):
                    pool.indirect_dma_start(tile(buf, c), None, x,
                                            bass.IndirectOffsetOnAxis(e_rec[:, at + c:at + c + 1], 0),
                                            bounds_check=top, oob_is_err=False).then_inc(arrived, 16)

            def put_load(s):
                k = s.slot()
                room.hold(pool, put[k], s.lin(16 * TILES, 0, div=2))
                pool.dma_start(rec[k][:, :], cols_of(facts, s.lin(), REC)).then_inc(rec_in[k], 16)

            def put_slots(s):
                k = s.slot()
                room.hold(pool, rec_in[k], s.lin(16, 16, div=2))
                for c in range(TILES):
                    pool.indirect_dma_start(slots, bass.IndirectOffsetOnAxis(rec[k][:, SCAT + c:SCAT + c + 1], 0),
                                            rec[k][:, PAY + 2 * c:PAY + 2 * c + 2], None, bounds_check=top,
                                            oob_is_err=False).then_inc(put[k], 16)

            def find_load(s):
                k = s.slot()
                room.hold(pool, found[k], s.lin(16 * TILES, 0, div=2))
                pool.dma_start(rec[k][:, :], cols_of(facts, s.lin(), REC)).then_inc(rec_in[k], 16)

            def find_slots(s):
                k = s.slot()
                room.hold(pool, kept[k], s.lin(16, 0, div=2))
                room.hold(pool, rec_in[k], s.lin(16, 16 * (uses(ng, k, 2) + 1), div=2))
                for c in range(TILES):
                    pool.indirect_dma_start(got[k][:, 2 * c:2 * c + 2], None, slots,
                                            bass.IndirectOffsetOnAxis(rec[k][:, SRC + c:SRC + c + 1], 0),
                                            bounds_check=top, oob_is_err=False).then_inc(found[k], 16)

            def keep_slots(s):
                k = s.slot()
                room.hold(pool, found[k], s.lin(16 * TILES, 16 * TILES, div=2))
                pool.dma_start(cols_of(mapped, s.lin(), 2 * TILES),
                               got[k][:, :]).then_inc(kept[k], 16)

            def paced(base, groups, loops, stages):
                def dense_time(t):
                    for lag, work in works:
                        if 0 <= t - lag < count:
                            work(Step(0, 4, t - lag))
                    if t < 4 * ng:
                        gather_edges(Lone(0, 1, t // 4), t % 4)

                def dense_at(s, part):
                    if s.fixed:
                        if 2 * s.lin() + part < groups:
                            dense_time(2 * s.lin() + part + base)
                        return
                    for lag, work in works:
                        work(Step(s.j, 4, 2 * s.off + part + base - lag))
                    gather_edges(Lone(s.j, 1, base // 4), 2 * s.off + part)

                run_groups(pool, loops, 2, [(0, lambda s: dense_at(s, 0))] + stages + [(0, lambda s: dense_at(s, 1))],
                           first=2 + max(lag for lag, _ in works) // 4)
                for t in range(base + 2 * loops, base + groups):
                    dense_time(t)

            paced(0, half, ng, [(1, put_slots), (0, put_load)])
            for k in range(2):
                pool.wait_ge(put[k], 16 * TILES * uses(ng, k, 2))
            paced(half, count + O_LAG - half, ng, [(2, keep_slots), (1, find_slots), (0, find_load)])
            for k in range(2):
                pool.wait_ge(kept[k], 16 * uses(ng, k, 2))


def max_layer(nc, w, ng, nodes, facts, along, mapped, t1, s1, t2):
    rows_all = ng * G
    with ExitStack() as ctx:
        room = Room(nc, ctx, "max")
        mask = room.two("mask", [P, TILES], I32, count=4)
        mi = room.two("mi", [P, 2 * TILES], I32, count=4)
        flags = room.two("flags", [P, 2, G], count=4)
        wr = room.two("wr", [P, G], count=4)
        xs, xd, xdT, ag, x2 = (room.two(k, [P, G], count=4) for k in "xs xd xdT ag x2".split())
        xsT, pre, hT, rT, zT = (room.two(k, [P, G]) for k in "xsT pre hT rT zT".split())
        ps_d, ps_s, ps_h, ps_m, ps_r, ps_u = (room.bank(k) for k in "dshmru")
        ps_z = [room.bank("z0"), room.bank("z1")]
        nz = Norm(room, "nz", w.eps[:, :])
        done = {k: room.sem(k + "_done") for k in "turnd turns xsT spread ha pre hT ma max ra rT ua zT turnz x2".split()}
        mask_in, mi_in, flags_in, wr_in, xd_in, xs_in, x2_out = (
            room.sem2(k, 4) for k in ("mask_in", "mi_in", "flags_in", "wr_in", "xd_in", "xs_in", "x2_out"))
        over_in = room.swdge2("over_in", 4)
        block = room.block()

        def group(s):
            return (ng - 1) - s.lin() if s.fixed else s.lin(-1, ng - 1)

        @block.sync
        def _(sp):
            def load(s):
                k = s.slot(4)
                g = group(s)
                room.hold(sp, done["turns"], s.lin(1, -3))
                sp.dma_start(mi[k][:, :], cols_of(mapped, g, 2 * TILES)).then_inc(mi_in[k], 16)
                sp.dma_start(tiles3(xs[k]), edge_rows(s1, g)).then_inc(xs_in[k], 16)
                room.hold(sp, done["turnd"], s.lin(1, -3))
                sp.dma_start(tiles3(xd[k]), edge_rows(t1, g)).then_inc(xd_in[k], 16)
                room.hold(sp, done["pre"], s.lin(1, -3))
                sp.dma_start(wr[k][:, :], flat(along, g, W_F)).then_inc(wr_in[k], 16)
                room.hold(sp, done["max"], s.lin(1, -3))
                sp.dma_start(flags[k][:, :, :], along[bass.ds(g, 1), PEN_B:KEEP_B + 1, :]
                             .rearrange("a k g -> (a k) g").partition_broadcast(P)).then_inc(flags_in[k], 16)

            def load_mask(s):
                k = s.slot(4)
                room.hold(sp, done["x2"], s.lin(1, -3))
                at = group(s) * REC + FIRST
                sp.dma_start(mask[k][:, :], facts[:, bass.ds(at, TILES)]).then_inc(mask_in[k], 16)

            def store(s):
                k = s.slot(4)
                room.hold(sp, done["x2"], s.lin(1, 1))
                sp.dma_start(edge_rows(t2, group(s), nodes), tiles3(x2[k])).then_inc(x2_out[k], 16)

            run_groups(sp, ng, 4, [(0, load), (4, load_mask), (8, store)])
            for k in range(4):
                sp.wait_ge(x2_out[k], 16 * uses(ng, k, 4))

        @block.gpsimd
        def _(pool):
            top = pool.to_reg(rows_all - 1)

            def overlay(s):
                k = s.slot(4)
                room.hold(pool, xs_in[k], s.lin(16, 16, div=4))
                room.hold(pool, mi_in[k], s.lin(16, 16, div=4))
                for c in range(TILES):
                    pool.indirect_dma_start(tile(xs[k], c), None, t1,
                                            bass.IndirectOffsetOnAxis(mi[k][:, 2 * c:2 * c + 1], 0),
                                            bounds_check=top, oob_is_err=False).then_inc(over_in[k], 16)

            run_groups(pool, ng, 4, [(0, overlay)])

        @block.tensor
        def _(pe):
            def turns(s):
                k4 = s.slot(4)
                pe.wait_ge(xd_in[k4], s.lin(16, 16, div=4))
                wait(pe, done["spread"], s.lin())
                for c in range(TILES):
                    ins = pe.transpose(tile(ps_d, c), tile(xd[k4], c), w.ident[:, :])
                ins.then_inc(done["turnd"], 1)
                pe.wait_ge(over_in[k4], s.lin(64, 64, div=4))
                wait(pe, done["xsT"], s.lin())
                for c in range(TILES):
                    ins = pe.transpose(tile(ps_s, c), tile(xs[k4], c), w.ident[:, :])
                ins.then_inc(done["turns"], 1)

            def hidden(s):
                k, k4 = s.slot(), s.slot(4)
                wait(pe, done["pre"], s.lin())
                pe.wait_ge(done["spread"], s.lin(1, 1))
                pe.matmul(ps_h[:, :], w.mat("M1D"), xdT[k4][:, :], start=True, stop=False)
                pe.wait_ge(done["xsT"], s.lin(1, 1))
                pe.matmul(ps_h[:, :], w.mat("M1S"), xsT[k][:, :], start=False, stop=True).then_inc(done["ha"], 1)

            def message(s):
                k = s.slot()
                pe.wait_ge(done["hT"], s.lin(1, 1))
                wait(pe, done["max"], s.lin())
                pe.matmul(ps_m[:, :], w.mat("M2"), hT[k][:, :], start=True, stop=True).then_inc(done["ma"], 1)

            def update1(s):
                k4 = s.slot(4)
                wait(pe, done["rT"], s.lin())
                pe.matmul(ps_r[:, :], w.mat("U1X"), xdT[k4][:, :], start=True, stop=False)
                pe.wait_ge(done["max"], s.lin(1, 1))
                pe.matmul(ps_r[:, :], w.mat("U1A"), ag[k4][:, :], start=False, stop=True).then_inc(done["ra"], 1)

            def update2(s):
                k = s.slot()
                wait(pe, done["zT"], s.lin())
                pe.wait_ge(done["rT"], s.lin(1, 1))
                pe.matmul(ps_u[:, :], w.mat("U2"), rT[k][:, :], start=True, stop=True).then_inc(done["ua"], 1)

            def turn_z(s):
                k = s.slot()
                pe.wait_ge(done["zT"], s.lin(1, 1))
                wait(pe, done["x2"], s.lin(1, -1))
                for c in range(TILES):
                    ins = pe.transpose(tile(ps_z[k], c), tile(zT[k], c), w.ident[:, :])
                ins.then_inc(done["turnz"], 1)

            run_groups(pe, ng, 4, [(0, turns), (5, turn_z), (2, message), (3, update1), (4, update2), (1, hidden)])

        @block.vector
        def _(v):
            def spread(s):
                k4 = s.slot(4)
                wait(v, done["zT"], s.lin(1, -3))
                v.wait_ge(flags_in[k4], s.lin(16, 16, div=4))
                v.wait_ge(done["turnd"], s.lin(1, 1))
                wait(v, done["spread"], s.lin())
                first = s.fixed and s.lin() == 0
                v.tensor_tensor_scan(xdT[k4][:, ::-1], flags[k4][:, 1, ::-1], ps_d[:, ::-1],
                                     0.0 if first else xdT[k4 - 1][:, 0:1], ALU.mult, ALU.add).then_inc(done["spread"], 1)

            def maximum(s):
                k4 = s.slot(4)
                wait(v, done["ra"], s.lin(1, -3))
                v.wait_ge(done["ma"], s.lin(1, 1))
                wait(v, done["max"], s.lin())
                first = s.fixed and s.lin() == 0
                v.tensor_tensor_scan(ag[k4][:, ::-1], flags[k4][:, 0, ::-1], ps_m[:, ::-1],
                                     0.0 if first else ag[k4 - 1][:, 0:1], ALU.add, ALU.max).then_inc(done["max"], 1)

            def add_weight(s):
                k, k4 = s.slot(), s.slot(4)
                v.wait_ge(wr_in[k4], s.lin(16, 16, div=4))
                v.wait_ge(done["ha"], s.lin(1, 1))
                wait(v, done["hT"], s.lin(1, -1))
                v.scalar_tensor_tensor(out=pre[k][:, :], in0=wr[k4][:, :], scalar=w.wcol[:, :], in1=ps_h[:, :],
                                       op0=ALU.mult, op1=ALU.add).then_inc(done["pre"], 1)

            def add_own(s):
                k, k4 = s.slot(), s.slot(4)
                v.wait_ge(done["ua"], s.lin(1, 1))
                wait(v, done["turnz"], s.lin(1, -1))
                v.scalar_tensor_tensor(out=zT[k][:, :], in0=ps_u[:, :], scalar=w.col("c2"), in1=xdT[k4][:, :],
                                       op0=ALU.add, op1=ALU.add).then_inc(done["zT"], 1)

            def mask_factors(s):
                k = s.slot(4)
                v.wait_ge(mask_in[k], s.lin(16, 16, div=4))
                nz.masked(v, s, mask[k][:, :].bitcast(F32))

            def finish(s):
                k = s.slot(4)
                wait(v, x2_out[k], s.lin(16, 0, div=4))
                nz.scale(v, s, ps_z[s.slot()], x2[k], done["x2"], masked=True)

            run_groups(v, ng, 4, [(6, lambda s: nz.invert(v, s)), (6, mask_factors), (6, finish),
                                  (5, lambda s: nz.stats(v, s, ps_z[s.slot()], done["turnz"])), (2, maximum),
                                  (5, lambda s: nz.moments(v, s)), (4, add_own), (0, spread), (1, add_weight)])

        @block.scalar
        def _(a):
            def copy_src(s):
                k = s.slot()
                wait(a, done["ha"], s.lin(1, -1))
                a.wait_ge(done["turns"], s.lin(1, 1))
                a.copy(xsT[k][:, :], ps_s[:, :]).then_inc(done["xsT"], 1)

            def relu1(s):
                k = s.slot()
                wait(a, done["ma"], s.lin(1, -1))
                a.wait_ge(done["pre"], s.lin(1, 1))
                a.activation(hT[k][:, :], pre[k][:, :], ACT.Relu, bias=w.col("mb1")).then_inc(done["hT"], 1)

            def relu2(s):
                k = s.slot()
                wait(a, done["ua"], s.lin(1, -1))
                a.wait_ge(done["ra"], s.lin(1, 1))
                a.activation(rT[k][:, :], ps_r[:, :], ACT.Relu, bias=w.c1b[:, :]).then_inc(done["rT"], 1)

            run_groups(a, ng, 4, [(0, copy_src), (5, lambda s: nz.root(a, s)), (3, relu2), (1, relu1)])


def attention_layer(nc, w, ng, nodes, facts, along, edge_attr, mapped, t2, t3, s3, d3):
    rows_all = nodes + ng * G
    with ExitStack() as ctx:
        room = Room(nc, ctx, "att")
        rec = room.two("rec", [P, REC], I32, count=4)
        mi = room.two("mi", [P, 2 * TILES], I32, count=4)
        keep, keep2, ea, xs, xd, xsT, xdT, x3, x3n, x3s, sc, pr = (
            room.two(k, [P, G], count=4) for k in "keep keep2 ea xs xd xsT xdT x3 x3n x3s sc pr".split())
        eT, q, ev, qk, qke, m, wv, zT = (room.two(k, [P, G]) for k in "eT q ev qk qke m wv zT".split())
        ps_d, ps_s, ps_q, ps_e, ps_k, ps_v, ps_sc, ps_z = (room.bank(k) for k in ("d", "s", "q", "e", "k", "v", "sc", "z"))
        nz = Norm(room, "nz", w.eps[:, :])
        ns = Norm(room, "ns", w.eps[:, :])
        done = {k: room.sem(k + "_done") for k in
                ("turnd turns turne xsT eT spread qa q eva ev ka qk qke sca sc pr va m sum zT turnz x3 x3n x3s").split()}
        keep2_in = room.sem2("keep2_in", 4)
        rec_in, mi_in, keep_in, ea_in, xd_in, x3_out, x3n_out, x3s_out = (
            room.sem2(k, 4) for k in ("rec_in", "mi_in", "keep_in", "ea_in", "xd_in", "x3_out", "x3n_out", "x3s_out"))
        xs_in = room.swdge2("xs_in", 4)
        block = room.block()

        @block.sync
        def _(sp):
            def load(s):
                k = s.slot(4)
                g = s.lin()
                room.hold(sp, xs_in[k], s.lin(64, 0, div=4))
                sp.dma_start(mi[k][:, :], cols_of(mapped, g, 2 * TILES)).then_inc(mi_in[k], 16)
                room.hold(sp, done["turnd"], s.lin(1, -3))
                sp.dma_start(tiles3(xd[k]), edge_rows(t2, g, nodes)).then_inc(xd_in[k], 16)
                room.hold(sp, done["turne"], s.lin(1, -3))
                sp.dma_start(tiles3(ea[k]), edge_rows(edge_attr, g)).then_inc(ea_in[k], 16)
                room.hold(sp, done["spread"], s.lin(1, -3))
                sp.dma_start(keep[k][:, :], flat(along, g, KEEP_F)).then_inc(keep_in[k], 16)

            def load_facts(s):
                k = s.slot(4)
                room.hold(sp, done["sum"], s.lin(1, -3))
                sp.dma_start(keep2[k][:, :], flat(along, s.lin(), KEEP_F)).then_inc(keep2_in[k], 16)
                room.hold(sp, done["x3n"], s.lin(1, -3))
                sp.dma_start(rec[k][:, :], cols_of(facts, s.lin(), REC)).then_inc(rec_in[k], 16)

            def store(s):
                k = s.slot(4)
                g = s.lin()
                room.hold(sp, done["x3s"], s.lin(1, 1))
                sp.dma_start(edge_rows(s3, g), tiles3(x3s[k])).then_inc(x3s_out[k], 16)

            def store_dst(s):
                k = s.slot(4)
                g = s.lin()
                room.hold(sp, done["x3"], s.lin(1, 1))
                sp.dma_start(edge_rows(d3, g), tiles3(x3[k])).then_inc(x3_out[k], 16)
                room.hold(sp, done["x3n"], s.lin(1, 1))
                sp.dma_start(edge_rows(t3, g), tiles3(x3n[k])).then_inc(x3n_out[k], 16)

            run_groups(sp, ng, 4, [(0, load), (3, store), (4, load_facts), (8, store_dst)])
            for k in range(4):
                for sem in (x3_out, x3n_out, x3s_out):
                    sp.wait_ge(sem[k], 16 * uses(ng, k, 4))

        @block.gpsimd
        def _(pool):
            top = pool.to_reg(rows_all - 1)

            def gather(s):
                k = s.slot(4)
                room.hold(pool, done["turns"], s.lin(1, -3))
                room.hold(pool, done["x3s"], s.lin(1, -3))
                room.hold(pool, mi_in[k], s.lin(16, 16, div=4))
                for c in range(TILES):
                    pool.indirect_dma_start(tile(xs[k], c), None, t2,
                                            bass.IndirectOffsetOnAxis(mi[k][:, 2 * c + 1:2 * c + 2], 0),
                                            bounds_check=top, oob_is_err=False).then_inc(xs_in[k], 16)

            def multiply_edge(s):
                k = s.slot()
                pool.wait_ge(done["qk"], s.lin(1, 1))
                pool.wait_ge(done["ev"], s.lin(1, 1))
                wait(pool, done["sca"], s.lin(1, -1))
                pool.tensor_tensor(qke[k][:, :], qk[k][:, :], ev[k][:, :], ALU.mult).then_inc(done["qke"], 1)

            def add_own(s):
                k, k4 = s.slot(), s.slot(4)
                pool.wait_ge(done["sum"], s.lin(1, 1))
                pool.wait_ge(done["spread"], s.lin(1, 1))
                wait(pool, done["turnz"], s.lin(1, -1))
                pool.tensor_tensor(zT[k][:, :], wv[k][:, :], xdT[k4][:, :], ALU.add).then_inc(done["zT"], 1)

            run_groups(pool, ng, 4, [(6, add_own), (3, multiply_edge), (0, gather)])

        @block.tensor
        def _(pe):
            def turn(s, buf, bank, arrived, per, freed, over):
                k = s.slot(4)
                pe.wait_ge(arrived[k], s.lin(per, per, div=4))
                wait(pe, freed, s.lin())
                for c in range(TILES):
                    ins = pe.transpose(tile(bank, c), tile(buf[k], c), w.ident[:, :])
                ins.then_inc(over, 1)

            def turns(s):
                wait(pe, done["ev"], s.lin())
                turn(s, ea, ps_e, ea_in, 16, done["eT"], done["turne"])
                turn(s, xd, ps_d, xd_in, 16, done["spread"], done["turnd"])
                turn(s, xs, ps_s, xs_in, 64, done["xsT"], done["turns"])

            def products(s):
                k, k4 = s.slot(), s.slot(4)
                pe.wait_ge(done["eT"], s.lin(1, 1))
                pe.matmul(ps_e[:, :], w.t(3), eT[k][:, :], start=True, stop=True).then_inc(done["eva"], 1)
                pe.wait_ge(done["spread"], s.lin(1, 1))
                wait(pe, done["q"], s.lin())
                pe.matmul(ps_q[:, :], w.t(1), xdT[k4][:, :], start=True, stop=True).then_inc(done["qa"], 1)
                pe.wait_ge(done["xsT"], s.lin(1, 1))
                wait(pe, done["qk"], s.lin())
                pe.matmul(ps_k[:, :], w.t(2), xsT[k4][:, :], start=True, stop=True).then_inc(done["ka"], 1)

            def values(s):
                pe.wait_ge(done["xsT"], s.lin(1, 1))
                wait(pe, done["m"], s.lin())
                pe.matmul(ps_v[:, :], w.t(4), xsT[s.slot(4)][:, :], start=True, stop=True).then_inc(done["va"], 1)

            def scores(s):
                k = s.slot()
                pe.wait_ge(done["qke"], s.lin(1, 1))
                wait(pe, done["sc"], s.lin())
                pe.matmul(ps_sc[:, :], w.heads[:, :], qke[k][:, :], start=True, stop=True).then_inc(done["sca"], 1)

            def turn_z(s):
                k = s.slot()
                pe.wait_ge(done["zT"], s.lin(1, 1))
                wait(pe, done["x3"], s.lin())
                for c in range(TILES):
                    ins = pe.transpose(tile(ps_z, c), tile(zT[k], c), w.ident[:, :])
                ins.then_inc(done["turnz"], 1)

            run_groups(pe, ng, 4, [(2, scores), (4, values), (5, turn_z), (1, products), (0, turns)])

        @block.vector
        def _(v):
            def spread(s):
                k4 = s.slot(4)
                wait(v, done["qa"], s.lin(1, -3))
                wait(v, done["zT"], s.lin(1, -3))
                v.wait_ge(keep_in[k4], s.lin(16, 16, div=4))
                v.wait_ge(done["turnd"], s.lin(1, 1))
                wait(v, done["spread"], s.lin())
                first = s.fixed and s.lin() == 0
                v.tensor_tensor_scan(xdT[k4][:, :], keep[k4][:, :], ps_d[:, :],
                                     0.0 if first else xdT[k4 - 1][:, G - 1:G], ALU.mult, ALU.add).then_inc(done["spread"], 1)

            def src_stats(s):
                k = s.slot(4)
                v.wait_ge(xs_in[k], s.lin(64, 64, div=4))
                ns.stats(v, s, xs[k])

            def multiply(s):
                k = s.slot()
                v.wait_ge(done["q"], s.lin(1, 1))
                v.wait_ge(done["ka"], s.lin(1, 1))
                wait(v, done["qke"], s.lin(1, -1))
                v.scalar_tensor_tensor(out=qk[k][:, :], in0=ps_k[:, :], scalar=w.col("bk"), in1=q[k][:, :],
                                       op0=ALU.add, op1=ALU.mult).then_inc(done["qk"], 1)

            def clip(s):
                k = s.slot()
                v.wait_ge(done["sca"], s.lin(1, 1))
                wait(v, done["pr"], s.lin(1, -3))
                v.tensor_scalar(sc[s.slot(4)][:, :], ps_sc[:, :], -5.0, 5.0, ALU.max, ALU.min).then_inc(done["sc"], 1)

            def weigh(s):
                k = s.slot()
                v.wait_ge(done["pr"], s.lin(1, 1))
                v.wait_ge(done["va"], s.lin(1, 1))
                v.scalar_tensor_tensor(out=m[k][:, :], in0=ps_v[:, :], scalar=w.col("bv"), in1=pr[s.slot(4)][:, :],
                                       op0=ALU.add, op1=ALU.mult).then_inc(done["m"], 1)

            def sum_up(s):
                k = s.slot()
                v.wait_ge(keep2_in[s.slot(4)], s.lin(16, 16, div=4))
                v.wait_ge(done["m"], s.lin(1, 1))
                wait(v, done["zT"], s.lin(1, -1))
                wait(v, done["sum"], s.lin())
                first = s.fixed and s.lin() == 0
                v.tensor_tensor_scan(wv[k][:, :], keep2[s.slot(4)][:, :], m[k][:, :],
                                     0.0 if first else wv[1 - k][:, G - 1:G], ALU.mult, ALU.add).then_inc(done["sum"], 1)

            def mask_factors(s):
                k = s.slot(4)
                v.wait_ge(rec_in[k], s.lin(16, 16, div=4))
                nz.masked(v, s, rec[k][:, LAST:LAST + TILES].bitcast(F32))

            def dst_out(s):
                k = s.slot(4)
                wait(v, x3_out[k], s.lin(16, 0, div=4))
                wait(v, done["x3n"], s.lin(1, -3))
                nz.scale(v, s, ps_z, x3[k], done["x3"], masked=True)

            run_groups(v, ng, 4, [(6, lambda s: nz.invert(v, s)), (1, lambda s: ns.invert(v, s)), (4, weigh),
                                  (6, mask_factors), (1, lambda s: ns.offset(v, s)), (6, dst_out), (2, clip),
                                  (4, sum_up), (0, src_stats), (5, lambda s: nz.stats(v, s, ps_z, done["turnz"])),
                                  (0, lambda s: ns.moments(v, s)), (1, multiply), (5, lambda s: nz.moments(v, s)),
                                  (0, spread)])

        @block.scalar
        def _(a):
            def out_of(s, out, bank, before, over, bias=None):
                a.wait_ge(before, s.lin(1, 1))
                if bias is None:
                    a.copy(out[:, :], bank[:, :]).then_inc(over, 1)
                else:
                    a.activation(out[:, :], bank[:, :], ACT.Identity, bias=bias).then_inc(over, 1)

            def edge_in(s):
                wait(a, done["eva"], s.lin(1, -1))
                out_of(s, eT[s.slot()], ps_e, done["turne"], done["eT"])

            def src_in(s):
                wait(a, done["ka"], s.lin(1, -3))
                wait(a, done["va"], s.lin(1, -3))
                out_of(s, xsT[s.slot(4)], ps_s, done["turns"], done["xsT"])

            def factors(s):
                wait(a, done["qke"], s.lin(1, -1))
                out_of(s, ev[s.slot()], ps_e, done["eva"], done["ev"], w.col("be"))
                wait(a, done["qk"], s.lin(1, -1))
                out_of(s, q[s.slot()], ps_q, done["qa"], done["q"], w.col("bq"))

            def src_out(s):
                k = s.slot(4)
                wait(a, x3s_out[k], s.lin(16, 0, div=4))
                a.wait_ge(xs_in[k], s.lin(64, 64, div=4))
                ns.scale_a(a, s, xs[k], x3s[k], done["x3s"])

            def own_scaled(s):
                k = s.slot(4)
                a.wait_ge(rec_in[k], s.lin(16, 16, div=4))
                a.wait_ge(done["x3"], s.lin(1, 1))
                wait(a, x3n_out[k], s.lin(16, 0, div=4))
                dinv = rec[k][:, DINV:DINV + TILES].bitcast(F32)
                for c in range(TILES):
                    ins = a.activation(tile(x3n[k], c), tile(x3[k], c), ACT.Copy, scale=dinv[:, c:c + 1])
                ins.then_inc(done["x3n"], 1)

            def exponent(s):
                k = s.slot(4)
                a.wait_ge(done["sc"], s.lin(1, 1))
                wait(a, done["m"], s.lin(1, -3))
                a.activation(pr[k][:, :], sc[k][:, :], ACT.Exp).then_inc(done["pr"], 1)

            def exponents(s):
                if s.slot() == 1:
                    exponent(Step(s.j, s.unroll, s.off - 1))
                    exponent(s)
                elif s.fixed and s.lin() == ng - 1:
                    exponent(s)

            run_groups(a, ng, 4, [(1, src_out), (6, own_scaled), (1, factors), (2, exponents),
                                  (0, lambda s: ns.root(a, s)), (5, lambda s: nz.root(a, s)), (0, edge_in), (0, src_in)])


def gcn_layer(nc, w, ng, nodes, facts, along, mapped, own_t, src_t, last, next_t=None, next_s=None, d3=None, out=None):
    with ExitStack() as ctx:
        room = Room(nc, ctx, "gcn2" if last else "gcn1")
        rec = room.two("rec", [P, REC], I32, count=4)
        mi = room.two("mi", [P, 2 * TILES], I32, count=4)
        flags = room.two("flags", [P, 2, G], count=4)
        xs, xd, o_d = (room.two(k, [P, G], count=4) for k in "xs xd o_d".split())
        xsT, ws, aT, sT, c_d, r_d, h_d, g_d = (room.two(k, [P, G]) for k in "xsT ws aT sT c_d r_d h_d g_d".split())
        x3 = room.two("x3", [P, G], count=4) if last else None
        r_s, h_s = (None, None) if last else (room.two(k, [P, G]) for k in "r_s h_s".split())
        g_s, o_s = (None, None) if last else (room.two(k, [P, G], count=4) for k in "g_s o_s".split())
        ps_s = [room.bank("s0"), room.bank("s1")]
        ps_d = [room.bank("d0"), room.bank("d1")]
        ps_pd = [room.bank("pd0"), room.bank("pd1")]
        ps_ps = [room.bank("ps0"), room.bank("ps1")]
        nd = Norm(room, "nd", w.eps[:, :])
        ns = None if last else Norm(room, "ns", w.eps[:, :])
        weight = w.mat("G2") if last else w.mat("G1")
        bias = w.row("gb2") if last else w.row("gb1")
        done = {k: room.sem(k + "_done") for k in
                "turns turnd xsT ws sum sT pd psr cd rd hd hg hb od rs hs sg os".split()}
        rec_in, mi_in, flags_in, xd_in, xs_in, x3_in, os_out = (
            room.sem2(k, 4) for k in ("rec_in", "mi_in", "flags_in", "xd_in", "xs_in", "x3_in", "os_out"))
        over_in = room.swdge2("over_in", 4)
        od_out = room.swdge2("od_out", 4) if last else room.sem2("od_out", 4)
        block = room.block()

        @block.sync
        def _(sp):
            def load(s):
                k = s.slot(4)
                g = s.lin()
                room.hold(sp, done["turns"], s.lin(1, -3))
                sp.dma_start(mi[k][:, :], cols_of(mapped, g, 2 * TILES)).then_inc(mi_in[k], 16)
                sp.dma_start(tiles3(xs[k]), edge_rows(src_t, g)).then_inc(xs_in[k], 16)
                room.hold(sp, done["turnd"], s.lin(1, -3))
                sp.dma_start(tiles3(xd[k]), edge_rows(own_t, g)).then_inc(xd_in[k], 16)
                room.hold(sp, done["sum"], s.lin(1, -3))
                sp.dma_start(flags[k][:, :, :], along[bass.ds(g, 1), KEEP_F:W_F + 1, :]
                             .rearrange("a k g -> (a k) g").partition_broadcast(P)).then_inc(flags_in[k], 16)

            def load_facts(s):
                k = s.slot(4)
                g = s.lin()
                room.hold(sp, done["od"], s.lin(1, -3))
                if last:
                    room.hold(sp, od_out[k], s.lin(16 * TILES, 0, div=4))
                sp.dma_start(rec[k][:, :], cols_of(facts, g, REC)).then_inc(rec_in[k], 16)
                if last:
                    sp.dma_start(tiles3(x3[k]), edge_rows(d3, g)).then_inc(x3_in[k], 16)

            def store(s):
                k = s.slot(4)
                g = s.lin()
                room.hold(sp, done["os"], s.lin(1, 1))
                sp.dma_start(edge_rows(next_s, g), tiles3(o_s[k])).then_inc(os_out[k], 16)
                room.hold(sp, done["od"], s.lin(1, 1))
                sp.dma_start(edge_rows(next_t, g), tiles3(o_d[k])).then_inc(od_out[k], 16)

            if last:
                run_groups(sp, ng, 4, [(0, load), (1, load_facts)])
            else:
                run_groups(sp, ng, 4, [(0, load), (2, load_facts), (7, store)])
                for k in range(4):
                    sp.wait_ge(os_out[k], 16 * uses(ng, k, 4))
                    sp.wait_ge(od_out[k], 16 * uses(ng, k, 4))

        @block.gpsimd
        def _(pool):
            top = pool.to_reg(ng * G - 1)
            top_node = pool.to_reg(nodes - 1)

            def overlay(s):
                k = s.slot(4)
                room.hold(pool, xs_in[k], s.lin(16, 16, div=4))
                room.hold(pool, mi_in[k], s.lin(16, 16, div=4))
                for c in range(TILES):
                    pool.indirect_dma_start(tile(xs[k], c), None, own_t,
                                            bass.IndirectOffsetOnAxis(mi[k][:, 2 * c:2 * c + 1], 0),
                                            bounds_check=top, oob_is_err=False).then_inc(over_in[k], 16)

            def weigh(s):
                k = s.slot()
                pool.wait_ge(done["xsT"], s.lin(1, 1))
                pool.wait_ge(flags_in[s.slot(4)], s.lin(16, 16, div=4))
                wait(pool, done["sum"], s.lin(1, -1))
                pool.tensor_tensor(ws[k][:, :], xsT[k][:, :], flags[s.slot(4)][:, 1, :], ALU.mult).then_inc(done["ws"], 1)

            def src_gamma(s):
                k = s.slot()
                pool.wait_ge(done["hs"], s.lin(1, 1))
                wait(pool, done["os"], s.lin(1, -3))
                pool.tensor_tensor(tiles3(g_s[s.slot(4)]), tiles3(h_s[k]), over_tiles(w.row("gamma")), ALU.mult).then_inc(done["sg"], 1)

            def scatter(s):
                k = s.slot(4)
                room.hold(pool, done["od"], s.lin(1, 1))
                for c in range(TILES):
                    pool.indirect_dma_start(out, bass.IndirectOffsetOnAxis(rec[k][:, SCAT + c:SCAT + c + 1], 0),
                                            tile(o_d[k], c), None, bounds_check=top_node,
                                            oob_is_err=False).then_inc(od_out[k], 16)

            if last:
                run_groups(pool, ng, 4, [(0, overlay), (3, scatter)])
                for k in range(4):
                    pool.wait_ge(od_out[k], 16 * TILES * uses(ng, k, 4))
            else:
                run_groups(pool, ng, 4, [(2, weigh), (4, src_gamma), (0, overlay)])

        @block.tensor
        def _(pe):
            def turns(s):
                k, k4 = s.slot(), s.slot(4)
                pe.wait_ge(over_in[k4], s.lin(64, 64, div=4))
                wait(pe, done["ws"] if last else done["xsT"], s.lin(1, -1))
                for c in range(TILES):
                    ins = pe.transpose(tile(ps_s[k], c), tile(xs[k4], c), w.ident[:, :])
                ins.then_inc(done["turns"], 1)
                pe.wait_ge(xd_in[k4], s.lin(16, 16, div=4))
                wait(pe, done["sT"], s.lin(1, -1))
                for c in range(TILES):
                    ins = pe.transpose(tile(ps_d[k], c), tile(xd[k4], c), w.ident[:, :])
                ins.then_inc(done["turnd"], 1)

            def src_product(s):
                k = s.slot()
                pe.wait_ge(done["xsT"], s.lin(1, 1))
                wait(pe, done["rs"], s.lin(1, -1))
                for c in range(TILES):
                    pe.matmul(tile(ps_ps[k], c), w.ones16[:, :], w.gb1s[:, :], start=True, stop=False)
                    ins = pe.matmul(tile(ps_ps[k], c), tile(xsT[k], c), weight, start=False, stop=True)
                ins.then_inc(done["psr"], 1)

            def dst_product(s):
                k = s.slot()
                pe.wait_ge(done["sT"], s.lin(1, 1))
                wait(pe, done["cd"], s.lin(1, -1))
                for c in range(TILES):
                    ins = pe.matmul(tile(ps_pd[k], c), tile(sT[k], c), weight, start=True, stop=True)
                ins.then_inc(done["pd"], 1)

            if last:
                run_groups(pe, ng, 4, [(1, dst_product), (0, turns)])
            else:
                run_groups(pe, ng, 4, [(0, turns), (2, dst_product), (1, src_product)])

        @block.vector
        def _(v):
            def weigh(s):
                k = s.slot()
                v.wait_ge(flags_in[s.slot(4)], s.lin(16, 16, div=4))
                v.wait_ge(done["turns"], s.lin(1, 1))
                v.tensor_tensor(ws[k][:, :], ps_s[k][:, :], flags[s.slot(4)][:, 1, :], ALU.mult).then_inc(done["ws"], 1)

            def sum_up(s):
                k = s.slot()
                v.wait_ge(flags_in[s.slot(4)], s.lin(16, 16, div=4))
                v.wait_ge(done["ws"], s.lin(1, 1))
                wait(v, done["sum"], s.lin())
                first = s.fixed and s.lin() == 0
                v.tensor_tensor_scan(aT[k][:, :], flags[s.slot(4)][:, 0, :], ws[k][:, :],
                                     0.0 if first else aT[1 - k][:, G - 1:G], ALU.mult, ALU.add).then_inc(done["sum"], 1)

            def add_own(s):
                k = s.slot()
                v.wait_ge(done["sum"], s.lin(1, 1))
                v.wait_ge(done["turnd"], s.lin(1, 1))
                wait(v, done["pd"], s.lin(1, -1))
                v.tensor_tensor(sT[k][:, :], aT[k][:, :], ps_d[k][:, :], ALU.add).then_inc(done["sT"], 1)

            def dst_bias(s):
                k, k4 = s.slot(), s.slot(4)
                dinv = rec[k4][:, DINV:DINV + TILES].bitcast(F32)
                v.wait_ge(rec_in[k4], s.lin(16, 16, div=4))
                v.wait_ge(done["pd"], s.lin(1, 1))
                wait(v, done["rd"], s.lin(1, -1))
                for c in range(TILES):
                    ins = v.scalar_tensor_tensor(out=tile(c_d[k], c), in0=tile(ps_pd[k], c), scalar=dinv[:, c:c + 1],
                                                 in1=bias, op0=ALU.mult, op1=ALU.add)
                ins.then_inc(done["cd"], 1)

            def dst_norm(s):
                nd.scale(v, s, r_d[s.slot()], h_d[s.slot()], done["hd"])

            def dst_gamma(s):
                k = s.slot()
                v.wait_ge(done["hd"], s.lin(1, 1))
                wait(v, done["od"], s.lin(1, -1))
                v.tensor_tensor(tiles3(g_d[k]), tiles3(h_d[k]), over_tiles(w.row("gamma")), ALU.mult).then_inc(done["hg"], 1)

            def dst_beta(s):
                k = s.slot()
                v.wait_ge(done["hg"], s.lin(1, 1))
                v.tensor_tensor(tiles3(g_d[k]), tiles3(g_d[k]), over_tiles(w.row("beta")), ALU.add).then_inc(done["hb"], 1)

            def src_beta(s):
                k4 = s.slot(4)
                v.wait_ge(done["sg"], s.lin(1, 1))
                wait(v, os_out[k4], s.lin(16, 0, div=4))
                v.tensor_tensor(tiles3(o_s[k4]), tiles3(g_s[k4]), over_tiles(w.row("beta")), ALU.add).then_inc(done["os"], 1)

            def add_x3(s):
                k, k4 = s.slot(), s.slot(4)
                v.wait_ge(done["cd"], s.lin(1, 1))
                v.wait_ge(x3_in[k4], s.lin(16, 16, div=4))
                v.tensor_tensor(r_d[k][:, :], c_d[k][:, :], x3[k4][:, :], ALU.add).then_inc(done["rd"], 1)

            def last_out(s):
                k4 = s.slot(4)
                wait(v, od_out[k4], s.lin(64, 0, div=4))
                nd.scale(v, s, r_d[s.slot()], o_d[k4], done["od"])

            dst_stats = lambda s: nd.stats(v, s, r_d[s.slot()], done["rd"])
            dst_moments = lambda s: nd.moments(v, s)
            if last:
                run_groups(v, ng, 4, [(2, lambda s: nd.invert(v, s)), (0, weigh), (1, dst_bias), (0, sum_up), (2, last_out),
                                      (1, add_x3), (0, add_own), (1, dst_stats), (1, dst_moments)])
            else:
                run_groups(v, ng, 4, [(4, src_beta), (4, dst_beta), (3, lambda s: nd.invert(v, s)),
                                      (2, lambda s: ns.invert(v, s)), (3, dst_norm), (2, lambda s: ns.offset(v, s)),
                                      (2, dst_bias), (3, dst_gamma), (1, sum_up),
                                      (1, lambda s: ns.stats(v, s, r_s[s.slot()], done["rs"])), (1, add_own),
                                      (2, dst_stats), (1, lambda s: ns.moments(v, s)), (2, dst_moments)])

        @block.scalar
        def _(a):
            def copy_src(s):
                k = s.slot()
                wait(a, done["psr"], s.lin(1, -1))
                wait(a, done["ws"], s.lin(1, -1))
                a.wait_ge(done["turns"], s.lin(1, 1))
                a.copy(xsT[k][:, :], ps_s[k][:, :]).then_inc(done["xsT"], 1)

            def dst_relu(s):
                k = s.slot()
                a.wait_ge(done["cd"], s.lin(1, 1))
                wait(a, done["hd"], s.lin(1, -1))
                a.activation(r_d[k][:, :], c_d[k][:, :], ACT.Relu).then_inc(done["rd"], 1)

            def src_relu(s):
                k = s.slot()
                a.wait_ge(done["psr"], s.lin(1, 1))
                wait(a, done["hs"], s.lin(1, -1))
                a.activation(r_s[k][:, :], ps_ps[k][:, :], ACT.Relu).then_inc(done["rs"], 1)

            def src_norm(s):
                wait(a, done["sg"], s.lin(1, -1))
                ns.scale_a(a, s, r_s[s.slot()], h_s[s.slot()], done["hs"])

            def dst_scaled(s):
                k, k4 = s.slot(), s.slot(4)
                a.wait_ge(done["hb"], s.lin(1, 1))
                wait(a, od_out[k4], s.lin(16, 0, div=4))
                dinv = rec[k4][:, DINV:DINV + TILES].bitcast(F32)
                for c in range(TILES):
                    ins = a.activation(tile(o_d[k4], c), tile(g_d[k], c), ACT.Copy, scale=dinv[:, c:c + 1])
                ins.then_inc(done["od"], 1)

            if last:
                run_groups(a, ng, 4, [(1, lambda s: nd.root(a, s))])
            else:
                run_groups(a, ng, 4, [(0, copy_src), (4, dst_scaled), (2, src_norm), (1, src_relu), (2, dst_relu),
                                      (1, lambda s: ns.root(a, s)), (2, lambda s: nd.root(a, s))])


def build(nc, x, ints, ew, edge_attr, mats, cols, rows, wrow, out):
    nodes = x.shape[0]
    ng = ew.shape[0]

    def table(name, shape, dt=F32):
        return nc.dram_tensor(name, shape, dt).ap()

    facts = table("facts", [P, ng * REC], I32)
    along = table("along", [ng, 4, G])
    slots = table("slots", [nodes, 2], I32)
    mapped = table("mapped", [P, ng * 2 * TILES], I32)
    t1, s1 = table("t1", [ng * G, D]), table("s1", [ng * G, D])
    t2 = table("t2", [nodes + ng * G, D])
    t3, s3, d3 = table("t3", [ng * G, D]), table("s3", [ng * G, D]), table("d3", [ng * G, D])
    th, sh = table("th", [ng * G, D]), table("sh", [ng * G, D])
    with ExitStack() as ctx:
        w = Weights(Room(nc, ctx, "w"))
        prepare_weights(nc, w, mats, cols, rows, wrow)
        prepare_edges(nc, w, ng, nodes, ints, ew, along, facts.rearrange("p (g r) -> p g r", r=REC), slots)
        dense_pass(nc, w, ng, nodes, x, out, t2, facts, along, slots, mapped, t1, s1)
        max_layer(nc, w, ng, nodes, facts, along, mapped, t1, s1, t2)
        attention_layer(nc, w, ng, nodes, facts, along, edge_attr, mapped, t2, t3, s3, d3)
        gcn_layer(nc, w, ng, nodes, facts, along, mapped, t3, s3, False, next_t=th, next_s=sh)
        gcn_layer(nc, w, ng, nodes, facts, along, mapped, th, sh, True, d3=d3, out=out)


def kernel(**inputs):
    import numpy as np
    import concourse.bacc as bacc
    from concourse.bass_utils import run_bass_kernel_spmd as run

    a = {k: np.ascontiguousarray(v) for k, v in inputs.items()}
    nodes, d = a["x"].shape
    edges = a["src"].shape[0]
    ng = -(-edges // G)
    pad = ng * G - edges
    fill = np.full((pad,), nodes, np.int32)
    src = np.concatenate([a["src"], np.zeros((pad,), np.int32)])
    dst = np.concatenate([a["dst"], fill])
    before = np.concatenate([np.full((1,), nodes + 1, np.int32), dst[:-1]])
    after = np.concatenate([dst[1:], np.full((1,), nodes + 1, np.int32)])
    m1 = a["L1_gnn_W1"]
    u1 = a["L1_gnn_U1"]
    mats = [a["L0_gnn_W"], a["L2_gnn_Wq"], a["L2_gnn_Wk"], a["L2_gnn_We"], a["L2_gnn_Wv"], m1[:d], m1[d:2 * d],
            a["L1_gnn_W2"], u1[:d], u1[d:], a["L1_gnn_U2"], a["L3_gnn_W1"], a["L3_gnn_W2"]]
    vecs = [a[k] for k in ("L0_gnn_b", "L1_gnn_b1", "L1_gnn_b2", "L1_gnn_c1", "L1_gnn_c2", "L2_gnn_bq", "L2_gnn_bk",
                           "L2_gnn_be", "L2_gnn_bv", "L3_gnn_b1", "L3_gnn_g1", "L3_gnn_beta1", "L3_gnn_b2")]
    arrays = {
        "x": a["x"],
        "ints": np.stack([src, dst, before, after]).reshape(4, ng, G),
        "ew": np.concatenate([a["edge_weight"], np.zeros((pad,), np.float32)]).reshape(ng, G),
        "edge_attr": np.concatenate([a["edge_attr_128"], np.zeros((pad, d), np.float32)]),
        "mats": np.ascontiguousarray(np.concatenate(mats, axis=1)),
        "cols": np.ascontiguousarray(np.stack(vecs, axis=1)),
        "rows": np.stack(vecs),
        "wrow": m1[2 * d:].reshape(d, 1),
    }
    nc = bacc.Bacc("TRN2", target_bir_lowering=False, num_devices=1)
    aps = [nc.dram_tensor(k, v.shape, mybir.dt.from_np(v.dtype), kind="ExternalInput").ap() for k, v in arrays.items()]
    out = nc.dram_tensor("out", (nodes, d), F32, kind="ExternalOutput").ap()
    build(nc, *aps, out)
    result = run(nc, [arrays], core_ids=[0])
    return result.results[0]["out"]
```
